# Optimizing a Trainium2 kernel written in Bass

```python
import numpy as np
import jax
import jax.numpy as jnp

def _softmax(x, axis=-1):
    return jax.nn.softmax(x, axis=axis)

def _gelu(x):
    return jax.nn.gelu(x, approximate=True)

def _silu(x):
    return jax.nn.silu(x)

def _sigmoid(x):
    return jax.nn.sigmoid(x)

def _layernorm(x, axis=-1, eps=1e-05):
    m = jnp.mean(x, axis=axis, keepdims=True)
    v = jnp.var(x, axis=axis, keepdims=True)
    return (x - m) / jnp.sqrt(v + eps)

def _scatter_add(tgt, idx, src, axis=0):
    return tgt.at[idx].add(src)

def _segment_sum(src, seg, n):
    return jax.ops.segment_sum(src, seg, n)
kernel_name = 'mk_gnn_resnorm_d2_gnn_r8_156d92'

def setup_inputs(seed: int=0):
    np.random.seed(seed)
    _w = jnp.asarray

    def _rec_inputs():
        import jax
        import jax.numpy as jnp
        _gk = jax.random.key(seed)
        x = -0.0006008 + 1.001 * jax.random.normal(jax.random.fold_in(_gk, 1), (6250, 128), jnp.float32)
        _s = jax.random.randint(jax.random.fold_in(_gk, 2), (50000,), 0, 6250, jnp.int32)
        _d = jax.random.randint(jax.random.fold_in(_gk, 3), (50000,), 0, 6250, jnp.int32)
        _loop = jnp.arange(6250, dtype=jnp.int32)
        src = jnp.concatenate([_s, _d, _loop])
        dst = jnp.concatenate([_d, _s, _loop])
        _o = jnp.argsort(dst, stable=True)
        src = src[_o]
        dst = dst[_o]
        return (x, src, dst)
    x, src, dst = _rec_inputs()

    def _L0_gnn_setup():
        import jax, jax.numpy as jnp
        import numpy as np
        TOPK = 2
        key = jax.random.key(seed)
        ks = jax.random.split(key, 18)
        N, E = (2500, 40000)
        IN, H, OUT, L = (128, 256, 128, 3)
        NW, NS = (4, 4)
        NE = NW + NS

        def w(k, shape, fan):
            return jax.random.normal(k, shape, dtype=jnp.float32) / np.float32(np.sqrt(fan))
        inp = {'x': jax.random.normal(ks[0], (N, IN), dtype=jnp.float32), 'edge_index': jax.random.randint(ks[1], (2, E), 0, N, dtype=jnp.int64), 'W_in': w(ks[2], (IN, H), IN), 'b_in': jnp.zeros((H,), jnp.float32), 'router_W': w(ks[3], (L, 2 * H, NE), 2 * H), 'router_b': jnp.zeros((L, NE), jnp.float32), 'weak_W': w(ks[4], (L, NW, H, H), H), 'weak_b': jnp.zeros((L, NW, H), jnp.float32), 'strong_W1': w(ks[5], (L, NS, H, 2 * H), H), 'strong_b1': jnp.zeros((L, NS, 2 * H), jnp.float32), 'strong_W2': w(ks[6], (L, NS, 2 * H, H), 2 * H), 'strong_b2': jnp.zeros((L, NS, H), jnp.float32), 'conf_W': w(ks[7], (L, H, 1), H), 'conf_b': jnp.zeros((L, 1), jnp.float32), 'W_out': w(ks[8], (H, OUT), H), 'b_out': jnp.zeros((OUT,), jnp.float32)}
        return inp
    _L0_gnn_all = _L0_gnn_setup()
    _L0_gnn_in = {k: v for k, v in _L0_gnn_all.items() if k in ('W_in', 'b_in', 'router_W', 'router_b', 'weak_W', 'weak_b', 'strong_W1', 'strong_b1', 'strong_W2', 'strong_b2', 'conf_W', 'conf_b', 'W_out', 'b_out')}
    del _L0_gnn_all

    def _L1_gnn_setup():
        import jax, jax.numpy as jnp
        import numpy as np
        N = 3750
        E = 60000
        IN_DIM = 128
        HID = 32
        HEADS = 4
        OUT_DIM = 128
        NEG_SLOPE = 0.2
        EPS = 1e-16

        def _gat_conv(x, src, dst, W, a_src, a_dst, bias, heads, ch, concat):
            n = x.shape[0]
            h = (x @ W).reshape(n, heads, ch)
            alpha_s = jnp.einsum('nhc,hc->nh', h, a_src)
            alpha_d = jnp.einsum('nhc,hc->nh', h, a_dst)
            e = jax.nn.leaky_relu(alpha_s[src] + alpha_d[dst], NEG_SLOPE)
            m = jax.ops.segment_max(e, dst, num_segments=n)
            m = jnp.where(jnp.isfinite(m), m, 0.0)
            ex = jnp.exp(e - m[dst])
            denom = jax.ops.segment_sum(ex, dst, num_segments=n)
            alpha = ex / (denom[dst] + EPS)
            out = jax.ops.segment_sum(h[src] * alpha[:, :, None], dst, num_segments=n)
            if concat:
                out = out.reshape(n, heads * ch)
            else:
                out = out.mean(axis=1)
            return out + bias
        key = jax.random.key(seed)
        ks = jax.random.split(key, 12)
        x = jax.random.normal(ks[0], (N, IN_DIM), dtype=jnp.float32)
        edge_index = jax.random.randint(ks[1], (2, E), 0, N, dtype=jnp.int32)

        def glorot(k, shape, fan_in):
            return jax.random.normal(k, shape, dtype=jnp.float32) / np.sqrt(fan_in)
        W1 = glorot(ks[2], (IN_DIM, HEADS * HID), IN_DIM)
        a_src1 = glorot(ks[3], (HEADS, HID), HID)
        a_dst1 = glorot(ks[4], (HEADS, HID), HID)
        b1 = jnp.zeros((HEADS * HID,), dtype=jnp.float32)
        W2 = glorot(ks[5], (HEADS * HID, OUT_DIM), HEADS * HID)
        a_src2 = glorot(ks[6], (1, OUT_DIM), OUT_DIM)
        a_dst2 = glorot(ks[7], (1, OUT_DIM), OUT_DIM)
        b2 = jnp.zeros((OUT_DIM,), dtype=jnp.float32)
        return {'x': x, 'edge_index': edge_index, 'W1': W1, 'a_src1': a_src1, 'a_dst1': a_dst1, 'b1': b1, 'W2': W2, 'a_src2': a_src2, 'a_dst2': a_dst2, 'b2': b2}
    _L1_gnn_all = _L1_gnn_setup()
    _L1_gnn_in = {k: v for k, v in _L1_gnn_all.items() if k in ('W1', 'a_src1', 'a_dst1', 'b1', 'W2', 'a_src2', 'a_dst2', 'b2')}
    del _L1_gnn_all
    return {'x': x, 'src': src, 'dst': dst, 'L0_gnn_W_in': _L0_gnn_in['W_in'], 'L0_gnn_b_in': _L0_gnn_in['b_in'], 'L0_gnn_router_W': _L0_gnn_in['router_W'], 'L0_gnn_router_b': _L0_gnn_in['router_b'], 'L0_gnn_weak_W': _L0_gnn_in['weak_W'], 'L0_gnn_weak_b': _L0_gnn_in['weak_b'], 'L0_gnn_strong_W1': _L0_gnn_in['strong_W1'], 'L0_gnn_strong_b1': _L0_gnn_in['strong_b1'], 'L0_gnn_strong_W2': _L0_gnn_in['strong_W2'], 'L0_gnn_strong_b2': _L0_gnn_in['strong_b2'], 'L0_gnn_conf_W': _L0_gnn_in['conf_W'], 'L0_gnn_conf_b': _L0_gnn_in['conf_b'], 'L0_gnn_W_out': _L0_gnn_in['W_out'], 'L0_gnn_b_out': _L0_gnn_in['b_out'], 'L1_gnn_W1': _L1_gnn_in['W1'], 'L1_gnn_a_src1': _L1_gnn_in['a_src1'], 'L1_gnn_a_dst1': _L1_gnn_in['a_dst1'], 'L1_gnn_b1': _L1_gnn_in['b1'], 'L1_gnn_W2': _L1_gnn_in['W2'], 'L1_gnn_a_src2': _L1_gnn_in['a_src2'], 'L1_gnn_a_dst2': _L1_gnn_in['a_dst2'], 'L1_gnn_b2': _L1_gnn_in['b2']}

def reference(x, src, dst, L0_gnn_W_in, L0_gnn_b_in, L0_gnn_router_W, L0_gnn_router_b, L0_gnn_weak_W, L0_gnn_weak_b, L0_gnn_strong_W1, L0_gnn_strong_b1, L0_gnn_strong_W2, L0_gnn_strong_b2, L0_gnn_conf_W, L0_gnn_conf_b, L0_gnn_W_out, L0_gnn_b_out, L1_gnn_W1, L1_gnn_a_src1, L1_gnn_a_dst1, L1_gnn_b1, L1_gnn_W2, L1_gnn_a_src2, L1_gnn_a_dst2, L1_gnn_b2):
    import jax
    import jax.numpy as jnp

    def _L0_gnn_ref(x, edge_index, W_in, b_in, router_W, router_b, weak_W, weak_b, strong_W1, strong_b1, strong_W2, strong_b2, conf_W, conf_b, W_out, b_out):
        import jax, jax.numpy as jnp
        import numpy as np
        TOPK = 2
        N = x.shape[0]
        L = router_W.shape[0]
        src = edge_index[0]
        dst = edge_index[1]
        deg = jax.ops.segment_sum(jnp.ones(src.shape, x.dtype), dst, num_segments=N)
        deg = jnp.clip(deg, 1.0)[:, None]
        h = x @ W_in + b_in
        rows = jnp.arange(N)[:, None]
        for l in range(L):
            agg = jax.ops.segment_sum(h[src], dst, num_segments=N) / deg
            logits = jnp.concatenate([h, agg], axis=-1) @ router_W[l] + router_b[l]
            vals, idx = jax.lax.top_k(logits, TOPK)
            gates = jax.nn.softmax(vals, axis=-1)
            gate_dense = jnp.zeros_like(logits).at[rows, idx].set(gates)
            weak = jax.nn.relu(jnp.einsum('nh,ehf->nef', agg, weak_W[l]) + weak_b[l])
            sh = jax.nn.relu(jnp.einsum('nh,ehf->nef', agg, strong_W1[l]) + strong_b1[l])
            strong = jnp.einsum('nef,efh->neh', sh, strong_W2[l]) + strong_b2[l]
            experts = jnp.concatenate([weak, strong], axis=1)
            moe = jnp.einsum('ne,neh->nh', gate_dense, experts)
            conf = jax.nn.sigmoid(h @ conf_W[l] + conf_b[l])
            h = h + conf * moe
        return h @ W_out + b_out

    def _L1_gnn_ref(x, edge_index, W1, a_src1, a_dst1, b1, W2, a_src2, a_dst2, b2):
        import jax, jax.numpy as jnp
        import numpy as np
        N = 3750
        E = 60000
        IN_DIM = 128
        HID = 32
        HEADS = 4
        OUT_DIM = 128
        NEG_SLOPE = 0.2
        EPS = 1e-16

        def _gat_conv(x, src, dst, W, a_src, a_dst, bias, heads, ch, concat):
            n = x.shape[0]
            h = (x @ W).reshape(n, heads, ch)
            alpha_s = jnp.einsum('nhc,hc->nh', h, a_src)
            alpha_d = jnp.einsum('nhc,hc->nh', h, a_dst)
            e = jax.nn.leaky_relu(alpha_s[src] + alpha_d[dst], NEG_SLOPE)
            m = jax.ops.segment_max(e, dst, num_segments=n)
            m = jnp.where(jnp.isfinite(m), m, 0.0)
            ex = jnp.exp(e - m[dst])
            denom = jax.ops.segment_sum(ex, dst, num_segments=n)
            alpha = ex / (denom[dst] + EPS)
            out = jax.ops.segment_sum(h[src] * alpha[:, :, None], dst, num_segments=n)
            if concat:
                out = out.reshape(n, heads * ch)
            else:
                out = out.mean(axis=1)
            return out + bias
        loops = jnp.arange(N, dtype=edge_index.dtype)
        src = jnp.concatenate([edge_index[0], loops])
        dst = jnp.concatenate([edge_index[1], loops])
        h = _gat_conv(x, src, dst, W1, a_src1, a_dst1, b1, HEADS, HID, concat=True)
        h = jax.nn.elu(h)
        out = _gat_conv(h, src, dst, W2, a_src2, a_dst2, b2, 1, OUT_DIM, concat=False)
        return out
    edge_index = jnp.stack([src, dst])
    x = _layernorm(x + _L0_gnn_ref(x, edge_index, L0_gnn_W_in, L0_gnn_b_in, L0_gnn_router_W, L0_gnn_router_b, L0_gnn_weak_W, L0_gnn_weak_b, L0_gnn_strong_W1, L0_gnn_strong_b1, L0_gnn_strong_W2, L0_gnn_strong_b2, L0_gnn_conf_W, L0_gnn_conf_b, L0_gnn_W_out, L0_gnn_b_out), axis=-1)
    x = _layernorm(x + _L1_gnn_ref(x, edge_index, L1_gnn_W1, L1_gnn_a_src1, L1_gnn_a_dst1, L1_gnn_b1, L1_gnn_W2, L1_gnn_a_src2, L1_gnn_a_dst2, L1_gnn_b2), axis=-1)
    return x

_drawn_inputs = setup_inputs


def setup_inputs(seed=0):
    import zlib

    import numpy as np

    out = dict(_drawn_inputs(seed))
    spreads = {'L0_gnn_b_in': (0.0, 0.1),
     'L0_gnn_router_b': (0.0, 0.1),
     'L0_gnn_weak_b': (0.0, 0.275),
     'L0_gnn_strong_b1': (0.0, 0.316),
     'L0_gnn_strong_b2': (0.0, 0.1),
     'L0_gnn_conf_b': (0.0, 0.8),
     'L0_gnn_b_out': (0.0, 0.1),
     'L1_gnn_b1': (0.0, 0.1),
     'L1_gnn_b2': (0.0, 0.1)}
    factors = {'L1_gnn_a_dst1': 3.128, 'L1_gnn_a_src2': 3.376, 'L1_gnn_a_dst2': 8.0}
    for name, (base, spread) in spreads.items():
        noise = np.random.default_rng([zlib.crc32(name.encode()), seed]).standard_normal(out[name].shape)
        drawn = base * np.exp(spread * noise) if base else spread * noise
        out[name] = jnp.asarray(drawn.astype(out[name].dtype))
    for name, factor in factors.items():
        out[name] = (out[name] * factor).astype(out[name].dtype)
    return out
```

```python
import concourse.bass as bass
from concourse import mybir
from contextlib import ExitStack

F32 = mybir.dt.float32
BF16 = mybir.dt.bfloat16
I32 = mybir.dt.int32
U32 = mybir.dt.uint32
ALU = mybir.AluOpType
ACT = mybir.ActivationFunctionType
AX = mybir.AxisListType

P = 128
N = 6250
E = 106250
GROUPS = -(-N // P)
NP = GROUPS * P
ET = 832
EP = ET * P
DUMMY = NP
IN, H, LAYERS = 128, 256, 3
LOOPS = 3750
NW, NS = 4, 4
NE = NW + NS
HEADS, HID = 4, 32
HC = HID + 1
GW = HEADS * HC + HEADS
SLOTS = 4
RING = 16
UNITS = RING // SLOTS
RUN = 64
COLS = GROUPS * RUN + RUN
UMAX = (E + GROUPS * SLOTS + RING) // SLOTS
CAP = UMAX * SLOTS + RUN
HIST = 8
LOWEST = -1.5e38
DUMMY_SCORE = -1.0e38
EPS_LN = 1e-5
EPS_GAT = 1e-16


def w(eng, sem, value):
    if not (isinstance(value, int) and value <= 0):
        eng.wait_ge(sem, value)


def gnn_kernel(nc, x, src, dst, W_in, b_in, router_W, router_b, weak_W, weak_b, strong_W1, strong_b1,
               strong_W2, strong_b2, conf_W, conf_b, W_out, b_out, W1, a_src1, a_dst1, b1, W2, a_src2,
               a_dst2, b2, out):
    ctx = ExitStack()
    with ctx:
        def sb(name, shape, dt=F32):
            return ctx.enter_context(nc.sbuf_tensor(name, shape, dt))

        def sem(name):
            return ctx.enter_context(nc.semaphore(name))

        def dram(name, shape, dt=F32):
            return nc.dram_tensor(name, shape, dt, kind="Internal").ap()

        hidden_tab = [dram(f"hidden_tab{i}", [NP + 1, H]) for i in range(LAYERS)]
        gat_tab = [dram(f"gat_tab{i}", [NP + 1, GW]) for i in range(2)]
        meta_tab = dram("meta_tab", [NP, 4], I32)
        slot_tab = dram("slot_tab", [P, CAP], I32)

        h_res = sb("h_res", [P, GROUPS, H])
        x_res = sb("x_res", [P, GROUPS, IN])
        perm = sb("perm", [P, GROUPS, 4], I32)
        rdeg = sb("rdeg", [P, GROUPS])
        loop_on = sb("loop_on", [P, GROUPS])
        loop_cap = sb("loop_cap", [P, GROUPS])
        ring = sb("ring", [P, RING, H])
        stage = sb("stage", [P, 2, RING // 2], I32)
        cum = sb("cum", [1, GROUPS + 2], I32)
        ad = [sb(f"ad{i}", [P, GROUPS, HEADS]) for i in range(2)]

        wbuf = sb("wbuf", [P, 10240])
        run_raw = wbuf[:, 0:GROUPS * RUN].bitcast(I32).rearrange("p (g k) -> p g k", k=RUN)
        slots_sb = wbuf[:, GROUPS * RUN:GROUPS * RUN + COLS].bitcast(I32)
        d_at = GROUPS * RUN + COLS
        bucket1h = wbuf[:, d_at:d_at + GROUPS * P // 2].bitcast(BF16).rearrange("p (g b) -> p g b", b=P)
        wk_w = wbuf[:, 0:2048].rearrange("p (k n) -> p k n", k=2)
        w1_w = wbuf[:, 2048:6144].rearrange("p (k s n) -> p k s n", k=2, s=NS)
        w2_w = wbuf[:, 6144:10240].rearrange("p (c s n) -> p c s n", c=4, s=NS)
        gat_rows = wbuf[:, 0:GROUPS * GW].rearrange("p (g n) -> p g n", n=GW)

        iota_i = sb("iota_i", [P, P], I32)
        iota = sb("iota", [P, P])
        iota_b = sb("iota_b", [P, P], BF16)
        ident = sb("ident", [P, P])
        tri = sb("tri", [P, P])
        tri_b = sb("tri_b", [P, P], BF16)
        ones_b = sb("ones_b", [P, P], BF16)
        zero_b = sb("zero_b", [P, P], BF16)
        ones_row = sb("ones_row", [1, P])
        dummy_row = sb("dummy_row", [1, H])
        dummy_score = sb("dummy_score", [1, HEADS])

        dst_i = sb("dst_i", [P, ET], I32)
        lo_i = ring[:, 0:4, :].rearrange("p a b -> p (a b)")[:, 0:ET].bitcast(I32)
        lo_f = ring[:, 4:8, :].rearrange("p a b -> p (a b)")[:, 0:ET]
        hi_f = ring[:, 8:12, :].rearrange("p a b -> p (a b)")[:, 0:ET]
        lo1h = sb("lo1h", [P, 2, HIST, P], BF16)
        hi1h = sb("hi1h", [P, 2, HIST, GROUPS], BF16)
        hist = sb("hist", [GROUPS, 3, P])
        row_pre = sb("row_pre", [GROUPS, 1])
        deg_n = sb("deg_n", [P, GROUPS])
        off_n = sb("off_n", [P, GROUPS])
        bucket = sb("bucket", [P, GROUPS])
        bkt_count = sb("bkt_count", [P, GROUPS])
        bkt_sum = sb("bkt_sum", [P, GROUPS])
        bkt_first = sb("bkt_first", [P, 1])
        bkt_base = sb("bkt_base", [P, GROUPS])
        zeros = sb("zeros", [P, P])
        rank = sb("rank", [P, GROUPS])
        sort_tmp = sb("sort_tmp", [P, 4, P])
        rank_i = sb("rank_i", [P, 3, GROUPS], I32)
        meta = sb("meta", [P, GROUPS, 4], I32)
        deg_p = sb("deg_p", [P, GROUPS])
        deg_t = sb("deg_t", [GROUPS, P])
        kmax = sb("kmax", [GROUPS, 1])
        kmax_i = sb("kmax_i", [GROUPS, 1], I32)
        cum_f = sb("cum_f", [1, GROUPS + 2])
        cum_at = sb("cum_at", [1, GROUPS + 2], I32)
        run_f = sb("run_f", [P, RUN])
        run_m = sb("run_m", [P, RUN])
        long_off = sb("long_off", [P, 2])
        long_idx = sb("long_idx", [P, 1], I32)
        long_raw = sb("long_raw", [P, SLOTS], I32)
        long_dummy = sb("long_dummy", [P, SLOTS], I32)
        long_meta = sb("long_meta", [P, 2], I32)

        w_in = sb("w_in", [P, H])
        b_in_r = sb("b_in_r", [1, H])
        rt_w = sb("rt_w", [P, LAYERS, 4, NE + 1])
        rt_b = sb("rt_b", [1, LAYERS, NE + 1])
        b1_rows = sb("b1_rows", [LAYERS * NS * 4, P])
        b1_t = sb("b1_t", [P, LAYERS * NS * 4])
        wk_b = sb("wk_b", [1, NW * H])
        b2_w = sb("b2_w", [NE, H])
        w_out = sb("w_out", [P, 2, IN])
        b_out_r = sb("b_out_r", [1, IN])
        gat_w = [sb(f"gat_w{i}", [P, P + 2 * HEADS]) for i in range(2)]
        gat_a = [sb(f"gat_a{i}", [P, 2 * HEADS]) for i in range(2)]
        gat_b = [sb(f"gat_b{i}", [P, P]) for i in range(2)]
        gat_wt = sb("gat_wt", [P, P])

        h_cur = sb("h_cur", [P, H])
        h_t = sb("h_t", [P, H])
        agg = sb("agg", [P, H])
        agg_t = sb("agg_t", [P, H])
        part = sb("part", [P, H])
        strong = sb("strong", [P, NS, 4, P])
        weak = sb("weak", [P, NW, H])
        logit = sb("logit", [P, NE + 1])
        top = sb("top", [P, 8])
        top_at = sb("top_at", [P, 8], U32)
        top_f = sb("top_f", [P, 2])
        ex_in = sb("ex_in", [P, 2])
        ex = sb("ex", [P, 2])
        gate_n = sb("gate_n", [P, 4])
        gate_ab = sb("gate_ab", [P, 2, NE])
        gates = sb("gates", [P, NE])
        gates_t = sb("gates_t", [NE, P])
        x1 = sb("x1", [P, IN])
        x1_t = sb("x1_t", [P, IN])
        ln_z = sb("ln_z", [P, IN])
        ln_st = sb("ln_st", [P, 6])
        ln_mv = sb("ln_mv", [P, 2])
        ln_r = sb("ln_r", [P, 3])
        ad_cur = sb("ad_cur", [P, HEADS])
        score = sb("score", [P, SLOTS + 1, HEADS])
        m_new = sb("m_new", [P, HEADS])
        shifted = sb("shifted", [P, SLOTS + 1, HEADS])
        terms = sb("terms", [P, SLOTS + 1, HEADS, HC])
        gacc = sb("gacc", [P, HEADS, HC])
        rden = sb("rden", [P, HEADS])
        y = sb("y", [P, P])
        y_neg = sb("y_neg", [P, P])
        y_exp = sb("y_exp", [P, P])

        def bank(name):
            return ctx.enter_context(nc.psum_tensor(name, [P, 512], F32))

        ps_w1 = [bank("ps_w1a"), bank("ps_w1b")]
        ps_weak = [bank("ps_weak_a"), bank("ps_weak_b")]
        ps_gate = bank("ps_gate")
        ps_moe = bank("ps_moe")
        ps_tr = bank("ps_tr")
        ps_sum = bank("ps_sum")
        acc = ps_sum[:, 0:H]

        s_const, s_ints, s_par, s_xin, s_dummy, s_wts = (sem(n) for n in (
            "s_const", "s_ints", "s_par", "s_xin", "s_dummy", "s_wts"))
        s_keys, s_1h, s_1h_used, s_hist, s_tot, s_pre, s_off, s_offT = (sem(n) for n in (
            "s_keys", "s_1h", "s_1h_used", "s_hist", "s_tot", "s_pre", "s_off", "s_offT"))
        s_bkt, s_bsum, s_bscan, s_below, s_base, s_own, s_rank, s_meta, s_scat, s_perm = (sem(n) for n in (
            "s_bkt", "s_bsum", "s_bscan", "s_below", "s_base", "s_own", "s_rank", "s_meta", "s_scat", "s_perm"))
        s_runs, s_hperm, s_xperm, s_degp, s_degT, s_kmax, s_cumP, s_cum, s_slots, s_slotst, s_long, s_longrun, s_longst = (sem(n) for n in (
            "s_runs", "s_hperm", "s_xperm", "s_degp", "s_degT", "s_kmax", "s_cumP", "s_cum", "s_slots",
            "s_slotst", "s_long", "s_longrun", "s_longst"))
        s_xc, s_xT, s_xTs, s_h0, s_h0s, s_h0st, s_prep, s_prepP = (sem(n) for n in (
            "s_xc", "s_xT", "s_xTs", "s_h0", "s_h0s", "s_h0st", "s_prep", "s_prepP"))
        gathered = [sem(f"gathered{u}") for u in range(UNITS)]
        staged = [sem(f"staged{h}") for h in range(2)]
        half_begun, arrived, round_gathered, ring_free, table_done = (sem(n) for n in (
            "half_begun", "arrived", "round_gathered", "ring_free", "table_done"))
        hcur_ready, hT_ready, hT_copied = sem("hcur_ready"), sem("hT_ready"), sem("hT_copied")
        agg_ready, aggT_ready, aggT_copied = sem("agg_ready"), sem("aggT_ready"), sem("aggT_copied")
        logits_ready, top_ready, exp_ready, gates_ready = (sem(n) for n in (
            "logits_ready", "top_ready", "exp_ready", "gates_ready"))
        w1_ready, relu_ready, gated, w2_ready = sem("w1_ready"), sem("relu_ready"), sem("gated"), sem("w2_ready")
        weak_ready, weak_copied, weak_added = sem("weak_ready"), sem("weak_copied"), sem("weak_added")
        bcast_ready, gatesT_copied, h_done = sem("bcast_ready"), sem("gatesT_copied"), sem("h_done")
        b_out_ready, var_ready, rstd_ready, x1_ready, x1T_ready, x1T_copied, row_ready, row_done = (sem(n) for n in (
            "b_out_ready", "var_ready", "rstd_ready", "x1_ready", "x1T_ready", "x1T_copied", "row_ready",
            "row_done"))
        shift_ready, p_ready, neg_ready, nexp_ready, y_ready, gvar_ready, grstd_ready, z_done = (sem(n) for n in (
            "shift_ready", "p_ready", "neg_ready", "nexp_ready", "y_ready", "gvar_ready", "grstd_ready",
            "z_done"))
        s_out = sem("s_out")

        block = ctx.enter_context(nc.Block())
        n_par = [0]

        def units_of(eng, g):
            return (eng.value_load(cum[0:1, bass.ds(g, 1)], min_val=0, max_val=UMAX),
                    eng.value_load(cum[0:1, bass.ds(g + 1, 1)], min_val=1, max_val=UMAX))

        def all_units(eng):
            return eng.value_load(cum[0:1, GROUPS:GROUPS + 1], min_val=UNITS, max_val=UMAX)

        PAR_DMAS = 5 + 4 * LAYERS + 2 * (2 + 2 * HEADS)

        @block.sync
        def _(sp):
            sp.dma_start(dst_i[:], dst.rearrange("(p t) -> p t", p=P)).then_inc(s_ints, 16)
            sp.dma_start(x_res[:], x.rearrange("(g p) n -> p g n", p=P)).then_inc(s_xin, 16)
            sp.wait_ge(s_prep, 1)

            def par(o, i):
                sp.dma_start(o, i).then_inc(s_par, 16)
                n_par[0] += 1

            par(w_in[:], W_in)
            par(b_in_r[:], b_in.rearrange("(a n) -> a n", a=1))
            par(w_out[:], W_out.rearrange("(k p) n -> p k n", p=P))
            par(b_out_r[:], b_out.rearrange("(a n) -> a n", a=1))
            par(b1_rows[:], strong_b1.rearrange("l s (c p) -> (l s c) p", p=P))
            with nc.allow_non_contiguous_dma(reason="a few columns of weights"):
                for l in range(LAYERS):
                    par(rt_w[:, l, :, 0:NE], router_W[l].rearrange("(k p) e -> p k e", p=P))
                    par(rt_w[:, l, 0:2, NE], conf_W[l].rearrange("(k p) o -> p (k o)", p=P))
                    par(rt_b[:, l, 0:NE], router_b[l:l + 1, :])
                    par(rt_b[:, l, NE:NE + 1], conf_b[l:l + 1, :])
                par(gat_w[0][:, 0:P], W1)
                par(gat_w[1][:, 0:P], W2)
                par(gat_b[0][:], b1.rearrange("(a n) -> a n", a=1).to_broadcast([P, P]))
                par(gat_b[1][:], b2.rearrange("(a n) -> a n", a=1).to_broadcast([P, P]))
                for k, (a_s, a_d) in enumerate(((a_src1, a_dst1), (a_src2, a_dst2))):
                    for h in range(HEADS):
                        rows = slice(HID * h, HID * h + HID) if k == 0 else slice(0, P)
                        vec = slice(h, h + 1) if k == 0 else slice(0, 1)
                        par(gat_a[k][rows, h:h + 1], a_s[vec, :].rearrange("a c -> c a"))
                        par(gat_a[k][rows, HEADS + h:HEADS + h + 1], a_d[vec, :].rearrange("a c -> c a"))

            sp.wait_ge(s_const, 1)
            for t in hidden_tab:
                sp.dma_start(t[DUMMY:DUMMY + 1, :], dummy_row[:, :]).then_inc(s_dummy, 16)
            for t in gat_tab:
                sp.dma_start(t[DUMMY:DUMMY + 1, 0:GW - HEADS], dummy_row[:, 0:GW - HEADS]).then_inc(s_dummy, 16)
                sp.dma_start(t[DUMMY:DUMMY + 1, GW - HEADS:GW], dummy_score[:, :]).then_inc(s_dummy, 16)

            with sp.Fori(0, GROUPS) as g:
                sp.wait_ge(s_h0s, g + 1)
                sp.dma_start(hidden_tab[0][bass.ds(g * P, P), :], h_res[:, bass.ds(g, 1), :].rearrange("p a n -> p (a n)"))\
                    .then_inc(s_h0st, 16)

            sp.wait_ge(s_scat, 16 * GROUPS)
            sp.dma_start(perm[:], meta_tab.rearrange("(p g) c -> p g c", p=P)).then_inc(s_perm, 16)
            sp.wait_ge(s_slots, 1)
            sp.dma_start(slot_tab[:, 0:COLS], slots_sb).then_inc(s_slotst, 16)
            sp.wait_ge(s_long, 1)

            total = all_units(sp)
            bodies = total // UNITS
            for r in range(LAYERS + 2):
                if r < LAYERS:
                    if r:
                        sp.wait_ge(w2_ready, r * GROUPS)
                    for k in range(2):
                        sp.dma_start(wk_w[:, k, :].rearrange("p (e n) -> p e n", e=NW),
                                     weak_W[r, :, k * P:(k + 1) * P, :].rearrange("e p n -> p e n")).then_inc(s_wts, 16)
                        sp.dma_start(w1_w[:, k, :, :],
                                     strong_W1[r, :, k * P:(k + 1) * P, :].rearrange("s p n -> p s n")).then_inc(s_wts, 16)
                    for c in range(4):
                        sp.dma_start(w2_w[:, c, :, :],
                                     strong_W2[r, :, c * P:(c + 1) * P, :].rearrange("s p n -> p s n")).then_inc(s_wts, 16)
                    sp.dma_start(wk_b[:, :], weak_b[r:r + 1].rearrange("a e n -> a (e n)")).then_inc(s_wts, 16)
                    sp.dma_start(b2_w[NW:NE, :], strong_b2[r]).then_inc(s_wts, 16)

                if r:
                    sp.wait_ge(round_gathered, r)
                for half in range(2):
                    sp.dma_start(stage[:, half, :], slot_tab[:, half * RING // 2:(half + 1) * RING // 2])\
                        .then_inc(staged[half], 16)
                with sp.Fori(1, bodies) as i:
                    for half in range(2):
                        sp.wait_ge(arrived, total * r + i * UNITS + (r + 1 - UNITS + (half + 1) * UNITS // 2))
                        sp.dma_start(stage[:, half, :], slot_tab[:, bass.ds(i * RING + half * RING // 2, RING // 2)])\
                            .then_inc(staged[half], 16)
            sp.wait_ge(s_out, 16 * GROUPS)

        @block.gpsimd
        def _(pool):
            nc.gpsimd.iota(iota_i[:], pattern=[[1, P]], base=0, channel_multiplier=0)
            nc.gpsimd.memset(dummy_row[:], 0.0)
            nc.gpsimd.memset(dummy_score[:], DUMMY_SCORE)
            nc.gpsimd.memset(rt_w[:], 0.0)
            nc.gpsimd.memset(b2_w[:], 0.0)
            nc.gpsimd.memset(gat_a[0][:], 0.0)
            nc.gpsimd.memset(gat_a[1][:], 0.0)
            nc.gpsimd.memset(ident[:], 0.0)
            nc.gpsimd.memset(tri[:], 1.0)
            nc.gpsimd.memset(ones_b[:], 1.0)
            nc.gpsimd.memset(zero_b[:], 0.0)
            nc.gpsimd.memset(ones_row[:], 1.0)
            pool.drain().then_inc(s_prep, 1)
            nc.gpsimd.tensor_copy(iota[:], iota_i[:])
            nc.gpsimd.affine_select(out=ident[:], in_=ident[:], compare_op=ALU.not_equal, fill=1.0,
                                    base=0, pattern=[[-1, P]], channel_multiplier=1)
            nc.gpsimd.affine_select(out=tri[:], in_=tri[:], compare_op=ALU.is_gt, fill=0.0,
                                    base=0, pattern=[[1, P]], channel_multiplier=-1)
            pool.drain()
            nc.gpsimd.tensor_copy(iota_b[:], iota[:])
            nc.gpsimd.tensor_copy(tri_b[:], tri[:])
            nc.gpsimd.iota(meta[:, :, 0], pattern=[[P, GROUPS]], base=0, channel_multiplier=1)
            nc.gpsimd.memset(meta[:, :, 3], 0)
            nc.gpsimd.memset(long_dummy[:], DUMMY)
            pool.drain().then_inc(s_const, 1)

            pool.wait_ge(s_meta, 1)
            for g in range(GROUPS):
                pool.indirect_dma_start(out=meta_tab, out_offset=bass.IndirectOffsetOnAxis(ap=rank_i[:, 2, g:g + 1], axis=0),
                                        in_=meta[:, g, :], in_offset=None).then_inc(s_scat, 16)
            pool.wait_ge(s_perm, 16)
            for g in range(GROUPS):
                pool.indirect_dma_start(out=run_raw[:, g, :], out_offset=None, in_=src.rearrange("(a e) -> a e", a=1),
                                        in_offset=bass.IndirectOffsetOnAxis(ap=perm[:, g, 1:2], axis=1))\
                    .then_inc(gathered[UNITS - 1] if g < SLOTS else s_runs, 16)
            pool.wait_ge(s_h0st, 16 * GROUPS)
            for g in range(GROUPS):
                pool.indirect_dma_start(out=h_res[:, g, :], out_offset=None, in_=hidden_tab[0],
                                        in_offset=bass.IndirectOffsetOnAxis(ap=perm[:, g, 0:1], axis=0)).then_inc(s_hperm, 16)

            pool.wait_ge(s_slotst, 16)
            pool.wait_ge(s_cum, 1)
            most = pool.value_load(cum[0:1, GROUPS + 1:GROUPS + 2], min_val=1, max_val=E)
            with pool.If(most > RUN // SLOTS):
                with pool.Fori(0, GROUPS) as g:
                    c0, c1 = units_of(pool, g)
                    nc.gpsimd.tensor_copy(long_meta[:], perm[:, bass.ds(g, 1), 1:3].rearrange("p a n -> p (a n)"))
                    pool.drain()
                    nc.gpsimd.tensor_copy(long_off[:], long_meta[:])
                    with pool.Fori(c0, c1) as c:
                        pool.drain()
                        nc.gpsimd.tensor_scalar(long_off[:, 0:1], long_off[:, 0:1], float(E), None, ALU.min)
                        pool.drain()
                        nc.gpsimd.tensor_copy(long_idx[:], long_off[:, 0:1])
                        pool.drain()
                        pool.indirect_dma_start(out=long_raw[:], out_offset=None, in_=src.rearrange("(a e) -> a e", a=1),
                                                in_offset=bass.IndirectOffsetOnAxis(ap=long_idx[:, 0:1], axis=1)).then_inc(s_longrun, 16)
                        pool.wait_ge(s_longrun, c * 16 + 16)
                        nc.gpsimd.tensor_tensor(long_raw[:], long_raw[:], long_dummy[:], ALU.subtract)
                        pool.drain()
                        nc.gpsimd.tensor_copy(run_f[:, 0:SLOTS], long_raw[:])
                        nc.gpsimd.tensor_scalar(run_m[:, 0:SLOTS], iota[:, 0:SLOTS], long_off[:, 1:2], None, ALU.is_lt)
                        pool.drain()
                        nc.gpsimd.tensor_tensor(run_f[:, 0:SLOTS], run_f[:, 0:SLOTS], run_m[:, 0:SLOTS], ALU.mult)
                        pool.drain()
                        nc.gpsimd.tensor_scalar(long_raw[:], run_f[:, 0:SLOTS], float(DUMMY), None, ALU.add)
                        pool.drain()
                        pool.dma_start(slot_tab[:, bass.ds(c * SLOTS, SLOTS)], long_raw[:]).then_inc(s_longst, 16)
                        nc.gpsimd.tensor_scalar(long_off[:, 0:1], long_off[:, 0:1], float(SLOTS), None, ALU.add)
                        nc.gpsimd.tensor_scalar(long_off[:, 1:2], long_off[:, 1:2], float(-SLOTS), None, ALU.add)
                        pool.wait_ge(s_longst, c * 16 + 16)
            pool.drain().then_inc(s_long, 1)

            pool.wait_ge(s_dummy, 16 * (LAYERS + 4))
            total = all_units(pool)
            bodies = total // UNITS
            for r in range(LAYERS + 2):
                table = hidden_tab[r] if r < LAYERS else gat_tab[r - LAYERS]
                width = H if r < LAYERS else GW
                with pool.Fori(bodies * r, bodies * (r + 1)) as i:
                    for b in range(RING):
                        if b % (RING // 2) == 0:
                            pool.wait_ge(staged[b * 2 // RING], i * 16 + 16)
                            pool.sem_inc(half_begun, 1)
                        if b % SLOTS == SLOTS // 2:
                            pool.wait_ge(ring_free, i * UNITS + (b // SLOTS + 2))
                            pool.wait_ge(gathered[(b // SLOTS - 1) % UNITS], i * (16 * SLOTS) + 16 * SLOTS)
                            pool.sem_inc(arrived, 1)
                        pool.indirect_dma_start(out=ring[:, b, 0:width], out_offset=None, in_=table,
                                                in_offset=bass.IndirectOffsetOnAxis(ap=stage[:, b * 2 // RING, b % (RING // 2):b % (RING // 2) + 1], axis=0))\
                            .then_inc(gathered[b // SLOTS], 16)
                pool.wait_ge(gathered[UNITS - 1], bodies * (16 * SLOTS * (r + 1)) + 16 * SLOTS)
                pool.sem_inc(arrived, 1)
                pool.sem_inc(round_gathered, 1)
                if r == LAYERS - 1:
                    for g in range(GROUPS):
                        pool.indirect_dma_start(out=x_res[:, g, :], out_offset=None, in_=x,
                                                in_offset=bass.IndirectOffsetOnAxis(ap=perm[:, g, 0:1], axis=0)).then_inc(s_xperm, 16)
                for g in range(GROUPS):
                    ids = bass.IndirectOffsetOnAxis(ap=perm[:, g, 0:1], axis=0)
                    if r < LAYERS - 1:
                        pool.wait_ge(h_done, r * GROUPS + g + 1)
                        pool.indirect_dma_start(out=hidden_tab[r + 1], out_offset=ids, in_=h_res[:, g, :], in_offset=None)\
                            .then_inc(table_done, 16)
                    elif r < LAYERS + 1:
                        pool.wait_ge(row_done, (r - LAYERS + 1) * GROUPS + g + 1)
                        pool.indirect_dma_start(out=gat_tab[r - LAYERS + 1], out_offset=ids, in_=gat_rows[:, g, :], in_offset=None)\
                            .then_inc(table_done, 16)
                    else:
                        pool.wait_ge(z_done, g + 1)
                        pool.indirect_dma_start(out=out, out_offset=ids, in_=x_res[:, g, :], in_offset=None)\
                            .then_inc(s_out, 16)
                if r < LAYERS + 1:
                    pool.wait_ge(table_done, 16 * GROUPS * (r + 1))

        @block.vector
        def _(dve):
            dve.sem_inc(ring_free, UNITS)
            nc.vector.memset(zeros[:], 0.0)
            nc.vector.memset(slots_sb, DUMMY)
            dve.wait_ge(s_ints, 16)
            dve.wait_ge(s_const, 1)
            nc.vector.tensor_scalar(lo_i, dst_i[:], 127, None, ALU.bitwise_and)
            nc.vector.tensor_scalar(dst_i[:], dst_i[:], 7, None, ALU.logical_shift_right)
            dve.drain()
            nc.vector.tensor_copy(lo_f, lo_i)
            nc.vector.tensor_copy(hi_f, dst_i[:])
            dve.drain()
            dve.sem_inc(s_1h_used, 2)
            with dve.Fori(0, ET // (2 * HIST)) as i:
                for half in range(2):
                    dve.wait_ge(s_1h_used, i * 2 + (half + 1))
                    for t in range(HIST):
                        at = bass.ds(i * 2 * HIST + (half * HIST + t), 1)
                        nc.vector.tensor_scalar(lo1h[:, half, t, :], iota_b[:], lo_f[:, at], None, ALU.is_equal)
                        last = nc.vector.tensor_scalar(hi1h[:, half, t, :], iota_b[:, 0:GROUPS], hi_f[:, at], None, ALU.is_equal)
                    last.then_inc(s_1h, 1)
            dve.wait_ge(s_hist, 1)
            nc.vector.tensor_copy(hist[:, 0, :], ps_sum[0:GROUPS, 0:P])
            dve.drain()
            nc.vector.tensor_tensor_scan(hist[:, 1, :], hist[:, 0, :], zeros[0:GROUPS, :], 0.0, ALU.add, ALU.add)
            dve.drain().then_inc(s_tot, 1)
            dve.wait_ge(s_pre, 1)
            nc.vector.tensor_copy(row_pre[:], ps_sum[0:GROUPS, 256:257])
            dve.drain()
            nc.vector.scalar_tensor_tensor(hist[:, 2, :], hist[:, 1, :], row_pre[:], hist[:, 0, :], ALU.add, ALU.subtract)
            dve.drain().then_inc(s_off, 1)
            dve.wait_ge(s_offT, 1)
            nc.vector.tensor_copy(deg_n[:], ps_tr[:, 0:GROUPS])
            nc.vector.tensor_copy(off_n[:], ps_tr[:, P:P + GROUPS])
            dve.drain()
            nc.vector.tensor_scalar(bucket[:], deg_n[:], float(P - 1), None, ALU.min)
            dve.drain()
            for g in range(GROUPS):
                last = nc.vector.tensor_scalar(bucket1h[:, g, :], iota_b[:], bucket[:, g:g + 1], None, ALU.is_equal)
            last.then_inc(s_bkt, 1)
            dve.wait_ge(s_bsum, 1)
            nc.vector.tensor_copy(bkt_count[:], ps_sum[:, 0:GROUPS])
            dve.drain()
            nc.vector.tensor_tensor_scan(bkt_sum[:], bkt_count[:], zeros[:, 0:GROUPS], 0.0, ALU.add, ALU.add)
            dve.drain().then_inc(s_bscan, 1)
            dve.wait_ge(s_below, 1)
            nc.vector.tensor_tensor(bkt_first[:], ps_sum[:, 128:129], bkt_sum[:, GROUPS - 1:GROUPS], ALU.add)
            dve.drain()
            nc.vector.tensor_scalar(bkt_first[:], bkt_first[:], -1.0, float(NP), ALU.mult, ALU.add)
            dve.drain()
            nc.vector.scalar_tensor_tensor(bkt_base[:], bkt_sum[:], bkt_first[:], bkt_count[:], ALU.add, ALU.subtract)
            dve.drain().then_inc(s_base, 1)
            for g in range(GROUPS):
                dve.wait_ge(s_own, g + 1)
                nc.vector.tensor_tensor_reduce(out=sort_tmp[:, g % 4, :], in0=(ps_gate, ps_moe)[g % 2][:, 0:P], in1=bucket1h[:, g, :],
                                               scale=1.0, scalar=0.0, op0=ALU.mult, op1=ALU.add,
                                               accum_out=rank[:, g:g + 1]).then_inc(s_rank, 1)
                if g >= 3:
                    dve.wait_ge(s_rank, g - 2)
            dve.wait_ge(s_rank, GROUPS)
            nc.vector.tensor_copy(rank_i[:, 0, :], rank[:])
            dve.drain()
            nc.vector.tensor_scalar(rank_i[:, 1, :], rank_i[:, 0, :], P - 1, None, ALU.bitwise_and)
            nc.vector.tensor_scalar(rank_i[:, 0, :], rank_i[:, 0, :], 7, None, ALU.logical_shift_right)
            dve.drain()
            nc.vector.scalar_tensor_tensor(rank_i[:, 2, :], rank_i[:, 1, :], float(GROUPS), rank_i[:, 0, :], ALU.mult, ALU.add)
            nc.vector.tensor_copy(meta[:, :, 1], off_n[:])
            nc.vector.tensor_copy(meta[:, :, 2], deg_n[:])
            dve.drain().then_inc(s_meta, 1)
            dve.wait_ge(s_perm, 16)
            nc.vector.tensor_copy(deg_p[:], perm[:, :, 2])
            dve.drain().then_inc(s_degp, 1)
            nc.vector.tensor_copy(loop_cap[:], perm[:, :, 0])
            dve.drain()
            nc.vector.tensor_scalar(loop_on[:], loop_cap[:], float(LOOPS), None, ALU.is_lt)
            dve.drain()
            nc.vector.tensor_scalar(loop_cap[:], loop_on[:], -0.5, -2.0 * LOWEST, ALU.add, ALU.mult)
            nc.vector.tensor_scalar(rdeg[:], deg_p[:], 1.0, None, ALU.max)
            dve.drain()
            nc.vector.reciprocal(rdeg[:], rdeg[:])
            dve.wait_ge(s_degT, 1)
            nc.vector.tensor_reduce(kmax[:], ps_tr[0:GROUPS, 256:384], AX.X, ALU.max)
            dve.drain()
            nc.vector.tensor_scalar(kmax_i[:], kmax[:], 1.0, float(SLOTS - 1), ALU.max, ALU.add)
            dve.drain()
            nc.vector.tensor_scalar(kmax_i[:], kmax_i[:], SLOTS.bit_length() - 1, None, ALU.logical_shift_right)
            dve.drain()
            nc.vector.tensor_copy(kmax[:], kmax_i[:])
            dve.drain().then_inc(s_kmax, 1)
            dve.wait_ge(s_cumP, 1)
            nc.vector.tensor_copy(cum_f[:, 0:GROUPS + 1], ps_sum[0:1, 128:128 + GROUPS + 1])
            nc.vector.tensor_reduce(cum_f[:, GROUPS + 1:GROUPS + 2], ps_sum[0:1, 256:256 + GROUPS], AX.X, ALU.max)
            dve.drain()
            nc.vector.tensor_copy(cum[:], cum_f[:])
            nc.vector.tensor_scalar(cum_at[:], cum_f[:], float(SLOTS), float(COLS - RUN), ALU.mult, ALU.min)
            dve.drain()
            nc.vector.tensor_scalar(cum[:, GROUPS:GROUPS + 1], cum_f[:, GROUPS:GROUPS + 1], float(UNITS - 1), None, ALU.add)
            dve.drain()
            nc.vector.tensor_scalar(cum[:, GROUPS:GROUPS + 1], cum[:, GROUPS:GROUPS + 1], UNITS.bit_length() - 1,
                                    UNITS.bit_length() - 1, ALU.logical_shift_right, ALU.logical_shift_left)
            dve.drain().then_inc(s_cum, 1)
            dve.wait_ge(gathered[UNITS - 1], 16 * SLOTS)
            dve.wait_ge(s_runs, 16 * (GROUPS - SLOTS))
            with dve.Fori(0, GROUPS) as g:
                at = dve.value_load(cum_at[0:1, bass.ds(g, 1)], min_val=0, max_val=COLS - RUN)
                nc.vector.tensor_scalar(run_f[:], run_raw[:, bass.ds(g, 1), :].rearrange("p a k -> p (a k)"), float(-DUMMY), None, ALU.add)
                dve.drain()
                nc.vector.scalar_tensor_tensor(run_m[:], iota[:, 0:RUN], deg_p[:, bass.ds(g, 1)], run_f[:], ALU.is_lt, ALU.mult)
                dve.drain()
                nc.vector.tensor_scalar(slots_sb[:, bass.ds(at, RUN)], run_m[:], float(DUMMY), None, ALU.add)
                dve.drain()
            dve.drain().then_inc(s_slots, 1)

            total = all_units(dve)

            def aggregate(r, g):
                n = g + r * GROUPS
                c0, c1 = units_of(dve, g)
                dve.drain()
                nc.vector.memset(acc, 0.0)
                with dve.Fori(total * r + c0, total * r + c1) as q:
                    dve.drain()
                    dve.wait_ge(arrived, q + (r + 2))
                    nc.vector.tensor_reduce(part[:], ring[:, bass.ds((q % UNITS) * SLOTS, SLOTS), :].rearrange("p s n -> p n s"),
                                            AX.X, ALU.add).then_inc(ring_free, 1)
                    dve.drain()
                    nc.vector.tensor_tensor(acc, acc, part[:], ALU.add)
                dve.drain()
                w(dve, aggT_ready, n)
                nc.vector.tensor_scalar(agg[:], acc, rdeg[:, bass.ds(g, 1)], None, ALU.mult).then_inc(agg_ready, 1)

            def gate_experts(r, g):
                n = g + r * GROUPS
                dve.wait_ge(bcast_ready, n + 1)
                for s in range(NS):
                    dve.wait_ge(relu_ready, n * NS + (s + 1))
                    nc.vector.tensor_tensor(strong[:, s, :, :], strong[:, s, :, :],
                                            ps_gate[:, s * P:(s + 1) * P].unsqueeze(1).to_broadcast([P, 4, P]), ALU.mult).then_inc(gated, 1)
                dve.wait_ge(weak_copied, n + 1)
                nc.vector.tensor_reduce(part[:], weak[:].rearrange("p e n -> p n e"), AX.X, ALU.add).then_inc(weak_added, 1)
                dve.drain()
                hg = h_res[:, bass.ds(g, 1), :].rearrange("p a n -> p (a n)")
                nc.vector.tensor_tensor(hg, hg, part[:], ALU.add)

            def add_strong(r, g):
                dve.drain()
                dve.wait_ge(w2_ready, g + (r * GROUPS + 1))
                hg = h_res[:, bass.ds(g, 1), :].rearrange("p a n -> p (a n)")
                nc.vector.tensor_tensor(hg, hg, ps_moe[:, 0:H], ALU.add).then_inc(h_done, 1)

            def choose(r, g):
                n = g + r * GROUPS
                dve.wait_ge(logits_ready, n + 1)
                nc.vector.tensor_copy(logit[:], ps_tr[:, H:H + NE + 1])
                dve.drain()
                nc.vector.max(top[:], logit[:, 0:NE])
                dve.drain()
                nc.vector.max_index(top_at[:], top[:], logit[:, 0:NE])
                nc.vector.tensor_tensor(ex_in[:, 0:1], top[:, 1:2], top[:, 0:1], ALU.subtract)
                nc.vector.tensor_scalar(ex_in[:, 1:2], logit[:, NE:NE + 1], -1.0, None, ALU.mult)
                dve.drain().then_inc(top_ready, 1)
                nc.vector.tensor_copy(top_f[:], top_at[:, 0:2])
                dve.wait_ge(exp_ready, n + 1)
                nc.vector.tensor_scalar(gate_n[:, 0:2], ex[:], 1.0, None, ALU.add)
                dve.drain()
                nc.vector.reciprocal(gate_n[:, 0:2], gate_n[:, 0:2])
                dve.drain()
                nc.vector.tensor_tensor(gate_n[:, 2:3], gate_n[:, 0:1], gate_n[:, 1:2], ALU.mult)
                dve.drain()
                nc.vector.tensor_tensor(gate_n[:, 3:4], gate_n[:, 2:3], ex[:, 0:1], ALU.mult)
                dve.drain()
                for k in range(2):
                    nc.vector.tensor_scalar(gate_ab[:, k, :], iota[:, 0:NE], top_f[:, k:k + 1], gate_n[:, 2 + k:3 + k], ALU.is_equal, ALU.mult)
                dve.drain()
                nc.vector.tensor_tensor(gates[:], gate_ab[:, 0, :], gate_ab[:, 1, :], ALU.add).then_inc(gates_ready, 1)

            dve.wait_ge(s_hperm, 16 * GROUPS)
            for r in range(LAYERS):
                aggregate(r, 0)
                choose(r, 0)
                aggregate(r, 1)
                gate_experts(r, 0)
                choose(r, 1)
                with dve.Fori(2, GROUPS) as g:
                    aggregate(r, g)
                    gate_experts(r, g - 1)
                    add_strong(r, g - 2)
                    choose(r, g)
                gate_experts(r, GROUPS - 1)
                add_strong(r, GROUPS - 2)
                add_strong(r, GROUPS - 1)

            def moments(z):
                nc.vector.bn_stats(ln_st[:], z)
                dve.drain()
                nc.vector.bn_aggr(ln_mv[:], ln_st[:])
                dve.drain()
                nc.vector.tensor_scalar(ln_r[:, 0:1], ln_mv[:, 1:2], EPS_LN, None, ALU.add)

            nc.vector.memset(gat_rows, 1.0)
            dve.wait_ge(s_xperm, 16 * GROUPS)
            dve.drain().then_inc(row_ready, 1)
            with dve.Fori(0, GROUPS) as g:
                xg = x_res[:, bass.ds(g, 1), :].rearrange("p a n -> p (a n)")
                dve.wait_ge(b_out_ready, g + 1)
                nc.vector.tensor_tensor(ln_z[:], ps_moe[:, 0:IN], xg, ALU.add)
                dve.drain()
                moments(ln_z[:])
                dve.drain().then_inc(var_ready, 1)
                dve.wait_ge(rstd_ready, g + 1)
                nc.vector.tensor_scalar(x1[:], ln_z[:], ln_mv[:, 0:1], ln_r[:, 2:3], ALU.subtract, ALU.mult)
                dve.drain().then_inc(x1_ready, 1)
                nc.vector.tensor_copy(xg, x1[:])
                dve.drain()
                dve.wait_ge(x1T_ready, g + 1)

            for k in range(2):
                r = LAYERS + k
                with dve.Fori(0, GROUPS) as g:
                    n = g + k * GROUPS
                    c0, c1 = units_of(dve, g)
                    dve.wait_ge(row_done, n + 1)
                    own = gat_rows[:, bass.ds(g, 1), :].rearrange("p a n -> p (a n)")
                    target = ad[k][:, bass.ds(g, 1), :].rearrange("p a n -> p (a n)")
                    nc.vector.tensor_copy(ad_cur[:], target)
                    nc.vector.tensor_tensor(m_new[:], own[:, GW - HEADS:GW], target, ALU.add)
                    nc.vector.tensor_scalar(gacc[:].rearrange("p h c -> p (h c)"), own[:, 0:HEADS * HC], loop_on[:, bass.ds(g, 1)], None, ALU.mult)
                    dve.drain()
                    nc.vector.scalar_tensor_tensor(m_new[:], m_new[:], 0.2, m_new[:], ALU.mult, ALU.max)
                    dve.drain()
                    nc.vector.tensor_scalar(score[:, SLOTS, :], m_new[:], loop_cap[:, bass.ds(g, 1)], None, ALU.min)
                    with dve.Fori(total * k + c0, total * k + c1) as q:
                        rows = ring[:, bass.ds((q % UNITS) * SLOTS, SLOTS), 0:GW]
                        dve.drain()
                        dve.wait_ge(arrived, total * LAYERS + q + (r + 2))
                        nc.vector.tensor_tensor(score[:, 0:SLOTS, :], rows[:, :, GW - HEADS:GW],
                                                ad_cur[:].unsqueeze(1).to_broadcast([P, SLOTS, HEADS]), ALU.add)
                        dve.drain()
                        nc.vector.scalar_tensor_tensor(score[:, 0:SLOTS, :], score[:, 0:SLOTS, :], 0.2, score[:, 0:SLOTS, :], ALU.mult, ALU.max)
                        dve.drain()
                        nc.vector.tensor_reduce(m_new[:], score[:].rearrange("p s h -> p h s"), AX.X, ALU.max)
                        dve.drain()
                        nc.vector.tensor_tensor(shifted[:], score[:], m_new[:].unsqueeze(1).to_broadcast([P, SLOTS + 1, HEADS]), ALU.subtract)
                        dve.drain().then_inc(shift_ready, 1)
                        nc.vector.tensor_copy(score[:, SLOTS, :], m_new[:])
                        dve.wait_ge(p_ready, q + 1)
                        p = ps_gate[:, 0:(SLOTS + 1) * HEADS].rearrange("p (s h) -> p s h", h=HEADS)
                        nc.vector.tensor_tensor(terms[:, SLOTS, :, :], gacc[:], p[:, SLOTS, :].unsqueeze(2).to_broadcast([P, HEADS, HC]), ALU.mult)
                        nc.vector.tensor_tensor(terms[:, 0:SLOTS, :, :], rows[:, :, 0:HEADS * HC].rearrange("p s (h c) -> p s h c", c=HC),
                                                p[:, 0:SLOTS, :].unsqueeze(3).to_broadcast([P, SLOTS, HEADS, HC]), ALU.mult).then_inc(ring_free, 1)
                        dve.drain()
                        nc.vector.tensor_reduce(gacc[:].rearrange("p h c -> p (h c)"), terms[:].rearrange("p s h c -> p (h c) s"), AX.X, ALU.add)
                    dve.drain()
                    nc.vector.tensor_scalar(rden[:], gacc[:, :, HID], EPS_GAT, None, ALU.add)
                    dve.drain()
                    nc.vector.reciprocal(rden[:], rden[:])
                    dve.drain()
                    nc.vector.tensor_tensor(y[:].rearrange("p (h c) -> p h c", c=HID), gacc[:, :, 0:HID],
                                            rden[:].unsqueeze(2).to_broadcast([P, HEADS, HID]), ALU.mult)
                    dve.drain()
                    nc.vector.tensor_tensor(y[:], y[:], gat_b[k][:], ALU.add)
                    dve.drain()
                    if k == 0:
                        nc.vector.tensor_scalar(y_neg[:], y[:], 0.0, None, ALU.min)
                        dve.drain().then_inc(neg_ready, 1)
                        nc.vector.tensor_scalar(y[:], y[:], 0.0, -1.0, ALU.max, ALU.add)
                        dve.drain()
                        dve.wait_ge(nexp_ready, g + 1)
                        dve.wait_ge(x1T_ready, g + GROUPS)
                        nc.vector.tensor_tensor(x1[:], y[:], y_exp[:], ALU.add).then_inc(x1_ready, 1)
                    else:
                        xg = x_res[:, bass.ds(g, 1), :].rearrange("p a n -> p (a n)")
                        nc.vector.tensor_tensor(ln_z[:], y[:], xg, ALU.add)
                        dve.drain()
                        moments(ln_z[:])
                        dve.drain().then_inc(var_ready, 1)
                        dve.wait_ge(rstd_ready, g + (GROUPS + 1))
                        nc.vector.tensor_scalar(xg, ln_z[:], ln_mv[:, 0:1], ln_r[:, 2:3], ALU.subtract, ALU.mult).then_inc(z_done, 1)

        @block.scalar
        def _(act):
            act.wait_ge(s_xin, 16)
            with act.Fori(0, GROUPS) as g:
                nc.scalar.activation(x1[:], x_res[:, bass.ds(g, 1), :].rearrange("p a n -> p (a n)"), ACT.Copy).then_inc(s_xc, 1)
                act.wait_ge(s_xT, g + 1)
                nc.scalar.activation(h_t[:, 0:P], ps_w1[0][:, 0:P], ACT.Copy).then_inc(s_xTs, 1)
                act.wait_ge(s_h0, g + 1)
                nc.scalar.activation(h_res[:, bass.ds(g, 1), :].rearrange("p a n -> p (a n)"), ps_w1[1][:, 0:H], ACT.Copy).then_inc(s_h0s, 1)
            act.wait_ge(s_prepP, 1)
            nc.scalar.activation(b1_t[:], ps_weak[0][:, 0:LAYERS * NS * 4], ACT.Copy)
            act.drain().then_inc(s_prepP, 1)
            for k in range(2):
                act.wait_ge(s_prepP, 3 + 4 * k)
                nc.scalar.activation(gat_wt[:], ps_weak[0][:, 128:256], ACT.Copy)
                act.drain().then_inc(s_prepP, 1)
                act.wait_ge(s_prepP, 5 + 4 * k)
                nc.scalar.activation(gat_w[k][:, P:P + 2 * HEADS], ps_weak[1][:, 0:2 * HEADS], ACT.Copy)
                act.drain().then_inc(s_prepP, 1)

            def experts(r, g):
                n = g + r * GROUPS
                if r == 0:
                    act.wait_ge(s_hperm, 16 * GROUPS)
                else:
                    act.wait_ge(h_done, g + ((r - 1) * GROUPS + 1))
                w(act, hT_ready, n)
                nc.scalar.activation(h_cur[:], h_res[:, bass.ds(g, 1), :].rearrange("p a n -> p (a n)"), ACT.Copy).then_inc(hcur_ready, 1)
                act.wait_ge(hT_ready, n + 1)
                w(act, logits_ready, n)
                nc.scalar.activation(h_t[:], ps_tr[:, 0:H], ACT.Copy).then_inc(hT_copied, 1)
                act.wait_ge(aggT_ready, n + 1)
                w(act, weak_ready, n)
                nc.scalar.activation(agg_t[:], ps_tr[:, 0:H], ACT.Copy).then_inc(aggT_copied, 1)
                act.wait_ge(top_ready, n + 1)
                nc.scalar.activation(ex[:], ex_in[:], ACT.Exp).then_inc(exp_ready, 1)
                w(act, w2_ready, n)
                for s in range(NS):
                    act.wait_ge(w1_ready, n * NS + (s + 1))
                    for c in range(4):
                        j = (r * NS + s) * 4 + c
                        last = nc.scalar.activation(strong[:, s, c, :], ps_w1[s % 2][:, c * P:(c + 1) * P], ACT.Relu, bias=b1_t[:, j:j + 1])
                    last.then_inc(relu_ready, 1)
                act.wait_ge(bcast_ready, n + 1)
                nc.scalar.activation(gates_t[:], ps_tr[0:NE, 384:512], ACT.Copy).then_inc(gatesT_copied, 1)
                act.wait_ge(weak_ready, n + 1)
                act.wait_ge(gates_ready, n + 1)
                w(act, weak_added, n)
                for e in range(NW):
                    last = nc.scalar.activation(weak[:, e, :], ps_weak[e // 2][:, (e % 2) * H:(e % 2 + 1) * H], ACT.Relu, scale=gates[:, e:e + 1])
                last.then_inc(weak_copied, 1)

            for r in range(LAYERS):
                experts(r, 0)
                with act.Fori(1, GROUPS) as g:
                    experts(r, g)

            def rstd(count):
                act.wait_ge(var_ready, count)
                nc.scalar.activation(ln_r[:, 1:2], ln_r[:, 0:1], ACT.Ln)
                act.drain()
                nc.scalar.activation(ln_r[:, 2:3], ln_r[:, 1:2], ACT.Exp, scale=-0.5).then_inc(rstd_ready, 1)

            def table_row(k, g):
                n = g + k * GROUPS
                act.wait_ge(x1T_ready, n + 1)
                nc.scalar.activation(x1_t[:], ps_tr[:, H:H + P], ACT.Copy).then_inc(x1T_copied, 1)
                act.wait_ge(row_ready, n + 2)
                row = gat_rows[:, bass.ds(g, 1), :].rearrange("p a n -> p (a n)")
                nc.scalar.activation(row[:, 0:HEADS * HC].rearrange("p (h c) -> p h c", c=HC)[:, :, 0:HID],
                                     ps_sum[:, 0:P].rearrange("p (h c) -> p h c", c=HID), ACT.Copy)
                nc.scalar.activation(row[:, GW - HEADS:GW], ps_sum[:, P:P + HEADS], ACT.Copy)
                nc.scalar.activation(ad[k][:, bass.ds(g, 1), :].rearrange("p a n -> p (a n)"), ps_sum[:, P + HEADS:P + 2 * HEADS], ACT.Copy)
                act.drain().then_inc(row_done, 1)

            with act.Fori(0, GROUPS) as g:
                act.wait_ge(h_done, g + (LAYERS - 1) * GROUPS + 1)
                act.wait_ge(hT_ready, g + LAYERS * GROUPS)
                nc.scalar.activation(h_cur[:], h_res[:, bass.ds(g, 1), :].rearrange("p a n -> p (a n)"), ACT.Copy).then_inc(hcur_ready, 1)
                act.wait_ge(hT_ready, g + (LAYERS * GROUPS + 1))
                nc.scalar.activation(h_t[:], ps_tr[:, 0:H], ACT.Copy).then_inc(hT_copied, 1)
                rstd(g + 1)
                table_row(0, g)

            total = all_units(act)
            for k in range(2):
                with act.Fori(0, GROUPS) as g:
                    c0, c1 = units_of(act, g)
                    with act.Fori(total * k + c0, total * k + c1) as q:
                        act.wait_ge(shift_ready, q + 1)
                        nc.scalar.activation(ps_gate[:, 0:(SLOTS + 1) * HEADS], shifted[:].rearrange("p s h -> p (s h)"), ACT.Exp).then_inc(p_ready, 1)
                    if k == 0:
                        act.wait_ge(neg_ready, g + 1)
                        nc.scalar.activation(y_exp[:], y_neg[:], ACT.Exp).then_inc(nexp_ready, 1)
                        act.wait_ge(table_done, 16 * GROUPS * LAYERS)
                        table_row(1, g)
                    else:
                        rstd(g + (GROUPS + 1))

        @block.tensor
        def _(pe):
            mm = nc.tensor.matmul
            pe.wait_ge(s_const, 1)
            pe.wait_ge(s_par, 16 * PAR_DMAS)
            mm(ps_sum[0:GROUPS, 0:P], zero_b[:, 0:GROUPS], zero_b[:], start=True, stop=False)
            with pe.Fori(0, ET // (2 * HIST)) as i:
                for half in range(2):
                    pe.wait_ge(s_1h, i * 2 + (half + 1))
                    for t in range(HIST):
                        last = mm(ps_sum[0:GROUPS, 0:P], hi1h[:, half, t, :], lo1h[:, half, t, :], start=False, stop=False)
                    last.then_inc(s_1h_used, 1)
            mm(ps_sum[0:GROUPS, 0:P], zero_b[:, 0:GROUPS], zero_b[:], start=False, stop=True).then_inc(s_hist, 1)
            pe.wait_ge(s_tot, 1)
            mm(ps_sum[0:GROUPS, 256:257], tri[0:GROUPS, 0:GROUPS], hist[:, 1, P - 1:P], start=True, stop=True).then_inc(s_pre, 1)
            pe.wait_ge(s_off, 1)
            nc.tensor.transpose(ps_tr[:, 0:GROUPS], hist[:, 0, :], ident[0:GROUPS, 0:GROUPS])
            nc.tensor.transpose(ps_tr[:, P:P + GROUPS], hist[:, 2, :], ident[0:GROUPS, 0:GROUPS]).then_inc(s_offT, 1)
            pe.wait_ge(s_bkt, 1)
            for g in range(GROUPS):
                last = mm(ps_sum[:, g:g + 1], bucket1h[:, g, :], ones_b[:, 0:1], start=True, stop=True)
            last.then_inc(s_bsum, 1)
            pe.wait_ge(s_bscan, 1)
            mm(ps_sum[:, 128:129], tri[:], bkt_sum[:, GROUPS - 1:GROUPS], start=True, stop=True).then_inc(s_below, 1)
            pe.wait_ge(s_base, 1)
            for g in range(GROUPS):
                own = (ps_gate, ps_moe)[g % 2][:, 0:P]
                w(pe, s_rank, g - 1)
                mm(own, bkt_base[:, g:g + 1].to_broadcast([P, P]), ident[:], start=True, stop=False)
                mm(own, tri_b[:], bucket1h[:, g, :], start=False, stop=True).then_inc(s_own, 1)

            with pe.Fori(0, GROUPS) as g:
                pe.wait_ge(s_xc, g + 1)
                nc.tensor.transpose(ps_w1[0][:, 0:P], x1[:], ident[:]).then_inc(s_xT, 1)
                pe.wait_ge(s_xTs, g + 1)
                mm(ps_w1[1][:, 0:H], ones_row[:], b_in_r[:], start=True, stop=False)
                mm(ps_w1[1][:, 0:H], h_t[:, 0:P], w_in[:], start=False, stop=True).then_inc(s_h0, 1)
                pe.wait_ge(s_h0s, g + 1)
            nc.tensor.transpose(ps_weak[0][:, 0:LAYERS * NS * 4], b1_rows[:], ident[0:LAYERS * NS * 4, 0:LAYERS * NS * 4]).then_inc(s_prepP, 1)
            for k in range(2):
                pe.wait_ge(s_prepP, 2 + 4 * k)
                nc.tensor.transpose(ps_weak[0][:, 128:256], gat_w[k][:, 0:P], ident[:]).then_inc(s_prepP, 1)
                pe.wait_ge(s_prepP, 4 + 4 * k)
                mm(ps_weak[1][:, 0:2 * HEADS], gat_wt[:], gat_a[k][:], start=True, stop=True).then_inc(s_prepP, 1)
            pe.wait_ge(s_prepP, 10)
            pe.wait_ge(s_degp, 1)
            nc.tensor.transpose(ps_tr[0:GROUPS, 256:384], deg_p[:], ident[:]).then_inc(s_degT, 1)
            pe.wait_ge(s_kmax, 1)
            mm(ps_sum[0:1, 128:128 + GROUPS + 1], kmax[:], tri[0:GROUPS, 0:GROUPS + 1], start=True, stop=True)
            nc.tensor.transpose(ps_sum[0:1, 256:256 + GROUPS], kmax[:], ident[0:GROUPS, 0:GROUPS]).then_inc(s_cumP, 1)

            def second(r, g):
                n = g + r * GROUPS
                pe.wait_ge(gatesT_copied, n + 1)
                w(pe, h_done, n)
                mm(ps_moe[:, 0:H], gates_t[:], b2_w[:], start=True, stop=False)
                for s in range(NS):
                    pe.wait_ge(gated, n * NS + (s + 1))
                    for c in range(4):
                        last = mm(ps_moe[:, 0:H], strong[:, s, c, :], w2_w[:, c, s, :], start=False, stop=s == NS - 1 and c == 3)
                last.then_inc(w2_ready, 1)

            def first(r, g, lag):
                n = g + r * GROUPS
                pe.wait_ge(hcur_ready, n + 1)
                w(pe, gatesT_copied, n)
                nc.tensor.transpose(ps_tr[:, 0:P], h_cur[:, 0:P], ident[:])
                nc.tensor.transpose(ps_tr[:, P:H], h_cur[:, P:H], ident[:]).then_inc(hT_ready, 1)
                pe.wait_ge(hT_copied, n + 1)
                pe.wait_ge(agg_ready, n + 1)
                nc.tensor.transpose(ps_tr[:, 0:P], agg[:, 0:P], ident[:])
                nc.tensor.transpose(ps_tr[:, P:H], agg[:, P:H], ident[:]).then_inc(aggT_ready, 1)
                pe.wait_ge(aggT_copied, n + 1)
                lg = ps_tr[:, H:H + NE + 1]
                mm(lg, ones_row[:], rt_b[:, r, :], start=True, stop=False)
                for k in range(2):
                    mm(lg, h_t[:, k * P:(k + 1) * P], rt_w[:, r, k, :], start=False, stop=False)
                for k in range(2):
                    last = mm(lg, agg_t[:, k * P:(k + 1) * P], rt_w[:, r, 2 + k, :], start=False, stop=k == 1)
                last.then_inc(logits_ready, 1)
                if lag:
                    second(r, g - 1)
                for s in range(NS):
                    w(pe, relu_ready, n * NS + (s - 1))
                    for c in range(4):
                        for k in range(2):
                            last = mm(ps_w1[s % 2][:, c * P:(c + 1) * P], w1_w[:, k, s, c * P:(c + 1) * P],
                                      agg_t[:, k * P:(k + 1) * P], start=k == 0, stop=k == 1)
                    last.then_inc(w1_ready, 1)
                w(pe, weak_copied, n)
                for j in range(2):
                    mm(ps_weak[j][:], ones_row[:], wk_b[:, j * 512:(j + 1) * 512], start=True, stop=False)
                    for k in range(2):
                        last = mm(ps_weak[j][:], agg_t[:, k * P:(k + 1) * P], wk_w[:, k, j * 512:(j + 1) * 512], start=False, stop=k == 1)
                last.then_inc(weak_ready, 1)
                pe.wait_ge(gates_ready, n + 1)
                w(pe, gated, n * NS)
                for s in range(NS):
                    mm(ps_gate[:, s * P:(s + 1) * P], gates[:, NW + s:NW + s + 1].to_broadcast([P, P]), ident[:], start=True, stop=True)
                nc.tensor.transpose(ps_tr[0:NE, 384:512], gates[:], ident[:]).then_inc(bcast_ready, 1)

            for r in range(LAYERS):
                pe.wait_ge(s_wts, 160 * (r + 1))
                first(r, 0, False)
                with pe.Fori(1, GROUPS) as g:
                    first(r, g, True)
                second(r, GROUPS - 1)

            def table_row(k, g):
                n = g + k * GROUPS
                pe.wait_ge(x1_ready, n + 1)
                nc.tensor.transpose(ps_tr[:, H:H + P], x1[:], ident[:]).then_inc(x1T_ready, 1)
                pe.wait_ge(x1T_copied, n + 1)
                w(pe, row_done, n)
                mm(ps_sum[:, 0:P + 2 * HEADS], x1_t[:], gat_w[k][:], start=True, stop=True).then_inc(row_ready, 1)

            with pe.Fori(0, GROUPS) as g:
                n = g + LAYERS * GROUPS
                pe.wait_ge(hcur_ready, n + 1)
                nc.tensor.transpose(ps_tr[:, 0:P], h_cur[:, 0:P], ident[:])
                nc.tensor.transpose(ps_tr[:, P:H], h_cur[:, P:H], ident[:]).then_inc(hT_ready, 1)
                pe.wait_ge(h_done, LAYERS * GROUPS)
                mm(ps_moe[:, 0:IN], ones_row[:], b_out_r[:], start=True, stop=False)
                pe.wait_ge(hT_copied, n + 1)
                for k in range(2):
                    last = mm(ps_moe[:, 0:IN], h_t[:, k * P:(k + 1) * P], w_out[:, k, :], start=False, stop=k == 1)
                last.then_inc(b_out_ready, 1)
                table_row(0, g)
            with pe.Fori(0, GROUPS) as g:
                table_row(1, g)


_INS = ['x', 'src', 'dst', 'L0_gnn_W_in', 'L0_gnn_b_in', 'L0_gnn_router_W', 'L0_gnn_router_b', 'L0_gnn_weak_W', 'L0_gnn_weak_b',
        'L0_gnn_strong_W1', 'L0_gnn_strong_b1', 'L0_gnn_strong_W2', 'L0_gnn_strong_b2', 'L0_gnn_conf_W', 'L0_gnn_conf_b',
        'L0_gnn_W_out', 'L0_gnn_b_out', 'L1_gnn_W1', 'L1_gnn_a_src1', 'L1_gnn_a_dst1', 'L1_gnn_b1', 'L1_gnn_W2',
        'L1_gnn_a_src2', 'L1_gnn_a_dst2', 'L1_gnn_b2']


def kernel(**inputs):
    import numpy as np
    import concourse.bacc as bacc
    from concourse.bass_utils import run_bass_kernel_spmd

    nc = bacc.Bacc("TRN2", target_bir_lowering=False, num_devices=1)
    arrays, args = {}, []
    for name in _INS:
        a = np.ascontiguousarray(inputs[name])
        if name == "x":
            a = np.concatenate([a, np.zeros((NP - N, IN), a.dtype)])
        elif name == "src":
            a = np.concatenate([a, np.zeros(EP - E, a.dtype)])
        elif name == "dst":
            a = np.concatenate([a, np.full(EP - E, NP, a.dtype)])
        arrays[f"in_{name}"] = a
        args.append(nc.dram_tensor(f"in_{name}", a.shape, mybir.dt.from_np(a.dtype), kind="ExternalInput").ap())
    args.append(nc.dram_tensor("out", (NP, IN), F32, kind="ExternalOutput").ap())
    gnn_kernel(nc, *args)
    r = run_bass_kernel_spmd(nc, [arrays], core_ids=[0])
    return r.results[0]["out"][:N]
```

```python
import concourse.bass as bass
from concourse import mybir
from contextlib import ExitStack

F32 = mybir.dt.float32
BF16 = mybir.dt.bfloat16
I32 = mybir.dt.int32
U32 = mybir.dt.uint32
ALU = mybir.AluOpType
ACT = mybir.ActivationFunctionType
AX = mybir.AxisListType

P = 128
N = 6250
E = 106250
GROUPS = -(-N // P)
NP = GROUPS * P
ET = 832
EP = ET * P
DUMMY = NP
IN, H, LAYERS = 128, 256, 3
LOOPS = 3750
NW, NS = 4, 4
NE = NW + NS
HEADS, HID = 4, 32
HC = HID + 1
GW = HEADS * HC + HEADS
SLOTS = 4
RING = 16
UNITS = RING // SLOTS
RUN = 64
COLS = GROUPS * RUN + RUN
UMAX = (E + GROUPS * SLOTS + RING) // SLOTS
CAP = UMAX * SLOTS + RUN
HIST = 8
LOWEST = -1.5e38
DUMMY_SCORE = -1.0e38
EPS_LN = 1e-5
EPS_GAT = 1e-16


def w(eng, sem, value):
    if not (isinstance(value, int) and value <= 0):
        eng.wait_ge(sem, value)


def gnn_kernel(nc, x, src, dst, W_in, b_in, router_W, router_b, weak_W, weak_b, strong_W1, strong_b1,
               strong_W2, strong_b2, conf_W, conf_b, W_out, b_out, W1, a_src1, a_dst1, b1, W2, a_src2,
               a_dst2, b2, out):
    ctx = ExitStack()
    with ctx:
        def sb(name, shape, dt=F32):
            return ctx.enter_context(nc.sbuf_tensor(name, shape, dt))

        def sem(name):
            return ctx.enter_context(nc.semaphore(name))

        def dram(name, shape, dt=F32):
            return nc.dram_tensor(name, shape, dt, kind="Internal").ap()

        hidden_tab = [dram(f"hidden_tab{i}", [NP + 1, H]) for i in range(LAYERS)]
        gat_tab = [dram(f"gat_tab{i}", [NP + 1, GW]) for i in range(2)]
        meta_tab = dram("meta_tab", [NP, 4], I32)
        slot_tab = dram("slot_tab", [P, CAP], I32)

        h_res = sb("h_res", [P, GROUPS, H])
        x_res = sb("x_res", [P, GROUPS, IN])
        perm = sb("perm", [P, GROUPS, 4], I32)
        rdeg = sb("rdeg", [P, GROUPS])
        loop_on = sb("loop_on", [P, GROUPS])
        loop_cap = sb("loop_cap", [P, GROUPS])
        ring = sb("ring", [P, RING, H])
        stage = sb("stage", [P, 2, RING // 2], I32)
        cum = sb("cum", [1, GROUPS + 2], I32)
        ad = [sb(f"ad{i}", [P, GROUPS, HEADS]) for i in range(2)]

        wbuf = sb("wbuf", [P, 10240])
        run_raw = wbuf[:, 0:GROUPS * RUN].bitcast(I32).rearrange("p (g k) -> p g k", k=RUN)
        slots_sb = wbuf[:, GROUPS * RUN:GROUPS * RUN + COLS].bitcast(I32)
        d_at = GROUPS * RUN + COLS
        bucket1h = wbuf[:, d_at:d_at + GROUPS * P // 2].bitcast(BF16).rearrange("p (g b) -> p g b", b=P)
        wk_w = wbuf[:, 0:2048].rearrange("p (k n) -> p k n", k=2)
        w1_w = wbuf[:, 2048:6144].rearrange("p (k s n) -> p k s n", k=2, s=NS)
        w2_w = wbuf[:, 6144:10240].rearrange("p (c s n) -> p c s n", c=4, s=NS)
        gat_rows = wbuf[:, 0:GROUPS * GW].rearrange("p (g n) -> p g n", n=GW)

        iota_i = sb("iota_i", [P, P], I32)
        iota = sb("iota", [P, P])
        iota_b = sb("iota_b", [P, P], BF16)
        ident = sb("ident", [P, P])
        tri = sb("tri", [P, P])
        tri_b = sb("tri_b", [P, P], BF16)
        ones_b = sb("ones_b", [P, P], BF16)
        zero_b = sb("zero_b", [P, P], BF16)
        ones_row = sb("ones_row", [1, P])
        dummy_row = sb("dummy_row", [1, H])
        dummy_score = sb("dummy_score", [1, HEADS])

        dst_i = sb("dst_i", [P, ET], I32)
        lo_i = ring[:, 0:4, :].rearrange("p a b -> p (a b)")[:, 0:ET].bitcast(I32)
        lo_f = ring[:, 4:8, :].rearrange("p a b -> p (a b)")[:, 0:ET]
        hi_f = ring[:, 8:12, :].rearrange("p a b -> p (a b)")[:, 0:ET]
        lo1h = sb("lo1h", [P, 2, HIST, P], BF16)
        hi1h = sb("hi1h", [P, 2, HIST, GROUPS], BF16)
        hist = sb("hist", [GROUPS, 3, P])
        row_pre = sb("row_pre", [GROUPS, 1])
        deg_n = sb("deg_n", [P, GROUPS])
        off_n = sb("off_n", [P, GROUPS])
        bucket = sb("bucket", [P, GROUPS])
        bkt_count = sb("bkt_count", [P, GROUPS])
        bkt_sum = sb("bkt_sum", [P, GROUPS])
        bkt_first = sb("bkt_first", [P, 1])
        bkt_base = sb("bkt_base", [P, GROUPS])
        zeros = sb("zeros", [P, P])
        rank = sb("rank", [P, GROUPS])
        sort_tmp = sb("sort_tmp", [P, 4, P])
        rank_i = sb("rank_i", [P, 3, GROUPS], I32)
        meta = sb("meta", [P, GROUPS, 4], I32)
        deg_p = sb("deg_p", [P, GROUPS])
        deg_t = sb("deg_t", [GROUPS, P])
        kmax = sb("kmax", [GROUPS, 1])
        kmax_i = sb("kmax_i", [GROUPS, 1], I32)
        cum_f = sb("cum_f", [1, GROUPS + 2])
        cum_at = sb("cum_at", [1, GROUPS + 2], I32)
        run_f = x_res[:].rearrange("p g n -> p (g n)")[:, 0:GROUPS * RUN]
        run_m = x_res[:].rearrange("p g n -> p (g n)")[:, GROUPS * RUN:2 * GROUPS * RUN]
        long_off = sb("long_off", [P, 2])
        long_idx = sb("long_idx", [P, 1], I32)
        long_raw = sb("long_raw", [P, SLOTS], I32)
        long_dummy = sb("long_dummy", [P, SLOTS], I32)
        long_meta = sb("long_meta", [P, 2], I32)

        w_in = sb("w_in", [P, H])
        b_in_r = sb("b_in_r", [1, H])
        rt_w = sb("rt_w", [P, LAYERS, 4, NE + 1])
        rt_b = sb("rt_b", [1, LAYERS, NE + 1])
        b1_rows = sb("b1_rows", [LAYERS * NS * 4, P])
        b1_t = sb("b1_t", [P, LAYERS * NS * 4])
        wk_b = sb("wk_b", [1, NW * H])
        b2_w = sb("b2_w", [NE, H])
        w_out = sb("w_out", [P, 2, IN])
        b_out_r = sb("b_out_r", [1, IN])
        gat_w = [sb(f"gat_w{i}", [P, P + 2 * HEADS]) for i in range(2)]
        gat_a = [sb(f"gat_a{i}", [P, 2 * HEADS]) for i in range(2)]
        gat_b = [sb(f"gat_b{i}", [P, P]) for i in range(2)]
        gat_wt = sb("gat_wt", [P, P])

        h_cur = [sb(f"h_cur{i}", [P, H]) for i in range(2)]
        h_t = [sb(f"h_t{i}", [P, H]) for i in range(2)]
        agg = sb("agg", [P, H])
        agg_t = [sb(f"agg_t{i}", [P, H]) for i in range(2)]
        part = sb("part", [P, H])
        strong = [sb(f"strong{i}", [P, NS, 4, P]) for i in range(2)]
        weak = sb("weak", [P, NW, H])
        logit = sb("logit", [P, NE + 1])
        top = sb("top", [P, 8])
        top_at = sb("top_at", [P, 8], U32)
        top_f = sb("top_f", [P, 2])
        ex_in = sb("ex_in", [P, 2])
        ex = sb("ex", [P, 2])
        gate_n = sb("gate_n", [P, 4])
        gate_ab = sb("gate_ab", [P, 2, NE])
        gates = sb("gates", [P, NE])
        gates_t = [sb(f"gates_t{i}", [NE, P]) for i in range(2)]
        x1 = [sb(f"x1_{i}", [P, IN]) for i in range(2)]
        x1_t = [sb(f"x1_t{i}", [P, IN]) for i in range(2)]
        ln_st = sb("ln_st", [P, 6])
        ln_of = sb("ln_of", [P, 2])
        ln_mv = sb("ln_mv", [P, GROUPS, 2])
        ln_r = sb("ln_r", [P, 3, GROUPS])
        ad_cur = sb("ad_cur", [P, HEADS])
        score = sb("score", [P, SLOTS + 1, HEADS])
        m_new = sb("m_new", [P, HEADS])
        shifted = sb("shifted", [P, SLOTS + 1, HEADS])
        terms = sb("terms", [P, SLOTS + 1, HEADS, HC])
        gacc = sb("gacc", [P, HEADS, HC])
        rden = sb("rden", [P, HEADS])
        y = sb("y", [P, P])
        y_neg = sb("y_neg", [P, P])
        y_exp = sb("y_exp", [P, P])

        def bank(name):
            return ctx.enter_context(nc.psum_tensor(name, [P, 512], F32))

        ps_w1 = [bank("ps_w1a"), bank("ps_w1b")]
        ps_weak = [bank("ps_weak_a"), bank("ps_weak_b")]
        ps_gate = bank("ps_gate")
        ps_moe = bank("ps_moe")
        ps_tr = bank("ps_tr")
        ps_sum = bank("ps_sum")
        acc = ps_sum[:, 0:H]

        s_const, s_ints, s_par, s_xin, s_dummy, s_wts = (sem(n) for n in (
            "s_const", "s_ints", "s_par", "s_xin", "s_dummy", "s_wts"))
        s_keys, s_1h, s_1h_used, s_hist, s_tot, s_pre, s_off, s_offT = (sem(n) for n in (
            "s_keys", "s_1h", "s_1h_used", "s_hist", "s_tot", "s_pre", "s_off", "s_offT"))
        s_bkt, s_bsum, s_bscan, s_below, s_base, s_own, s_rank, s_meta, s_scat, s_perm = (sem(n) for n in (
            "s_bkt", "s_bsum", "s_bscan", "s_below", "s_base", "s_own", "s_rank", "s_meta", "s_scat", "s_perm"))
        s_runs, s_hperm, s_xperm, s_degp, s_degT, s_kmax, s_cumP, s_cum, s_slots, s_slotst, s_long, s_longrun, s_longst = (sem(n) for n in (
            "s_runs", "s_hperm", "s_xperm", "s_degp", "s_degT", "s_kmax", "s_cumP", "s_cum", "s_slots",
            "s_slotst", "s_long", "s_longrun", "s_longst"))
        s_xc, s_xT, s_xTs, s_h0, s_h0s, s_h0st, s_prep, s_prepP = (sem(n) for n in (
            "s_xc", "s_xT", "s_xTs", "s_h0", "s_h0s", "s_h0st", "s_prep", "s_prepP"))
        gathered = [sem(f"gathered{u}") for u in range(UNITS)]
        staged = [sem(f"staged{h}") for h in range(2)]
        half_begun, arrived, round_gathered, ring_free, table_done = (sem(n) for n in (
            "half_begun", "arrived", "round_gathered", "ring_free", "table_done"))
        hcur_ready, hT_ready, hT_copied = sem("hcur_ready"), sem("hT_ready"), sem("hT_copied")
        agg_ready, aggT_ready, aggT_copied = sem("agg_ready"), sem("aggT_ready"), sem("aggT_copied")
        logits_ready, logits_copied, top_ready, exp_ready, gates_ready = (sem(n) for n in (
            "logits_ready", "logits_copied", "top_ready", "exp_ready", "gates_ready"))
        w1_ready, relu_ready, gated, w2_ready = sem("w1_ready"), sem("relu_ready"), sem("gated"), sem("w2_ready")
        weak_ready, weak_copied, weak_added = sem("weak_ready"), sem("weak_copied"), sem("weak_added")
        bcast_ready, gatesT_ready, gatesT_copied, h_done = sem("bcast_ready"), sem("gatesT_ready"), sem("gatesT_copied"), sem("h_done")
        hout_ready, houtT_ready, houtT_copied, b_out_ready, z_ready, var_ready, rstd_ready = (sem(n) for n in (
            "hout_ready", "houtT_ready", "houtT_copied", "b_out_ready", "z_ready", "var_ready", "rstd_ready"))
        x1_ready, x1T_ready, x1T_copied, ones_set, row_ready, row_done = (sem(n) for n in (
            "x1_ready", "x1T_ready", "x1T_copied", "ones_set", "row_ready", "row_done"))
        shift_ready, p_ready, neg_ready, nexp_ready, z_done = (sem(n) for n in (
            "shift_ready", "p_ready", "neg_ready", "nexp_ready", "z_done"))
        s_out = sem("s_out")

        block = ctx.enter_context(nc.Block())
        n_par = [0]

        def units_of(eng, g):
            return (eng.value_load(cum[0:1, bass.ds(g, 1)], min_val=0, max_val=UMAX),
                    eng.value_load(cum[0:1, bass.ds(g + 1, 1)], min_val=1, max_val=UMAX))

        def all_units(eng):
            return eng.value_load(cum[0:1, GROUPS:GROUPS + 1], min_val=UNITS, max_val=UMAX)

        PAR_DMAS = 5 + 4 * LAYERS + 2 * (2 + 2 * HEADS)

        @block.sync
        def _(sp):
            sp.dma_start(dst_i[:], dst.rearrange("(p t) -> p t", p=P)).then_inc(s_ints, 16)
            sp.dma_start(x_res[:], x.rearrange("(g p) n -> p g n", p=P)).then_inc(s_xin, 16)
            sp.wait_ge(s_prep, 1)

            def par(o, i):
                sp.dma_start(o, i).then_inc(s_par, 16)
                n_par[0] += 1

            par(w_in[:], W_in)
            par(b_in_r[:], b_in.rearrange("(a n) -> a n", a=1))
            par(w_out[:], W_out.rearrange("(k p) n -> p k n", p=P))
            par(b_out_r[:], b_out.rearrange("(a n) -> a n", a=1))
            par(b1_rows[:], strong_b1.rearrange("l s (c p) -> (l s c) p", p=P))
            with nc.allow_non_contiguous_dma(reason="a few columns of weights"):
                for l in range(LAYERS):
                    par(rt_w[:, l, :, 0:NE], router_W[l].rearrange("(k p) e -> p k e", p=P))
                    par(rt_w[:, l, 0:2, NE], conf_W[l].rearrange("(k p) o -> p (k o)", p=P))
                    par(rt_b[:, l, 0:NE], router_b[l:l + 1, :])
                    par(rt_b[:, l, NE:NE + 1], conf_b[l:l + 1, :])
                par(gat_w[0][:, 0:P], W1)
                par(gat_w[1][:, 0:P], W2)
                par(gat_b[0][:], b1.rearrange("(a n) -> a n", a=1).to_broadcast([P, P]))
                par(gat_b[1][:], b2.rearrange("(a n) -> a n", a=1).to_broadcast([P, P]))
                for k, (a_s, a_d) in enumerate(((a_src1, a_dst1), (a_src2, a_dst2))):
                    for h in range(HEADS):
                        rows = slice(HID * h, HID * h + HID) if k == 0 else slice(0, P)
                        vec = slice(h, h + 1) if k == 0 else slice(0, 1)
                        par(gat_a[k][rows, h:h + 1], a_s[vec, :].rearrange("a c -> c a"))
                        par(gat_a[k][rows, HEADS + h:HEADS + h + 1], a_d[vec, :].rearrange("a c -> c a"))

            sp.wait_ge(s_const, 1)
            for t in hidden_tab:
                sp.dma_start(t[DUMMY:DUMMY + 1, :], dummy_row[:, :]).then_inc(s_dummy, 16)
            for t in gat_tab:
                sp.dma_start(t[DUMMY:DUMMY + 1, 0:GW - HEADS], dummy_row[:, 0:GW - HEADS]).then_inc(s_dummy, 16)
                sp.dma_start(t[DUMMY:DUMMY + 1, GW - HEADS:GW], dummy_score[:, :]).then_inc(s_dummy, 16)

            with sp.Fori(0, GROUPS) as g:
                sp.wait_ge(s_h0s, g + 1)
                sp.dma_start(hidden_tab[0][bass.ds(g * P, P), :], h_res[:, bass.ds(g, 1), :].rearrange("p a n -> p (a n)"))\
                    .then_inc(s_h0st, 16)

            sp.wait_ge(s_scat, 16 * GROUPS)
            sp.dma_start(perm[:], meta_tab.rearrange("(p g) c -> p g c", p=P)).then_inc(s_perm, 16)
            sp.wait_ge(s_slots, 1)
            sp.dma_start(slot_tab[:, 0:COLS], slots_sb).then_inc(s_slotst, 16)
            sp.wait_ge(s_long, 1)

            total = all_units(sp)
            bodies = total // UNITS
            for r in range(LAYERS + 2):
                if r < LAYERS:
                    if r:
                        sp.wait_ge(w2_ready, r * GROUPS)
                    for k in range(2):
                        sp.dma_start(wk_w[:, k, :].rearrange("p (e n) -> p e n", e=NW),
                                     weak_W[r, :, k * P:(k + 1) * P, :].rearrange("e p n -> p e n")).then_inc(s_wts, 16)
                        sp.dma_start(w1_w[:, k, :, :],
                                     strong_W1[r, :, k * P:(k + 1) * P, :].rearrange("s p n -> p s n")).then_inc(s_wts, 16)
                    for c in range(4):
                        sp.dma_start(w2_w[:, c, :, :],
                                     strong_W2[r, :, c * P:(c + 1) * P, :].rearrange("s p n -> p s n")).then_inc(s_wts, 16)
                    sp.dma_start(wk_b[:, :], weak_b[r:r + 1].rearrange("a e n -> a (e n)")).then_inc(s_wts, 16)
                    sp.dma_start(b2_w[NW:NE, :], strong_b2[r]).then_inc(s_wts, 16)

                if r:
                    sp.wait_ge(round_gathered, r)
                for half in range(2):
                    sp.dma_start(stage[:, half, :], slot_tab[:, half * RING // 2:(half + 1) * RING // 2])\
                        .then_inc(staged[half], 16)
                with sp.Fori(1, bodies) as i:
                    for half in range(2):
                        sp.wait_ge(arrived, total * r + i * UNITS + (r + 1 - UNITS + (half + 1) * UNITS // 2))
                        sp.dma_start(stage[:, half, :], slot_tab[:, bass.ds(i * RING + half * RING // 2, RING // 2)])\
                            .then_inc(staged[half], 16)
            sp.wait_ge(s_out, 16 * GROUPS)

        @block.gpsimd
        def _(pool):
            nc.gpsimd.iota(iota_i[:], pattern=[[1, P]], base=0, channel_multiplier=0)
            nc.gpsimd.memset(dummy_row[:], 0.0)
            nc.gpsimd.memset(dummy_score[:], DUMMY_SCORE)
            nc.gpsimd.memset(rt_w[:], 0.0)
            nc.gpsimd.memset(b2_w[:], 0.0)
            nc.gpsimd.memset(gat_a[0][:], 0.0)
            nc.gpsimd.memset(gat_a[1][:], 0.0)
            nc.gpsimd.memset(ident[:], 0.0)
            nc.gpsimd.memset(tri[:], 1.0)
            nc.gpsimd.memset(ones_b[:], 1.0)
            nc.gpsimd.memset(zero_b[:], 0.0)
            nc.gpsimd.memset(ones_row[:], 1.0)
            pool.drain().then_inc(s_prep, 1)
            nc.gpsimd.tensor_copy(iota[:], iota_i[:])
            nc.gpsimd.affine_select(out=ident[:], in_=ident[:], compare_op=ALU.not_equal, fill=1.0,
                                    base=0, pattern=[[-1, P]], channel_multiplier=1)
            nc.gpsimd.affine_select(out=tri[:], in_=tri[:], compare_op=ALU.is_gt, fill=0.0,
                                    base=0, pattern=[[1, P]], channel_multiplier=-1)
            pool.drain()
            nc.gpsimd.tensor_copy(iota_b[:], iota[:])
            nc.gpsimd.tensor_copy(tri_b[:], tri[:])
            nc.gpsimd.iota(meta[:, :, 0], pattern=[[P, GROUPS]], base=0, channel_multiplier=1)
            nc.gpsimd.memset(meta[:, :, 3], 0)
            nc.gpsimd.memset(long_dummy[:], DUMMY)
            pool.drain().then_inc(s_const, 1)

            pool.wait_ge(s_meta, 1)
            for g in range(GROUPS):
                pool.indirect_dma_start(out=meta_tab, out_offset=bass.IndirectOffsetOnAxis(ap=rank_i[:, 2, g:g + 1], axis=0),
                                        in_=meta[:, g, :], in_offset=None).then_inc(s_scat, 16)
            pool.wait_ge(s_perm, 16)
            for g in range(GROUPS):
                pool.indirect_dma_start(out=run_raw[:, g, :], out_offset=None, in_=src.rearrange("(a e) -> a e", a=1),
                                        in_offset=bass.IndirectOffsetOnAxis(ap=perm[:, g, 1:2], axis=1))\
                    .then_inc(gathered[UNITS - 1] if g < SLOTS else s_runs, 16)
            pool.wait_ge(s_h0st, 16 * GROUPS)
            for g in range(GROUPS):
                pool.indirect_dma_start(out=h_res[:, g, :], out_offset=None, in_=hidden_tab[0],
                                        in_offset=bass.IndirectOffsetOnAxis(ap=perm[:, g, 0:1], axis=0)).then_inc(s_hperm, 16)

            pool.wait_ge(s_slotst, 16)
            pool.wait_ge(s_cum, 1)
            most = pool.value_load(cum[0:1, GROUPS + 1:GROUPS + 2], min_val=1, max_val=E)
            with pool.If(most > RUN // SLOTS):
                with pool.Fori(0, GROUPS) as g:
                    c0, c1 = units_of(pool, g)
                    nc.gpsimd.tensor_copy(long_meta[:], perm[:, bass.ds(g, 1), 1:3].rearrange("p a n -> p (a n)"))
                    pool.drain()
                    nc.gpsimd.tensor_copy(long_off[:], long_meta[:])
                    with pool.Fori(c0, c1) as c:
                        pool.drain()
                        nc.gpsimd.tensor_scalar(long_off[:, 0:1], long_off[:, 0:1], float(E), None, ALU.min)
                        pool.drain()
                        nc.gpsimd.tensor_copy(long_idx[:], long_off[:, 0:1])
                        pool.drain()
                        pool.indirect_dma_start(out=long_raw[:], out_offset=None, in_=src.rearrange("(a e) -> a e", a=1),
                                                in_offset=bass.IndirectOffsetOnAxis(ap=long_idx[:, 0:1], axis=1)).then_inc(s_longrun, 16)
                        pool.wait_ge(s_longrun, c * 16 + 16)
                        nc.gpsimd.tensor_tensor(long_raw[:], long_raw[:], long_dummy[:], ALU.subtract)
                        pool.drain()
                        nc.gpsimd.tensor_copy(run_f[:, 0:SLOTS], long_raw[:])
                        nc.gpsimd.tensor_scalar(run_m[:, 0:SLOTS], iota[:, 0:SLOTS], long_off[:, 1:2], None, ALU.is_lt)
                        pool.drain()
                        nc.gpsimd.tensor_tensor(run_f[:, 0:SLOTS], run_f[:, 0:SLOTS], run_m[:, 0:SLOTS], ALU.mult)
                        pool.drain()
                        nc.gpsimd.tensor_scalar(long_raw[:], run_f[:, 0:SLOTS], float(DUMMY), None, ALU.add)
                        pool.drain()
                        pool.dma_start(slot_tab[:, bass.ds(c * SLOTS, SLOTS)], long_raw[:]).then_inc(s_longst, 16)
                        nc.gpsimd.tensor_scalar(long_off[:, 0:1], long_off[:, 0:1], float(SLOTS), None, ALU.add)
                        nc.gpsimd.tensor_scalar(long_off[:, 1:2], long_off[:, 1:2], float(-SLOTS), None, ALU.add)
                        pool.wait_ge(s_longst, c * 16 + 16)
            pool.drain().then_inc(s_long, 1)

            pool.wait_ge(s_dummy, 16 * (LAYERS + 4))
            total = all_units(pool)
            bodies = total // UNITS
            for r in range(LAYERS + 2):
                table = hidden_tab[r] if r < LAYERS else gat_tab[r - LAYERS]
                width = H if r < LAYERS else GW
                with pool.Fori(bodies * r, bodies * (r + 1)) as i:
                    for b in range(RING):
                        if b % (RING // 2) == 0:
                            pool.wait_ge(staged[b * 2 // RING], i * 16 + 16)
                            pool.sem_inc(half_begun, 1)
                        if b % SLOTS == SLOTS // 2:
                            pool.wait_ge(ring_free, i * UNITS + (b // SLOTS + 2))
                            pool.wait_ge(gathered[(b // SLOTS - 1) % UNITS], i * (16 * SLOTS) + 16 * SLOTS)
                            pool.sem_inc(arrived, 1)
                        pool.indirect_dma_start(out=ring[:, b, 0:width], out_offset=None, in_=table,
                                                in_offset=bass.IndirectOffsetOnAxis(ap=stage[:, b * 2 // RING, b % (RING // 2):b % (RING // 2) + 1], axis=0))\
                            .then_inc(gathered[b // SLOTS], 16)
                pool.wait_ge(gathered[UNITS - 1], bodies * (16 * SLOTS * (r + 1)) + 16 * SLOTS)
                pool.sem_inc(arrived, 1)
                pool.sem_inc(round_gathered, 1)
                if r == LAYERS - 1:
                    for g in range(GROUPS):
                        pool.indirect_dma_start(out=x_res[:, g, :], out_offset=None, in_=x,
                                                in_offset=bass.IndirectOffsetOnAxis(ap=perm[:, g, 0:1], axis=0)).then_inc(s_xperm, 16)
                for g in range(GROUPS):
                    ids = bass.IndirectOffsetOnAxis(ap=perm[:, g, 0:1], axis=0)
                    if r < LAYERS - 1:
                        pool.wait_ge(h_done, r * GROUPS + g + 1)
                        pool.indirect_dma_start(out=hidden_tab[r + 1], out_offset=ids, in_=h_res[:, g, :], in_offset=None)\
                            .then_inc(table_done, 16)
                    elif r < LAYERS + 1:
                        pool.wait_ge(row_done, (r - LAYERS + 1) * GROUPS + g + 1)
                        pool.indirect_dma_start(out=gat_tab[r - LAYERS + 1], out_offset=ids, in_=gat_rows[:, g, :], in_offset=None)\
                            .then_inc(table_done, 16)
                    else:
                        pool.wait_ge(z_done, g + 1)
                        pool.indirect_dma_start(out=out, out_offset=ids, in_=x_res[:, g, :], in_offset=None)\
                            .then_inc(s_out, 16)
                if r < LAYERS + 1:
                    pool.wait_ge(table_done, 16 * GROUPS * (r + 1))

        @block.vector
        def _(dve):
            dve.sem_inc(ring_free, UNITS)
            nc.vector.memset(zeros[:], 0.0)
            nc.vector.memset(slots_sb, DUMMY)
            dve.wait_ge(s_ints, 16)
            dve.wait_ge(s_const, 1)
            nc.vector.tensor_scalar(lo_i, dst_i[:], 127, None, ALU.bitwise_and)
            nc.vector.tensor_scalar(dst_i[:], dst_i[:], 7, None, ALU.logical_shift_right)
            dve.drain()
            nc.vector.tensor_copy(lo_f, lo_i)
            nc.vector.tensor_copy(hi_f, dst_i[:])
            dve.drain()
            dve.sem_inc(s_1h_used, 2)
            with dve.Fori(0, ET // (2 * HIST)) as i:
                for half in range(2):
                    dve.wait_ge(s_1h_used, i * 2 + (half + 1))
                    for t in range(HIST):
                        at = bass.ds(i * 2 * HIST + (half * HIST + t), 1)
                        nc.vector.tensor_scalar(lo1h[:, half, t, :], iota_b[:], lo_f[:, at], None, ALU.is_equal)
                        last = nc.vector.tensor_scalar(hi1h[:, half, t, :], iota_b[:, 0:GROUPS], hi_f[:, at], None, ALU.is_equal)
                    last.then_inc(s_1h, 1)
            dve.wait_ge(s_hist, 1)
            nc.vector.tensor_copy(hist[:, 0, :], ps_sum[0:GROUPS, 0:P])
            dve.drain()
            nc.vector.tensor_tensor_scan(hist[:, 1, :], hist[:, 0, :], zeros[0:GROUPS, :], 0.0, ALU.add, ALU.add)
            dve.drain().then_inc(s_tot, 1)
            dve.wait_ge(s_pre, 1)
            nc.vector.tensor_copy(row_pre[:], ps_sum[0:GROUPS, 256:257])
            dve.drain()
            nc.vector.scalar_tensor_tensor(hist[:, 2, :], hist[:, 1, :], row_pre[:], hist[:, 0, :], ALU.add, ALU.subtract)
            dve.drain().then_inc(s_off, 1)
            dve.wait_ge(s_offT, 1)
            nc.vector.tensor_copy(deg_n[:], ps_tr[:, 0:GROUPS])
            nc.vector.tensor_copy(off_n[:], ps_tr[:, P:P + GROUPS])
            dve.drain()
            nc.vector.tensor_scalar(bucket[:], deg_n[:], float(P - 1), None, ALU.min)
            dve.drain()
            for g in range(GROUPS):
                last = nc.vector.tensor_scalar(bucket1h[:, g, :], iota_b[:], bucket[:, g:g + 1], None, ALU.is_equal)
            last.then_inc(s_bkt, 1)
            dve.wait_ge(s_bsum, 1)
            nc.vector.tensor_copy(bkt_count[:], ps_sum[:, 0:GROUPS])
            dve.drain()
            nc.vector.tensor_tensor_scan(bkt_sum[:], bkt_count[:], zeros[:, 0:GROUPS], 0.0, ALU.add, ALU.add)
            dve.drain().then_inc(s_bscan, 1)
            dve.wait_ge(s_below, 1)
            nc.vector.tensor_tensor(bkt_first[:], ps_sum[:, 128:129], bkt_sum[:, GROUPS - 1:GROUPS], ALU.add)
            dve.drain()
            nc.vector.tensor_scalar(bkt_first[:], bkt_first[:], -1.0, float(NP), ALU.mult, ALU.add)
            dve.drain()
            nc.vector.scalar_tensor_tensor(bkt_base[:], bkt_sum[:], bkt_first[:], bkt_count[:], ALU.add, ALU.subtract)
            dve.drain().then_inc(s_base, 1)
            for g in range(GROUPS):
                dve.wait_ge(s_own, g + 1)
                nc.vector.tensor_tensor_reduce(out=sort_tmp[:, g % 4, :], in0=(ps_gate, ps_moe)[g % 2][:, 0:P], in1=bucket1h[:, g, :],
                                               scale=1.0, scalar=0.0, op0=ALU.mult, op1=ALU.add,
                                               accum_out=rank[:, g:g + 1]).then_inc(s_rank, 1)
                if g >= 3:
                    dve.wait_ge(s_rank, g - 2)
            dve.wait_ge(s_rank, GROUPS)
            nc.vector.tensor_copy(rank_i[:, 0, :], rank[:])
            dve.drain()
            nc.vector.tensor_scalar(rank_i[:, 1, :], rank_i[:, 0, :], P - 1, None, ALU.bitwise_and)
            nc.vector.tensor_scalar(rank_i[:, 0, :], rank_i[:, 0, :], 7, None, ALU.logical_shift_right)
            dve.drain()
            nc.vector.scalar_tensor_tensor(rank_i[:, 2, :], rank_i[:, 1, :], float(GROUPS), rank_i[:, 0, :], ALU.mult, ALU.add)
            nc.vector.tensor_copy(meta[:, :, 1], off_n[:])
            nc.vector.tensor_copy(meta[:, :, 2], deg_n[:])
            dve.drain().then_inc(s_meta, 1)
            dve.wait_ge(s_perm, 16)
            nc.vector.tensor_copy(deg_p[:], perm[:, :, 2])
            dve.drain().then_inc(s_degp, 1)
            nc.vector.tensor_copy(loop_cap[:], perm[:, :, 0])
            dve.drain()
            nc.vector.tensor_scalar(loop_on[:], loop_cap[:], float(LOOPS), None, ALU.is_lt)
            dve.drain()
            nc.vector.tensor_scalar(loop_cap[:], loop_on[:], -0.5, -2.0 * LOWEST, ALU.add, ALU.mult)
            nc.vector.tensor_scalar(rdeg[:], deg_p[:], 1.0, None, ALU.max)
            dve.drain()
            nc.vector.reciprocal(rdeg[:], rdeg[:])
            dve.wait_ge(s_degT, 1)
            nc.vector.tensor_reduce(kmax[:], ps_tr[0:GROUPS, 256:384], AX.X, ALU.max)
            dve.drain()
            nc.vector.tensor_scalar(kmax_i[:], kmax[:], 1.0, float(SLOTS - 1), ALU.max, ALU.add)
            dve.drain()
            nc.vector.tensor_scalar(kmax_i[:], kmax_i[:], SLOTS.bit_length() - 1, None, ALU.logical_shift_right)
            dve.drain()
            nc.vector.tensor_copy(kmax[:], kmax_i[:])
            dve.drain().then_inc(s_kmax, 1)
            dve.wait_ge(s_cumP, 1)
            nc.vector.tensor_copy(cum_f[:, 0:GROUPS + 1], ps_sum[0:1, 128:128 + GROUPS + 1])
            nc.vector.tensor_reduce(cum_f[:, GROUPS + 1:GROUPS + 2], ps_sum[0:1, 256:256 + GROUPS], AX.X, ALU.max)
            dve.drain()
            nc.vector.tensor_copy(cum[:], cum_f[:])
            nc.vector.tensor_scalar(cum_at[:], cum_f[:], float(SLOTS), float(COLS - RUN), ALU.mult, ALU.min)
            dve.drain()
            nc.vector.tensor_scalar(cum[:, GROUPS:GROUPS + 1], cum_f[:, GROUPS:GROUPS + 1], float(UNITS - 1), None, ALU.add)
            dve.drain()
            nc.vector.tensor_scalar(cum[:, GROUPS:GROUPS + 1], cum[:, GROUPS:GROUPS + 1], UNITS.bit_length() - 1,
                                    UNITS.bit_length() - 1, ALU.logical_shift_right, ALU.logical_shift_left)
            dve.drain().then_inc(s_cum, 1)
            dve.wait_ge(s_h0s, GROUPS)
            nc.vector.tensor_tensor(run_m.rearrange("p (g k) -> p g k", k=RUN), iota[:, 0:RUN].unsqueeze(1).to_broadcast([P, GROUPS, RUN]),
                                    deg_p[:].unsqueeze(2).to_broadcast([P, GROUPS, RUN]), ALU.is_lt)
            dve.wait_ge(gathered[UNITS - 1], 16 * SLOTS)
            dve.wait_ge(s_runs, 16 * (GROUPS - SLOTS))
            nc.vector.tensor_scalar(run_f, run_raw.rearrange("p g k -> p (g k)"), float(-DUMMY), None, ALU.add)
            dve.drain()
            nc.vector.tensor_tensor(run_f, run_f, run_m, ALU.mult)
            dve.drain()
            nc.vector.tensor_scalar(run_raw.rearrange("p g k -> p (g k)"), run_f, float(DUMMY), None, ALU.add)
            with dve.Fori(0, GROUPS) as g:
                at = dve.value_load(cum_at[0:1, bass.ds(g, 1)], min_val=0, max_val=COLS - RUN)
                dve.drain()
                nc.vector.tensor_copy(slots_sb[:, bass.ds(at, RUN)], run_raw[:, bass.ds(g, 1), :].rearrange("p a k -> p (a k)"))
            dve.drain().then_inc(s_slots, 1)

            total = all_units(dve)

            def aggregate(r, g):
                n = g + r * GROUPS
                c0, c1 = units_of(dve, g)
                dve.drain()
                nc.vector.memset(acc, 0.0)
                with dve.Fori(total * r + c0, total * r + c1) as q:
                    dve.drain()
                    dve.wait_ge(arrived, q + (r + 2))
                    nc.vector.tensor_reduce(part[:], ring[:, bass.ds((q % UNITS) * SLOTS, SLOTS), :].rearrange("p s n -> p n s"),
                                            AX.X, ALU.add).then_inc(ring_free, 1)
                    dve.drain()
                    nc.vector.tensor_tensor(acc, acc, part[:], ALU.add)
                dve.drain()
                w(dve, aggT_ready, n)
                nc.vector.tensor_scalar(agg[:], acc, rdeg[:, bass.ds(g, 1)], None, ALU.mult).then_inc(agg_ready, 1)

            def gate_experts(r, g, odd):
                n = g + r * GROUPS
                dve.wait_ge(bcast_ready, n + 1)
                for s in range(NS):
                    dve.wait_ge(relu_ready, n * NS + (s + 1))
                    nc.vector.tensor_tensor(strong[odd][:, s, :, :], strong[odd][:, s, :, :],
                                            ps_gate[:, s * P:(s + 1) * P].unsqueeze(1).to_broadcast([P, 4, P]), ALU.mult).then_inc(gated, 1)
                dve.wait_ge(weak_copied, n + 1)
                nc.vector.tensor_reduce(part[:], weak[:].rearrange("p e n -> p n e"), AX.X, ALU.add).then_inc(weak_added, 1)
                dve.drain()
                hg = h_res[:, bass.ds(g, 1), :].rearrange("p a n -> p (a n)")
                nc.vector.tensor_tensor(hg, hg, part[:], ALU.add)

            def add_strong(r, g):
                dve.drain()
                dve.wait_ge(w2_ready, g + (r * GROUPS + 1))
                hg = h_res[:, bass.ds(g, 1), :].rearrange("p a n -> p (a n)")
                nc.vector.tensor_tensor(hg, hg, ps_moe[:, 0:H], ALU.add).then_inc(h_done, 1)

            def choose(r, g):
                n = g + r * GROUPS
                dve.wait_ge(logits_copied, n + 1)
                nc.vector.tensor_scalar(ex_in[:, 1:2], logit[:, NE:NE + 1], -1.0, None, ALU.mult)
                nc.vector.max(top[:], logit[:, 0:NE])
                dve.drain()
                nc.vector.max_index(top_at[:], top[:], logit[:, 0:NE])
                nc.vector.tensor_tensor(ex_in[:, 0:1], top[:, 1:2], top[:, 0:1], ALU.subtract)
                dve.drain().then_inc(top_ready, 1)
                nc.vector.tensor_copy(top_f[:], top_at[:, 0:2])
                dve.drain()
                dve.wait_ge(exp_ready, n + 1)
                nc.vector.tensor_scalar(gate_n[:, 0:2], ex[:], 1.0, None, ALU.add)
                dve.drain()
                nc.vector.reciprocal(gate_n[:, 0:2], gate_n[:, 0:2])
                dve.drain()
                nc.vector.tensor_tensor(gate_n[:, 2:3], gate_n[:, 0:1], gate_n[:, 1:2], ALU.mult)
                dve.drain()
                nc.vector.tensor_tensor(gate_n[:, 3:4], gate_n[:, 2:3], ex[:, 0:1], ALU.mult)
                dve.drain()
                for k in range(2):
                    nc.vector.tensor_scalar(gate_ab[:, k, :], iota[:, 0:NE], top_f[:, k:k + 1], gate_n[:, 2 + k:3 + k], ALU.is_equal, ALU.mult)
                dve.drain()
                nc.vector.tensor_tensor(gates[:], gate_ab[:, 0, :], gate_ab[:, 1, :], ALU.add).then_inc(gates_ready, 1)

            dve.wait_ge(s_hperm, 16 * GROUPS)
            for r in range(LAYERS):
                def step(g, odd):
                    aggregate(r, g)
                    gate_experts(r, g - 2, odd)
                    choose(r, g - 1)
                    add_strong(r, g - 3)

                aggregate(r, 0)
                aggregate(r, 1)
                choose(r, 0)
                aggregate(r, 2)
                gate_experts(r, 0, 0)
                choose(r, 1)
                with dve.Fori(0, (GROUPS - 3) // 2) as i:
                    step(i * 2 + 3, 1)
                    step(i * 2 + 4, 0)
                gate_experts(r, GROUPS - 2, 1)
                choose(r, GROUPS - 1)
                add_strong(r, GROUPS - 3)
                gate_experts(r, GROUPS - 1, 0)
                add_strong(r, GROUPS - 2)
                add_strong(r, GROUPS - 1)

            def moments(g):
                dve.drain()
                nc.vector.bn_stats(ln_st[:], x_res[:, bass.ds(g, 1), :].rearrange("p a n -> p (a n)"))
                dve.drain()
                nc.vector.bn_aggr(ln_of[:], ln_st[:])
                dve.drain()
                nc.vector.tensor_copy(ln_mv[:, bass.ds(g, 1), :].rearrange("p a n -> p (a n)"), ln_of[:])

            def all_rstd(count):
                dve.drain()
                nc.vector.tensor_scalar(ln_r[:, 0, :], ln_mv[:, :, 1], EPS_LN, None, ALU.add).then_inc(var_ready, 1)
                dve.wait_ge(rstd_ready, count)

            nc.vector.memset(gat_rows, 1.0).then_inc(ones_set, 1)
            dve.wait_ge(s_xperm, 16 * GROUPS)

            def residual(g, odd):
                xg = x_res[:, bass.ds(g, 1), :].rearrange("p a n -> p (a n)")
                dve.wait_ge(b_out_ready, g + 1)
                nc.vector.tensor_tensor(xg, ps_weak[odd][:, 0:IN], xg, ALU.add).then_inc(z_ready, 1)
                moments(g)

            with dve.Fori(0, GROUPS // 2) as i:
                residual(i * 2, 0)
                residual(i * 2 + 1, 1)
            residual(GROUPS - 1, 0)
            all_rstd(1)

            def normalize(g, odd):
                xg = x_res[:, bass.ds(g, 1), :].rearrange("p a n -> p (a n)")
                return nc.vector.tensor_scalar(xg, xg, ln_mv[:, bass.ds(g, 1), 0:1].rearrange("p a n -> p (a n)"),
                                               ln_r[:, 2, bass.ds(g, 1)], ALU.subtract, ALU.mult)

            def x1_row(g, odd, before):
                if before:
                    dve.wait_ge(x1T_ready, g - 1)
                normalize(g, odd)
                dve.drain()
                nc.vector.tensor_copy(x1[odd][:], x_res[:, bass.ds(g, 1), :].rearrange("p a n -> p (a n)")).then_inc(x1_ready, 1)

            x1_row(0, 0, False)
            x1_row(1, 1, False)
            with dve.Fori(1, GROUPS // 2) as i:
                x1_row(i * 2, 0, True)
                x1_row(i * 2 + 1, 1, True)
            x1_row(GROUPS - 1, 0, True)

            for k in range(2):
                r = LAYERS + k
                with dve.Fori(0, GROUPS) as g:
                    n = g + k * GROUPS
                    c0, c1 = units_of(dve, g)
                    dve.wait_ge(row_done, n + 1)
                    own = gat_rows[:, bass.ds(g, 1), :].rearrange("p a n -> p (a n)")
                    target = ad[k][:, bass.ds(g, 1), :].rearrange("p a n -> p (a n)")
                    nc.vector.tensor_copy(ad_cur[:], target)
                    nc.vector.tensor_tensor(m_new[:], own[:, GW - HEADS:GW], target, ALU.add)
                    nc.vector.tensor_scalar(gacc[:].rearrange("p h c -> p (h c)"), own[:, 0:HEADS * HC], loop_on[:, bass.ds(g, 1)], None, ALU.mult)
                    dve.drain()
                    nc.vector.scalar_tensor_tensor(m_new[:], m_new[:], 0.2, m_new[:], ALU.mult, ALU.max)
                    dve.drain()
                    nc.vector.tensor_scalar(score[:, SLOTS, :], m_new[:], loop_cap[:, bass.ds(g, 1)], None, ALU.min)
                    with dve.Fori(total * k + c0, total * k + c1) as q:
                        rows = ring[:, bass.ds((q % UNITS) * SLOTS, SLOTS), 0:GW]
                        dve.drain()
                        dve.wait_ge(arrived, total * LAYERS + q + (r + 2))
                        nc.vector.tensor_tensor(score[:, 0:SLOTS, :], rows[:, :, GW - HEADS:GW],
                                                ad_cur[:].unsqueeze(1).to_broadcast([P, SLOTS, HEADS]), ALU.add)
                        dve.drain()
                        nc.vector.scalar_tensor_tensor(score[:, 0:SLOTS, :], score[:, 0:SLOTS, :], 0.2, score[:, 0:SLOTS, :], ALU.mult, ALU.max)
                        dve.drain()
                        nc.vector.tensor_reduce(m_new[:], score[:].rearrange("p s h -> p h s"), AX.X, ALU.max)
                        dve.drain()
                        nc.vector.tensor_tensor(shifted[:], score[:], m_new[:].unsqueeze(1).to_broadcast([P, SLOTS + 1, HEADS]), ALU.subtract)
                        dve.drain().then_inc(shift_ready, 1)
                        nc.vector.tensor_copy(score[:, SLOTS, :], m_new[:])
                        dve.wait_ge(p_ready, q + 1)
                        p = ps_gate[:, 0:(SLOTS + 1) * HEADS].rearrange("p (s h) -> p s h", h=HEADS)
                        nc.vector.tensor_tensor(terms[:, SLOTS, :, :], gacc[:], p[:, SLOTS, :].unsqueeze(2).to_broadcast([P, HEADS, HC]), ALU.mult)
                        nc.vector.tensor_tensor(terms[:, 0:SLOTS, :, :], rows[:, :, 0:HEADS * HC].rearrange("p s (h c) -> p s h c", c=HC),
                                                p[:, 0:SLOTS, :].unsqueeze(3).to_broadcast([P, SLOTS, HEADS, HC]), ALU.mult).then_inc(ring_free, 1)
                        dve.drain()
                        nc.vector.tensor_reduce(gacc[:].rearrange("p h c -> p (h c)"), terms[:].rearrange("p s h c -> p (h c) s"), AX.X, ALU.add)
                    dve.drain()
                    nc.vector.tensor_scalar(rden[:], gacc[:, :, HID], EPS_GAT, None, ALU.add)
                    dve.drain()
                    nc.vector.reciprocal(rden[:], rden[:])
                    dve.drain()
                    nc.vector.tensor_tensor(y[:].rearrange("p (h c) -> p h c", c=HID), gacc[:, :, 0:HID],
                                            rden[:].unsqueeze(2).to_broadcast([P, HEADS, HID]), ALU.mult)
                    dve.drain()
                    nc.vector.tensor_tensor(y[:], y[:], gat_b[k][:], ALU.add)
                    dve.drain()
                    if k == 0:
                        nc.vector.tensor_scalar(y_neg[:], y[:], 0.0, None, ALU.min)
                        dve.drain().then_inc(neg_ready, 1)
                        nc.vector.tensor_scalar(y[:], y[:], 0.0, -1.0, ALU.max, ALU.add)
                        dve.drain()
                        dve.wait_ge(nexp_ready, g + 1)
                        dve.wait_ge(x1T_ready, g + GROUPS)
                        nc.vector.tensor_tensor(x1[0][:], y[:], y_exp[:], ALU.add).then_inc(x1_ready, 1)
                    else:
                        xg = x_res[:, bass.ds(g, 1), :].rearrange("p a n -> p (a n)")
                        nc.vector.tensor_tensor(xg, y[:], xg, ALU.add)
                        moments(g)
            all_rstd(2)
            with dve.Fori(0, GROUPS) as g:
                normalize(g, 0).then_inc(z_done, 1)

        @block.scalar
        def _(act):
            act.wait_ge(s_prepP, 1)
            nc.scalar.activation(b1_t[:], ps_weak[0][:, 0:LAYERS * NS * 4], ACT.Copy)
            act.drain().then_inc(s_prepP, 1)
            for k in range(2):
                act.wait_ge(s_prepP, 3 + 4 * k)
                nc.scalar.activation(gat_wt[:], ps_weak[0][:, 128:256], ACT.Copy)
                act.drain().then_inc(s_prepP, 1)
                act.wait_ge(s_prepP, 5 + 4 * k)
                nc.scalar.activation(gat_w[k][:, P:P + 2 * HEADS], ps_weak[1][:, 0:2 * HEADS], ACT.Copy)
                act.drain().then_inc(s_prepP, 1)

            act.wait_ge(s_xin, 16)
            with act.Fori(0, GROUPS) as g:
                nc.scalar.activation(x1[0][:], x_res[:, bass.ds(g, 1), :].rearrange("p a n -> p (a n)"), ACT.Copy).then_inc(s_xc, 1)
                act.wait_ge(s_xT, g + 1)
                nc.scalar.activation(x1_t[0][:], ps_w1[0][:, 0:P], ACT.Copy).then_inc(s_xTs, 1)
                act.wait_ge(s_h0, g + 1)
                nc.scalar.activation(h_res[:, bass.ds(g, 1), :].rearrange("p a n -> p (a n)"), ps_w1[1][:, 0:H], ACT.Copy).then_inc(s_h0s, 1)

            def operands(r, g, odd):
                n = g + r * GROUPS
                if r == 0:
                    act.wait_ge(s_hperm, 16 * GROUPS)
                else:
                    act.wait_ge(h_done, g + ((r - 1) * GROUPS + 1))
                w(act, hT_ready, n)
                nc.scalar.activation(h_cur[0][:], h_res[:, bass.ds(g, 1), :].rearrange("p a n -> p (a n)"), ACT.Copy).then_inc(hcur_ready, 1)
                act.wait_ge(hT_ready, n + 1)
                w(act, logits_ready, n)
                nc.scalar.activation(h_t[0][:], ps_tr[:, 0:H], ACT.Copy).then_inc(hT_copied, 1)
                act.wait_ge(aggT_ready, n + 1)
                w(act, weak_ready, n - 1)
                nc.scalar.activation(agg_t[odd][:], ps_tr[:, 0:H], ACT.Copy).then_inc(aggT_copied, 1)

            def logits(r, g):
                n = g + r * GROUPS
                act.wait_ge(logits_ready, n + 1)
                w(act, exp_ready, n)
                nc.scalar.activation(logit[:], ps_tr[:, H:H + NE + 1], ACT.Copy).then_inc(logits_copied, 1)

            def gate_exp(r, g):
                act.wait_ge(top_ready, g + (r * GROUPS + 1))
                nc.scalar.activation(ex[:], ex_in[:], ACT.Exp).then_inc(exp_ready, 1)

            def relu(r, g, odd, experts):
                n = g + r * GROUPS
                w(act, w2_ready, n - 1)
                for s in experts:
                    act.wait_ge(w1_ready, n * NS + (s + 1))
                    for c in range(4):
                        j = (r * NS + s) * 4 + c
                        last = nc.scalar.activation(strong[odd][:, s, c, :], ps_w1[s % 2][:, c * P:(c + 1) * P], ACT.Relu, bias=b1_t[:, j:j + 1])
                    last.then_inc(relu_ready, 1)

            def weak_relu(r, g, odd):
                n = g + r * GROUPS
                act.wait_ge(weak_ready, n + 1)
                act.wait_ge(gates_ready, n + 1)
                w(act, weak_added, n)
                for e in range(NW):
                    last = nc.scalar.activation(weak[:, e, :], ps_weak[e // 2][:, (e % 2) * H:(e % 2 + 1) * H], ACT.Relu, scale=gates[:, e:e + 1])
                last.then_inc(weak_copied, 1)
                act.wait_ge(gatesT_ready, n + 1)
                w(act, w2_ready, n - 1)
                nc.scalar.activation(gates_t[odd][:], ps_tr[0:NE, 384:512], ACT.Copy).then_inc(gatesT_copied, 1)

            for r in range(LAYERS):
                def step(g, odd):
                    operands(r, g, odd)
                    gate_exp(r, g - 1)
                    relu(r, g - 1, 1 - odd, (0, 1))
                    logits(r, g)
                    relu(r, g - 1, 1 - odd, (2, 3))
                    weak_relu(r, g - 1, 1 - odd)

                operands(r, 0, 0)
                logits(r, 0)
                step(1, 1)
                step(2, 0)
                with act.Fori(0, (GROUPS - 3) // 2) as i:
                    step(i * 2 + 3, 1)
                    step(i * 2 + 4, 0)
                gate_exp(r, GROUPS - 1)
                relu(r, GROUPS - 1, 0, range(NS))
                weak_relu(r, GROUPS - 1, 0)

            def state(g, odd, before):
                act.wait_ge(h_done, g + (LAYERS - 1) * GROUPS + 1)
                if before:
                    act.wait_ge(houtT_ready, g - 1)
                nc.scalar.activation(h_cur[odd][:], h_res[:, bass.ds(g, 1), :].rearrange("p a n -> p (a n)"), ACT.Copy).then_inc(hout_ready, 1)

            def state_t(g, odd):
                act.wait_ge(houtT_ready, g + 1)
                nc.scalar.activation(h_t[odd][:], ps_w1[odd][:, 0:H], ACT.Copy).then_inc(houtT_copied, 1)

            state(0, 0, False)
            state(1, 1, False)
            state_t(0, 0)
            with act.Fori(1, GROUPS // 2) as i:
                state(i * 2, 0, True)
                state_t(i * 2 - 1, 1)
                state(i * 2 + 1, 1, True)
                state_t(i * 2, 0)
            state(GROUPS - 1, 0, True)
            state_t(GROUPS - 2, 1)
            state_t(GROUPS - 1, 0)

            def all_rstd(count):
                act.wait_ge(var_ready, count)
                nc.scalar.activation(ln_r[:, 1, :], ln_r[:, 0, :], ACT.Ln)
                act.drain()
                nc.scalar.activation(ln_r[:, 2, :], ln_r[:, 1, :], ACT.Exp, scale=-0.5).then_inc(rstd_ready, 1)

            all_rstd(1)

            def table_operand(k, g, odd):
                act.wait_ge(x1T_ready, g + (k * GROUPS + 1))
                nc.scalar.activation(x1_t[odd][:], ps_w1[odd][:, 0:P], ACT.Copy).then_inc(x1T_copied, 1)

            def table_row(k, g, odd):
                act.wait_ge(row_ready, g + (k * GROUPS + 1))
                row = gat_rows[:, bass.ds(g, 1), :].rearrange("p a n -> p (a n)")
                nc.scalar.activation(row[:, 0:HEADS * HC].rearrange("p (h c) -> p h c", c=HC)[:, :, 0:HID],
                                     ps_weak[odd][:, 0:P].rearrange("p (h c) -> p h c", c=HID), ACT.Copy)
                nc.scalar.activation(row[:, GW - HEADS:GW], ps_weak[odd][:, P:P + HEADS], ACT.Copy)
                nc.scalar.activation(ad[k][:, bass.ds(g, 1), :].rearrange("p a n -> p (a n)"), ps_weak[odd][:, P + HEADS:P + 2 * HEADS], ACT.Copy)
                act.drain().then_inc(row_done, 1)

            act.wait_ge(ones_set, 1)
            table_operand(0, 0, 0)
            with act.Fori(0, GROUPS // 2) as i:
                table_operand(0, i * 2 + 1, 1)
                table_row(0, i * 2, 0)
                table_operand(0, i * 2 + 2, 0)
                table_row(0, i * 2 + 1, 1)
            table_row(0, GROUPS - 1, 0)

            total = all_units(act)

            def weights(k, g):
                c0, c1 = units_of(act, g)
                with act.Fori(total * k + c0, total * k + c1) as q:
                    act.wait_ge(shift_ready, q + 1)
                    nc.scalar.activation(ps_gate[:, 0:(SLOTS + 1) * HEADS], shifted[:].rearrange("p s h -> p (s h)"), ACT.Exp).then_inc(p_ready, 1)

            def elu_exp(g):
                act.wait_ge(neg_ready, g + 1)
                nc.scalar.activation(y_exp[:], y_neg[:], ACT.Exp).then_inc(nexp_ready, 1)

            for g in range(2):
                weights(0, g)
                elu_exp(g)
            table_operand(1, 0, 0)
            act.wait_ge(table_done, 16 * GROUPS * LAYERS)
            with act.Fori(2, GROUPS) as g:
                weights(0, g)
                elu_exp(g)
                table_row(1, g - 2, 0)
                table_operand(1, g - 1, 0)
            table_row(1, GROUPS - 2, 0)
            table_operand(1, GROUPS - 1, 0)
            table_row(1, GROUPS - 1, 0)
            with act.Fori(0, GROUPS) as g:
                weights(1, g)
            all_rstd(2)

        @block.tensor
        def _(pe):
            mm = nc.tensor.matmul
            pe.wait_ge(s_const, 1)
            pe.wait_ge(s_par, 16 * PAR_DMAS)
            nc.tensor.transpose(ps_weak[0][:, 0:LAYERS * NS * 4], b1_rows[:], ident[0:LAYERS * NS * 4, 0:LAYERS * NS * 4]).then_inc(s_prepP, 1)
            for k in range(2):
                pe.wait_ge(s_prepP, 2 + 4 * k)
                nc.tensor.transpose(ps_weak[0][:, 128:256], gat_w[k][:, 0:P], ident[:]).then_inc(s_prepP, 1)
                pe.wait_ge(s_prepP, 4 + 4 * k)
                mm(ps_weak[1][:, 0:2 * HEADS], gat_wt[:], gat_a[k][:], start=True, stop=True).then_inc(s_prepP, 1)
            pe.wait_ge(s_prepP, 10)
            def count(i, half):
                pe.wait_ge(s_1h, i * 2 + (half + 1))
                for t in range(HIST):
                    last = mm(ps_sum[0:GROUPS, 0:P], hi1h[:, half, t, :], lo1h[:, half, t, :], start=False, stop=False)
                last.then_inc(s_1h_used, 1)

            mm(ps_sum[0:GROUPS, 0:P], zero_b[:, 0:GROUPS], zero_b[:], start=True, stop=False)
            with pe.Fori(0, GROUPS) as g:
                pe.wait_ge(s_xc, g + 1)
                nc.tensor.transpose(ps_w1[0][:, 0:P], x1[0][:], ident[:]).then_inc(s_xT, 1)
                count(g, 0)
                pe.wait_ge(s_xTs, g + 1)
                mm(ps_w1[1][:, 0:H], ones_row[:], b_in_r[:], start=True, stop=False)
                mm(ps_w1[1][:, 0:H], x1_t[0][:], w_in[:], start=False, stop=True).then_inc(s_h0, 1)
                count(g, 1)
                pe.wait_ge(s_h0s, g + 1)
            with pe.Fori(GROUPS, ET // (2 * HIST)) as i:
                count(i, 0)
                count(i, 1)
            mm(ps_sum[0:GROUPS, 0:P], zero_b[:, 0:GROUPS], zero_b[:], start=False, stop=True).then_inc(s_hist, 1)
            pe.wait_ge(s_tot, 1)
            mm(ps_sum[0:GROUPS, 256:257], tri[0:GROUPS, 0:GROUPS], hist[:, 1, P - 1:P], start=True, stop=True).then_inc(s_pre, 1)
            pe.wait_ge(s_off, 1)
            nc.tensor.transpose(ps_tr[:, 0:GROUPS], hist[:, 0, :], ident[0:GROUPS, 0:GROUPS])
            nc.tensor.transpose(ps_tr[:, P:P + GROUPS], hist[:, 2, :], ident[0:GROUPS, 0:GROUPS]).then_inc(s_offT, 1)
            pe.wait_ge(s_bkt, 1)
            for g in range(GROUPS):
                last = mm(ps_sum[:, g:g + 1], bucket1h[:, g, :], ones_b[:, 0:1], start=True, stop=True)
            last.then_inc(s_bsum, 1)
            pe.wait_ge(s_bscan, 1)
            mm(ps_sum[:, 128:129], tri[:], bkt_sum[:, GROUPS - 1:GROUPS], start=True, stop=True).then_inc(s_below, 1)
            pe.wait_ge(s_base, 1)
            for g in range(GROUPS):
                own = (ps_gate, ps_moe)[g % 2][:, 0:P]
                w(pe, s_rank, g - 1)
                mm(own, bkt_base[:, g:g + 1].to_broadcast([P, P]), ident[:], start=True, stop=False)
                mm(own, tri_b[:], bucket1h[:, g, :], start=False, stop=True).then_inc(s_own, 1)

            pe.wait_ge(s_degp, 1)
            nc.tensor.transpose(ps_tr[0:GROUPS, 256:384], deg_p[:], ident[:]).then_inc(s_degT, 1)
            pe.wait_ge(s_kmax, 1)
            mm(ps_sum[0:1, 128:128 + GROUPS + 1], kmax[:], tri[0:GROUPS, 0:GROUPS + 1], start=True, stop=True)
            nc.tensor.transpose(ps_sum[0:1, 256:256 + GROUPS], kmax[:], ident[0:GROUPS, 0:GROUPS]).then_inc(s_cumP, 1)

            def operands(r, g):
                n = g + r * GROUPS
                pe.wait_ge(hcur_ready, n + 1)
                w(pe, logits_copied, n)
                w(pe, gatesT_copied, n - 1)
                nc.tensor.transpose(ps_tr[:, 0:P], h_cur[0][:, 0:P], ident[:])
                nc.tensor.transpose(ps_tr[:, P:H], h_cur[0][:, P:H], ident[:]).then_inc(hT_ready, 1)
                pe.wait_ge(hT_copied, n + 1)
                pe.wait_ge(agg_ready, n + 1)
                nc.tensor.transpose(ps_tr[:, 0:P], agg[:, 0:P], ident[:])
                nc.tensor.transpose(ps_tr[:, P:H], agg[:, P:H], ident[:]).then_inc(aggT_ready, 1)

            def router(r, g, odd):
                pe.wait_ge(aggT_copied, g + (r * GROUPS + 1))
                lg = ps_tr[:, H:H + NE + 1]
                mm(lg, ones_row[:], rt_b[:, r, :], start=True, stop=False)
                for k in range(2):
                    mm(lg, h_t[0][:, k * P:(k + 1) * P], rt_w[:, r, k, :], start=False, stop=False)
                for k in range(2):
                    last = mm(lg, agg_t[odd][:, k * P:(k + 1) * P], rt_w[:, r, 2 + k, :], start=False, stop=k == 1)
                last.then_inc(logits_ready, 1)

            def strong_first(r, g, odd, experts):
                n = g + r * GROUPS
                for s in experts:
                    w(pe, relu_ready, n * NS + (s - 1))
                    for c in range(4):
                        for k in range(2):
                            last = mm(ps_w1[s % 2][:, c * P:(c + 1) * P], w1_w[:, k, s, c * P:(c + 1) * P],
                                      agg_t[odd][:, k * P:(k + 1) * P], start=k == 0, stop=k == 1)
                    last.then_inc(w1_ready, 1)

            def weak_gates(r, g, odd):
                n = g + r * GROUPS
                w(pe, weak_copied, n)
                for j in range(2):
                    mm(ps_weak[j][:], ones_row[:], wk_b[:, j * 512:(j + 1) * 512], start=True, stop=False)
                    for k in range(2):
                        last = mm(ps_weak[j][:], agg_t[odd][:, k * P:(k + 1) * P], wk_w[:, k, j * 512:(j + 1) * 512], start=False, stop=k == 1)
                last.then_inc(weak_ready, 1)
                pe.wait_ge(gates_ready, n + 1)
                if logits_after:
                    pe.wait_ge(logits_copied, n + 2)
                nc.tensor.transpose(ps_tr[0:NE, 384:512], gates[:], ident[:]).then_inc(gatesT_ready, 1)

            def broadcast(r, g):
                n = g + r * GROUPS
                w(pe, gated, n * NS)
                for s in range(NS):
                    last = mm(ps_gate[:, s * P:(s + 1) * P], gates[:, NW + s:NW + s + 1].to_broadcast([P, P]), ident[:], start=True, stop=True)
                last.then_inc(bcast_ready, 1)

            def second(r, g, odd):
                n = g + r * GROUPS
                pe.wait_ge(gatesT_copied, n + 1)
                w(pe, h_done, n)
                mm(ps_moe[:, 0:H], gates_t[odd][:], b2_w[:], start=True, stop=False)
                for s in range(NS):
                    pe.wait_ge(gated, n * NS + (s + 1))
                    for c in range(4):
                        last = mm(ps_moe[:, 0:H], strong[odd][:, s, c, :], w2_w[:, c, s, :], start=False, stop=s == NS - 1 and c == 3)
                last.then_inc(w2_ready, 1)

            for r in range(LAYERS):
                def step(g, odd, lag=True):
                    operands(r, g)
                    strong_first(r, g - 1, 1 - odd, (0, 1))
                    router(r, g, odd)
                    strong_first(r, g - 1, 1 - odd, (2, 3))
                    weak_gates(r, g - 1, 1 - odd)
                    if lag:
                        second(r, g - 2, odd)
                    broadcast(r, g - 1)

                logits_after = True
                pe.wait_ge(s_wts, 160 * (r + 1))
                operands(r, 0)
                router(r, 0, 0)
                step(1, 1, False)
                step(2, 0)
                with pe.Fori(0, (GROUPS - 3) // 2) as i:
                    step(i * 2 + 3, 1)
                    step(i * 2 + 4, 0)
                logits_after = False
                strong_first(r, GROUPS - 1, 0, range(NS))
                weak_gates(r, GROUPS - 1, 0)
                second(r, GROUPS - 2, 1)
                broadcast(r, GROUPS - 1)
                second(r, GROUPS - 1, 0)

            def state_t(g, odd, before):
                pe.wait_ge(hout_ready, g + 1)
                if before:
                    pe.wait_ge(houtT_copied, g - 1)
                nc.tensor.transpose(ps_w1[odd][:, 0:P], h_cur[odd][:, 0:P], ident[:])
                nc.tensor.transpose(ps_w1[odd][:, P:H], h_cur[odd][:, P:H], ident[:]).then_inc(houtT_ready, 1)

            def project(g, odd, before):
                if before:
                    pe.wait_ge(z_ready, g - 1)
                mm(ps_weak[odd][:, 0:IN], ones_row[:], b_out_r[:], start=True, stop=False)
                pe.wait_ge(houtT_copied, g + 1)
                for k in range(2):
                    last = mm(ps_weak[odd][:, 0:IN], h_t[odd][:, k * P:(k + 1) * P], w_out[:, k, :], start=False, stop=k == 1)
                last.then_inc(b_out_ready, 1)

            state_t(0, 0, False)
            state_t(1, 1, False)
            project(0, 0, False)
            state_t(2, 0, True)
            project(1, 1, False)
            with pe.Fori(1, GROUPS // 2) as i:
                state_t(i * 2 + 1, 1, True)
                project(i * 2, 0, True)
                state_t(i * 2 + 2, 0, True)
                project(i * 2 + 1, 1, True)
            project(GROUPS - 1, 0, True)

            def table_operand(k, g, odd, before):
                n = g + k * GROUPS
                pe.wait_ge(x1_ready, n + 1)
                if before:
                    pe.wait_ge(x1T_copied, n + 1 - before)
                nc.tensor.transpose(ps_w1[odd][:, 0:P], x1[odd][:], ident[:]).then_inc(x1T_ready, 1)

            def table_row(k, g, odd, before):
                n = g + k * GROUPS
                pe.wait_ge(x1T_copied, n + 1)
                if before:
                    pe.wait_ge(row_done, n + 1 - before)
                mm(ps_weak[odd][:, 0:P + 2 * HEADS], x1_t[odd][:], gat_w[k][:], start=True, stop=True).then_inc(row_ready, 1)

            pe.wait_ge(z_ready, GROUPS)
            table_operand(0, 0, 0, 0)
            table_operand(0, 1, 1, 0)
            table_row(0, 0, 0, 0)
            table_operand(0, 2, 0, 2)
            table_row(0, 1, 1, 0)
            with pe.Fori(1, GROUPS // 2) as i:
                table_operand(0, i * 2 + 1, 1, 2)
                table_row(0, i * 2, 0, 2)
                table_operand(0, i * 2 + 2, 0, 2)
                table_row(0, i * 2 + 1, 1, 2)
            table_row(0, GROUPS - 1, 0, 2)
            with pe.Fori(0, GROUPS) as g:
                table_operand(1, g, 0, 1)
                table_row(1, g, 0, 1)


_INS = ['x', 'src', 'dst', 'L0_gnn_W_in', 'L0_gnn_b_in', 'L0_gnn_router_W', 'L0_gnn_router_b', 'L0_gnn_weak_W', 'L0_gnn_weak_b',
        'L0_gnn_strong_W1', 'L0_gnn_strong_b1', 'L0_gnn_strong_W2', 'L0_gnn_strong_b2', 'L0_gnn_conf_W', 'L0_gnn_conf_b',
        'L0_gnn_W_out', 'L0_gnn_b_out', 'L1_gnn_W1', 'L1_gnn_a_src1', 'L1_gnn_a_dst1', 'L1_gnn_b1', 'L1_gnn_W2',
        'L1_gnn_a_src2', 'L1_gnn_a_dst2', 'L1_gnn_b2']


def kernel(**inputs):
    import numpy as np
    import concourse.bacc as bacc
    from concourse.bass_utils import run_bass_kernel_spmd

    nc = bacc.Bacc("TRN2", target_bir_lowering=False, num_devices=1)
    arrays, args = {}, []
    for name in _INS:
        a = np.ascontiguousarray(inputs[name])
        if name == "x":
            a = np.concatenate([a, np.zeros((NP - N, IN), a.dtype)])
        elif name == "src":
            a = np.concatenate([a, np.zeros(EP - E, a.dtype)])
        elif name == "dst":
            a = np.concatenate([a, np.full(EP - E, NP, a.dtype)])
        arrays[f"in_{name}"] = a
        args.append(nc.dram_tensor(f"in_{name}", a.shape, mybir.dt.from_np(a.dtype), kind="ExternalInput").ap())
    args.append(nc.dram_tensor("out", (NP, IN), F32, kind="ExternalOutput").ap())
    gnn_kernel(nc, *args)
    r = run_bass_kernel_spmd(nc, [arrays], core_ids=[0])
    return r.results[0]["out"][:N]
```

```python
import concourse.bass as bass
from concourse import mybir
from contextlib import ExitStack

F32 = mybir.dt.float32
BF16 = mybir.dt.bfloat16
I32 = mybir.dt.int32
U32 = mybir.dt.uint32
ALU = mybir.AluOpType
ACT = mybir.ActivationFunctionType
AX = mybir.AxisListType

P = 128
N = 6250
E = 106250
GROUPS = -(-N // P)
NP = GROUPS * P
ET = 832
EP = ET * P
DUMMY = NP
IN, H, LAYERS = 128, 256, 3
LOOPS = 3750
NW, NS = 4, 4
NE = NW + NS
HEADS, HID = 4, 32
HC = HID + 1
GW = HEADS * HC + HEADS
SLOTS = 4
RING = 32
UNITS = RING // SLOTS
RUN = 64
COLS = GROUPS * RUN + RUN
UMAX = (E + GROUPS * 2 * SLOTS + RING) // SLOTS
CAP = UMAX * SLOTS + RUN
STRIDE = 12
BATCH = 4
HIST = 8
LOWEST = -1.5e38
DUMMY_SCORE = -1.0e38
EPS_LN = 1e-5
EPS_GAT = 1e-16


def w(eng, sem, value):
    if not (isinstance(value, int) and value <= 0):
        eng.wait_ge(sem, value)


def gnn_kernel(nc, x, src, dst, W_in, b_in, router_W, router_b, weak_W, weak_b, strong_W1, strong_b1,
               strong_W2, strong_b2, conf_W, conf_b, W_out, b_out, W1, a_src1, a_dst1, b1, W2, a_src2,
               a_dst2, b2, out):
    ctx = ExitStack()
    with ctx:
        def sb(name, shape, dt=F32):
            return ctx.enter_context(nc.sbuf_tensor(name, shape, dt))

        def sem(name):
            return ctx.enter_context(nc.semaphore(name))

        def dram(name, shape, dt=F32):
            return nc.dram_tensor(name, shape, dt, kind="Internal").ap()

        hidden_tab = [dram(f"hidden_tab{i}", [NP + 1, H]) for i in range(LAYERS)]
        gat_tab = [dram(f"gat_tab{i}", [NP + 1, GW]) for i in range(2)]
        meta_tab = dram("meta_tab", [NP, 4], I32)
        slot_tab = dram("slot_tab", [P, CAP], I32)

        PART_ROWS = (0, 32, 64)

        h_res = sb("h_res", [P, GROUPS, H])
        x_res = sb("x_res", [P, GROUPS, IN])
        perm = sb("perm", [P, GROUPS, 4], I32)
        rdeg = sb("rdeg", [P, GROUPS])
        self_on = sb("self_on", [P, GROUPS])
        loop_on = sb("loop_on", [P, GROUPS])
        loop_cap = sb("loop_cap", [P, GROUPS])
        ring = sb("ring", [P, RING, H])
        stage = sb("stage", [P, 2, RING // 2], I32)
        cum = sb("cum", [1, GROUPS + 2], I32)
        cum_full = sb("cum_full", [1, GROUPS + 2], I32)
        ad = [sb(f"ad{i}", [P, GROUPS, HEADS]) for i in range(2)]

        wbuf = sb("wbuf", [P, 10240])
        run_raw = wbuf[:, 0:GROUPS * RUN].bitcast(I32).rearrange("p (g k) -> p g k", k=RUN)
        slots_sb = wbuf[:, GROUPS * RUN:GROUPS * RUN + COLS].bitcast(I32)
        bias_f = wbuf[:, 0:LAYERS * NW * H]
        d_at = GROUPS * RUN + COLS
        bucket1h = wbuf[:, d_at:d_at + GROUPS * P // 2].bitcast(BF16).rearrange("p (g b) -> p g b", b=P)
        wk_w = wbuf[:, 0:2048].rearrange("p (k n) -> p k n", k=2)
        w1_w = wbuf[:, 2048:6144].rearrange("p (k s n) -> p k s n", k=2, s=NS)
        w2_w = wbuf[:, 6144:10240].rearrange("p (c s n) -> p c s n", c=4, s=NS)
        gat_rows = wbuf[:, 0:GROUPS * GW].rearrange("p (g n) -> p g n", n=GW)

        iota_i = sb("iota_i", [P, P], I32)
        iota = sb("iota", [P, P])
        iota_b = sb("iota_b", [P, P], BF16)
        ident = sb("ident", [P, P])
        tri = sb("tri", [P, P])
        tri_b = sb("tri_b", [P, P], BF16)
        ones_b = sb("ones_b", [P, P], BF16)
        zero_b = sb("zero_b", [P, P], BF16)
        ones_row = sb("ones_row", [1, P])
        dummy_row = sb("dummy_row", [1, H])
        dummy_score = sb("dummy_score", [1, HEADS])

        lo_i = ring[:, 0:4, :].rearrange("p a b -> p (a b)")[:, 0:ET].bitcast(I32)
        lo_b = ring[:, 4:6, :].rearrange("p a b -> p (a b)").bitcast(BF16)[:, 0:ET]
        hi_b = ring[:, 6:8, :].rearrange("p a b -> p (a b)").bitcast(BF16)[:, 0:ET]
        hist = sb("hist", [GROUPS, 3, P])
        row_pre = sb("row_pre", [GROUPS, 1])
        deg_n = sb("deg_n", [P, GROUPS])
        off_n = sb("off_n", [P, GROUPS])
        bucket = sb("bucket", [P, GROUPS], BF16)
        bkt_count = sb("bkt_count", [P, GROUPS])
        bkt_sum = sb("bkt_sum", [P, GROUPS])
        bkt_first = sb("bkt_first", [P, 1])
        bkt_base = sb("bkt_base", [P, GROUPS])
        zeros = sb("zeros", [P, P])
        rank = sb("rank", [P, GROUPS])
        rank_i = sb("rank_i", [P, 3, GROUPS], I32)
        meta = sb("meta", [P, GROUPS, 4], I32)
        deg_p = sb("deg_p", [P, GROUPS])
        kmax = sb("kmax", [GROUPS, 1])
        kmax_i = sb("kmax_i", [GROUPS, 1], I32)
        cum_f = sb("cum_f", [1, GROUPS + 2])
        cum_at = sb("cum_at", [1, GROUPS + 2], I32)
        run_f = x_res[:].rearrange("p g n -> p (g n)")[:, 0:GROUPS * RUN]
        run_m = x_res[:].rearrange("p g n -> p (g n)")[:, GROUPS * RUN:2 * GROUPS * RUN]
        long_off = sb("long_off", [P, 2])
        long_idx = sb("long_idx", [P, 1], I32)
        long_raw = sb("long_raw", [P, SLOTS], I32)
        long_dummy = sb("long_dummy", [P, SLOTS], I32)
        long_meta = sb("long_meta", [P, 2], I32)

        w_in = sb("w_in", [P, H])
        b_in_r = sb("b_in_r", [1, H])
        rt_w = sb("rt_w", [P, LAYERS, 4, NE + 1])
        rt_b = sb("rt_b", [1, LAYERS, NE + 1])
        b1_rows = sb("b1_rows", [LAYERS * NS * 4, P])
        b1_t = sb("b1_t", [P, LAYERS * NS * 4])
        wk_parts = sb("wk_parts", [P, LAYERS, NW * H], BF16)
        b2_w = sb("b2_w", [NE, H])
        w_out = sb("w_out", [P, 2, IN])
        b_out_r = sb("b_out_r", [1, IN])
        gat_w = [sb(f"gat_w{i}", [P, P + 2 * HEADS]) for i in range(2)]
        gat_a = [sb(f"gat_a{i}", [P, 2 * HEADS]) for i in range(2)]
        gat_b = [sb(f"gat_b{i}", [P, P]) for i in range(2)]
        gat_wt = sb("gat_wt", [P, P])

        h_cur = [sb(f"h_cur{i}", [P, H]) for i in range(2)]
        h_t = [sb(f"h_t{i}", [P, H]) for i in range(2)]
        agg = sb("agg", [P, H])
        agg_t = [sb(f"agg_t{i}", [P, H]) for i in range(2)]
        part = sb("part", [P, H])
        strong = [sb(f"strong{i}", [P, NS, 4, P]) for i in range(2)]
        weak = sb("weak", [P, NW, H])
        room = [t[:].rearrange("p s c n -> p (s c n)") for t in strong]
        lo1h = room[0][:, 0:HIST * P].bitcast(BF16).rearrange("p (a t n) -> p a t n", a=2, n=P)
        hi1h = room[0][:, HIST * P:HIST * (P + GROUPS)].bitcast(BF16).rearrange("p (a t n) -> p a t n", a=2, n=GROUPS)
        dst_i = room[1][:, 0:ET].bitcast(I32)
        sort_tmp = room[1][:, ET:ET + 4 * P].rearrange("p (a n) -> p a n", n=P)
        node, last_at = (room[1][:, ET + 4 * P + i * GROUPS:ET + 4 * P + (i + 1) * GROUPS] for i in range(2))
        terms = room[0][:, 0:(SLOTS + 1) * HEADS * HC].rearrange("p (s h c) -> p s h c", h=HEADS, c=HC)
        y, y_neg, y_exp = (room[1][:, i * P:(i + 1) * P] for i in range(3))
        logit = sb("logit", [P, NE + 1])
        top = sb("top", [P, 8])
        top_at = sb("top_at", [P, 8], U32)
        top_f = sb("top_f", [P, 2])
        ex_in = sb("ex_in", [P, 2])
        ex = sb("ex", [P, 2])
        gate_n = sb("gate_n", [P, 4])
        gate_ab = sb("gate_ab", [P, 2, NE])
        gates = sb("gates", [P, NE])
        gates_t = [sb(f"gates_t{i}", [NE, P]) for i in range(2)]
        x1 = [sb(f"x1_{i}", [P, IN]) for i in range(2)]
        x1_t = [sb(f"x1_t{i}", [P, IN]) for i in range(2)]
        ln_st = sb("ln_st", [P, 2, 6])
        ln_of = sb("ln_of", [P, 2, 2])
        ln_mv = sb("ln_mv", [P, GROUPS, 2])
        ln_r = sb("ln_r", [P, 3, GROUPS])
        ad_cur = sb("ad_cur", [P, HEADS])
        score = sb("score", [P, SLOTS + 1, HEADS])
        m_new = sb("m_new", [P, HEADS])
        shifted = sb("shifted", [P, SLOTS + 1, HEADS])
        gacc = sb("gacc", [P, HEADS, HC])
        rden = sb("rden", [P, HEADS])

        def bank(name):
            return ctx.enter_context(nc.psum_tensor(name, [P, 512], F32))

        ps_w1 = [bank("ps_w1a"), bank("ps_w1b")]
        ps_weak = [bank("ps_weak_a"), bank("ps_weak_b")]
        ps_gate = bank("ps_gate")
        ps_moe = bank("ps_moe")
        ps_tr = bank("ps_tr")
        ps_sum = bank("ps_sum")
        acc = ps_sum[:, 0:H]

        s_const, s_ints, s_par, s_xin, s_dummy, s_wts = (sem(n) for n in (
            "s_const", "s_ints", "s_par", "s_xin", "s_dummy", "s_wts"))
        s_1h, s_1h_used, s_hist, s_tot, s_pre, s_off, s_offT = (sem(n) for n in (
            "s_1h", "s_1h_used", "s_hist", "s_tot", "s_pre", "s_off", "s_offT"))
        s_bkt, s_bsum, s_bscan, s_below, s_base, s_own, s_rank, s_meta, s_scat, s_perm = (sem(n) for n in (
            "s_bkt", "s_bsum", "s_bscan", "s_below", "s_base", "s_own", "s_rank", "s_meta", "s_scat", "s_perm"))
        s_runs, s_hperm, s_xperm, s_degp, s_degT, s_kmax, s_cumP, s_cum, s_compact, s_slots, s_slotst, s_slotst_rest, s_long, s_longrun, s_longst = (sem(n) for n in (
            "s_runs", "s_hperm", "s_xperm", "s_degp", "s_degT", "s_kmax", "s_cumP", "s_cum", "s_compact", "s_slots",
            "s_slotst", "s_slotst_rest", "s_long", "s_longrun", "s_longst"))
        s_xc, s_xT, s_xTs, s_h0, s_h0s, s_h0st, s_prep, s_prepP = (sem(n) for n in (
            "s_xc", "s_xT", "s_xTs", "s_h0", "s_h0s", "s_h0st", "s_prep", "s_prepP"))
        gathered = [sem(f"gathered{u}") for u in range(UNITS)]
        staged = [sem(f"staged{h}") for h in range(2)]
        half_begun, arrived, round_gathered, ring_free, table_done = (sem(n) for n in (
            "half_begun", "arrived", "round_gathered", "ring_free", "table_done"))
        hcur_ready, agg_ready, opT_ready, opT_copied = sem("hcur_ready"), sem("agg_ready"), sem("opT_ready"), sem("opT_copied")
        logits_ready, logits_copied, top_ready, exp_ready, gates_ready = (sem(n) for n in (
            "logits_ready", "logits_copied", "top_ready", "exp_ready", "gates_ready"))
        w1_ready, relu_ready, gated, w2_ready = sem("w1_ready"), sem("relu_ready"), sem("gated"), sem("w2_ready")
        weak_ready, weak_copied, weak_added = sem("weak_ready"), sem("weak_copied"), sem("weak_added")
        bcast_ready, gatesT_ready, gatesT_copied, h_done = sem("bcast_ready"), sem("gatesT_ready"), sem("gatesT_copied"), sem("h_done")
        hout_ready, houtT_ready, houtT_copied, b_out_ready, z_ready, var_ready, rstd_ready = (sem(n) for n in (
            "hout_ready", "houtT_ready", "houtT_copied", "b_out_ready", "z_ready", "var_ready", "rstd_ready"))
        x1_ready, x1T_ready, x1T_copied, ones_set, row_ready, row_done = (sem(n) for n in (
            "x1_ready", "x1T_ready", "x1T_copied", "ones_set", "row_ready", "row_done"))
        shift_ready, p_ready, neg_ready, nexp_ready, z_done = (sem(n) for n in (
            "shift_ready", "p_ready", "neg_ready", "nexp_ready", "z_done"))
        s_out = sem("s_out")

        block = ctx.enter_context(nc.Block())
        n_par = [0]

        def units_of(eng, g, table=cum):
            return (eng.value_load(table[0:1, bass.ds(g, 1)], min_val=0, max_val=UMAX),
                    eng.value_load(table[0:1, bass.ds(g + 1, 1)], min_val=2, max_val=UMAX))

        def all_units(eng):
            return eng.value_load(cum_full[0:1, GROUPS:GROUPS + 1], min_val=UNITS, max_val=UMAX)

        WT_DMAS = 2 * 2 + 4 + 1
        PAR_DMAS = 5 + 3 + 4 * LAYERS + 2 * (2 + 2 * HEADS)

        @block.sync
        def _(sp):
            sp.dma_start(dst_i[:], dst.rearrange("(p t) -> p t", p=P)).then_inc(s_ints, 16)
            sp.dma_start(x_res[:], x.rearrange("(g p) n -> p g n", p=P)).then_inc(s_xin, 16)
            sp.wait_ge(s_prep, 1)

            def par(o, i):
                sp.dma_start(o, i).then_inc(s_par, 16)
                n_par[0] += 1

            par(w_in[:], W_in)
            par(b_in_r[:], b_in.rearrange("(a n) -> a n", a=1))
            par(w_out[:], W_out.rearrange("(k p) n -> p k n", p=P))
            par(b_out_r[:], b_out.rearrange("(a n) -> a n", a=1))
            par(b1_rows[:], strong_b1.rearrange("l s (c p) -> (l s c) p", p=P))
            for row in PART_ROWS:
                par(bias_f[row:row + 1, :], weak_b.rearrange("(a l) e n -> a (l e n)", a=1))
            with nc.allow_non_contiguous_dma(reason="a few columns of weights"):
                for l in range(LAYERS):
                    par(rt_w[:, l, :, 0:NE], router_W[l].rearrange("(k p) e -> p k e", p=P))
                    par(rt_w[:, l, 0:2, NE], conf_W[l].rearrange("(k p) o -> p (k o)", p=P))
                    par(rt_b[:, l, 0:NE], router_b[l:l + 1, :])
                    par(rt_b[:, l, NE:NE + 1], conf_b[l:l + 1, :])
                par(gat_w[0][:, 0:P], W1)
                par(gat_w[1][:, 0:P], W2)
                par(gat_b[0][:], b1.rearrange("(a n) -> a n", a=1).to_broadcast([P, P]))
                par(gat_b[1][:], b2.rearrange("(a n) -> a n", a=1).to_broadcast([P, P]))
                for k, (a_s, a_d) in enumerate(((a_src1, a_dst1), (a_src2, a_dst2))):
                    for h in range(HEADS):
                        rows = slice(HID * h, HID * h + HID) if k == 0 else slice(0, P)
                        vec = slice(h, h + 1) if k == 0 else slice(0, 1)
                        par(gat_a[k][rows, h:h + 1], a_s[vec, :].rearrange("a c -> c a"))
                        par(gat_a[k][rows, HEADS + h:HEADS + h + 1], a_d[vec, :].rearrange("a c -> c a"))

            sp.wait_ge(s_const, 1)
            for t in hidden_tab:
                sp.dma_start(t[DUMMY:DUMMY + 1, :], dummy_row[:, :]).then_inc(s_dummy, 16)
            for t in gat_tab:
                sp.dma_start(t[DUMMY:DUMMY + 1, 0:GW - HEADS], dummy_row[:, 0:GW - HEADS]).then_inc(s_dummy, 16)
                sp.dma_start(t[DUMMY:DUMMY + 1, GW - HEADS:GW], dummy_score[:, :]).then_inc(s_dummy, 16)

            with sp.Fori(0, GROUPS) as g:
                sp.wait_ge(s_h0s, g + 1)
                sp.dma_start(hidden_tab[0][bass.ds(g * P, P), :], h_res[:, bass.ds(g, 1), :].rearrange("p a n -> p (a n)"))\
                    .then_inc(s_h0st, 16)

            sp.wait_ge(s_scat, 16 * GROUPS)
            sp.dma_start(perm[:], meta_tab.rearrange("(p g) c -> p g c", p=P)).then_inc(s_perm, 16)
            sp.wait_ge(s_slots, 1)
            sp.dma_start(slot_tab[:, 0:RING], slots_sb[:, 0:RING]).then_inc(s_slotst, 16)
            sp.dma_start(slot_tab[:, RING:COLS], slots_sb[:, RING:COLS]).then_inc(s_slotst_rest, 16)
            sp.wait_ge(s_slotst, 16)
            sp.wait_ge(s_long, 1)

            total = all_units(sp)
            bodies = total // UNITS
            for r in range(LAYERS + 2):
                if r < LAYERS:
                    if r:
                        sp.wait_ge(w2_ready, r * GROUPS)
                    for k in range(2):
                        sp.dma_start(wk_w[:, k, :].rearrange("p (e n) -> p e n", e=NW),
                                     weak_W[r, :, k * P:(k + 1) * P, :].rearrange("e p n -> p e n")).then_inc(s_wts, 16)
                        sp.dma_start(w1_w[:, k, :, :],
                                     strong_W1[r, :, k * P:(k + 1) * P, :].rearrange("s p n -> p s n")).then_inc(s_wts, 16)
                    for c in range(4):
                        sp.dma_start(w2_w[:, c, :, :],
                                     strong_W2[r, :, c * P:(c + 1) * P, :].rearrange("s p n -> p s n")).then_inc(s_wts, 16)
                    sp.dma_start(b2_w[NW:NE, :], strong_b2[r]).then_inc(s_wts, 16)

                if r:
                    sp.wait_ge(round_gathered, r)
                for half in range(2):
                    sp.dma_start(stage[:, half, :], slot_tab[:, half * RING // 2:(half + 1) * RING // 2])\
                        .then_inc(staged[half], 16)
                if r == 0:
                    sp.wait_ge(s_slotst_rest, 16)
                with sp.Fori(1, bodies) as i:
                    for half in range(2):
                        sp.wait_ge(arrived, total * r + i * UNITS + (r + 1 - UNITS + (half + 1) * UNITS // 2))
                        sp.dma_start(stage[:, half, :], slot_tab[:, bass.ds(i * RING + half * RING // 2, RING // 2)])\
                            .then_inc(staged[half], 16)
            sp.wait_ge(s_out, 16 * GROUPS)

        @block.gpsimd
        def _(pool):
            nc.gpsimd.iota(iota_i[:], pattern=[[1, P]], base=0, channel_multiplier=0)
            nc.gpsimd.memset(dummy_row[:], 0.0)
            nc.gpsimd.memset(dummy_score[:], DUMMY_SCORE)
            nc.gpsimd.memset(rt_w[:], 0.0)
            nc.gpsimd.memset(b2_w[:], 0.0)
            nc.gpsimd.memset(gat_a[0][:], 0.0)
            nc.gpsimd.memset(gat_a[1][:], 0.0)
            nc.gpsimd.memset(wk_parts[:], 0.0)
            nc.gpsimd.memset(ident[:], 0.0)
            nc.gpsimd.memset(tri[:], 1.0)
            nc.gpsimd.memset(ones_b[:], 1.0)
            nc.gpsimd.memset(zero_b[:], 0.0)
            nc.gpsimd.memset(ones_row[:], 1.0)
            pool.drain().then_inc(s_prep, 1)
            nc.gpsimd.tensor_copy(iota[:], iota_i[:])
            nc.gpsimd.affine_select(out=ident[:], in_=ident[:], compare_op=ALU.not_equal, fill=1.0,
                                    base=0, pattern=[[-1, P]], channel_multiplier=1)
            nc.gpsimd.affine_select(out=tri[:], in_=tri[:], compare_op=ALU.is_gt, fill=0.0,
                                    base=0, pattern=[[1, P]], channel_multiplier=-1)
            pool.drain()
            nc.gpsimd.tensor_copy(iota_b[:], iota[:])
            nc.gpsimd.tensor_copy(tri_b[:], tri[:])
            nc.gpsimd.iota(meta[:, :, 0], pattern=[[P, GROUPS]], base=0, channel_multiplier=1)
            nc.gpsimd.memset(meta[:, :, 3], 0)
            nc.gpsimd.memset(long_dummy[:], DUMMY)
            pool.drain().then_inc(s_const, 1)

            pool.wait_ge(s_par, 16 * PAR_DMAS)
            parts = wk_parts[:].rearrange("p l n -> p (l n)")
            for nth, row in enumerate(PART_ROWS):
                nc.gpsimd.tensor_copy(parts[row:row + 1, :], bias_f[row:row + 1, :])
                for _ in range(nth):
                    pool.drain()
                    nc.gpsimd.tensor_tensor(bias_f[row:row + 1, :], bias_f[row:row + 1, :], parts[row:row + 1, :], ALU.subtract)
                    pool.drain()
                    nc.gpsimd.tensor_copy(parts[row:row + 1, :], bias_f[row:row + 1, :])
            pool.drain()

            pool.wait_ge(s_meta, 1)
            for g in range(GROUPS):
                pool.indirect_dma_start(out=meta_tab, out_offset=bass.IndirectOffsetOnAxis(ap=rank_i[:, 2, g:g + 1], axis=0),
                                        in_=meta[:, g, :], in_offset=None).then_inc(s_scat, 16)
            pool.wait_ge(s_perm, 16)
            for g in range(GROUPS):
                pool.indirect_dma_start(out=run_raw[:, g, :], out_offset=None, in_=src.rearrange("(a e) -> a e", a=1),
                                        in_offset=bass.IndirectOffsetOnAxis(ap=perm[:, g, 1:2], axis=1))\
                    .then_inc(gathered[UNITS - 1] if g < SLOTS else s_runs, 16)
            pool.wait_ge(s_h0st, 16 * GROUPS)
            for g in range(GROUPS):
                pool.indirect_dma_start(out=h_res[:, g, :], out_offset=None, in_=hidden_tab[0],
                                        in_offset=bass.IndirectOffsetOnAxis(ap=perm[:, g, 0:1], axis=0)).then_inc(s_hperm, 16)

            pool.wait_ge(s_cum, 1)
            most = pool.value_load(cum[0:1, GROUPS + 1:GROUPS + 2], min_val=1, max_val=E)
            with pool.If(most > RUN // SLOTS):
                pool.wait_ge(s_slotst, 16)
                pool.wait_ge(s_slotst_rest, 16)
                with pool.Fori(0, GROUPS) as g:
                    c0, c1 = units_of(pool, g, cum_full)
                    nc.gpsimd.tensor_copy(long_meta[:], perm[:, bass.ds(g, 1), 1:3].rearrange("p a n -> p (a n)"))
                    pool.drain()
                    nc.gpsimd.tensor_copy(long_off[:], long_meta[:])
                    with pool.Fori(c0, c1) as c:
                        pool.drain()
                        nc.gpsimd.tensor_scalar(long_off[:, 0:1], long_off[:, 0:1], float(E), None, ALU.min)
                        pool.drain()
                        nc.gpsimd.tensor_copy(long_idx[:], long_off[:, 0:1])
                        pool.drain()
                        pool.indirect_dma_start(out=long_raw[:], out_offset=None, in_=src.rearrange("(a e) -> a e", a=1),
                                                in_offset=bass.IndirectOffsetOnAxis(ap=long_idx[:, 0:1], axis=1)).then_inc(s_longrun, 16)
                        pool.wait_ge(s_longrun, c * 16 + 16)
                        nc.gpsimd.tensor_tensor(long_raw[:], long_raw[:], long_dummy[:], ALU.subtract)
                        pool.drain()
                        nc.gpsimd.tensor_copy(run_f[:, 0:SLOTS], long_raw[:])
                        nc.gpsimd.tensor_scalar(run_m[:, 0:SLOTS], iota[:, 0:SLOTS], long_off[:, 1:2], None, ALU.is_lt)
                        pool.drain()
                        nc.gpsimd.tensor_tensor(run_f[:, 0:SLOTS], run_f[:, 0:SLOTS], run_m[:, 0:SLOTS], ALU.mult)
                        pool.drain()
                        nc.gpsimd.tensor_scalar(long_raw[:], run_f[:, 0:SLOTS], float(DUMMY), None, ALU.add)
                        pool.drain()
                        pool.dma_start(slot_tab[:, bass.ds(c * SLOTS, SLOTS)], long_raw[:]).then_inc(s_longst, 16)
                        nc.gpsimd.tensor_scalar(long_off[:, 0:1], long_off[:, 0:1], float(SLOTS), None, ALU.add)
                        nc.gpsimd.tensor_scalar(long_off[:, 1:2], long_off[:, 1:2], float(-SLOTS), None, ALU.add)
                        pool.wait_ge(s_longst, c * 16 + 16)
            pool.drain().then_inc(s_long, 1)

            pool.wait_ge(s_dummy, 16 * (LAYERS + 4))
            total = all_units(pool)
            bodies = total // UNITS
            for r in range(LAYERS + 2):
                table = hidden_tab[r] if r < LAYERS else gat_tab[r - LAYERS]
                width = H if r < LAYERS else GW
                with pool.Fori(bodies * r, bodies * (r + 1)) as i:
                    for b in range(RING):
                        if b % (RING // 2) == 0:
                            pool.wait_ge(staged[b * 2 // RING], i * 16 + 16)
                            pool.sem_inc(half_begun, 1)
                        if b % SLOTS == SLOTS // 2:
                            pool.wait_ge(ring_free, i * UNITS + (b // SLOTS + 2))
                            pool.wait_ge(gathered[(b // SLOTS - 1) % UNITS], i * (16 * SLOTS) + 16 * SLOTS)
                            pool.sem_inc(arrived, 1)
                        pool.indirect_dma_start(out=ring[:, b, 0:width], out_offset=None, in_=table,
                                                in_offset=bass.IndirectOffsetOnAxis(ap=stage[:, b * 2 // RING, b % (RING // 2):b % (RING // 2) + 1], axis=0))\
                            .then_inc(gathered[b // SLOTS], 16)
                pool.wait_ge(gathered[UNITS - 1], bodies * (16 * SLOTS * (r + 1)) + 16 * SLOTS)
                pool.sem_inc(arrived, 1)
                pool.sem_inc(round_gathered, 1)
                if r == LAYERS - 1:
                    for g in range(GROUPS):
                        pool.indirect_dma_start(out=x_res[:, g, :], out_offset=None, in_=x,
                                                in_offset=bass.IndirectOffsetOnAxis(ap=perm[:, g, 0:1], axis=0)).then_inc(s_xperm, 16)
                for g in range(GROUPS):
                    ids = bass.IndirectOffsetOnAxis(ap=perm[:, g, 0:1], axis=0)
                    if r < LAYERS - 1:
                        pool.wait_ge(h_done, r * GROUPS + g + 1)
                        pool.indirect_dma_start(out=hidden_tab[r + 1], out_offset=ids, in_=h_res[:, g, :], in_offset=None)\
                            .then_inc(table_done, 16)
                    elif r < LAYERS + 1:
                        pool.wait_ge(row_done, (r - LAYERS + 1) * GROUPS + g + 1)
                        pool.indirect_dma_start(out=gat_tab[r - LAYERS + 1], out_offset=ids, in_=gat_rows[:, g, :], in_offset=None)\
                            .then_inc(table_done, 16)
                    else:
                        pool.wait_ge(z_done, g + 1)
                        pool.indirect_dma_start(out=out, out_offset=ids, in_=x_res[:, g, :], in_offset=None)\
                            .then_inc(s_out, 16)
                if r < LAYERS + 1:
                    pool.wait_ge(table_done, 16 * GROUPS * (r + 1))

        @block.vector
        def _(dve):
            dve.sem_inc(ring_free, UNITS)
            nc.vector.memset(zeros[:], 0.0)
            nc.vector.memset(slots_sb, DUMMY)
            dve.wait_ge(s_ints, 16)
            dve.wait_ge(s_const, 1)
            nc.vector.tensor_scalar(lo_i, dst_i[:], 127, None, ALU.bitwise_and)
            nc.vector.tensor_scalar(dst_i[:], dst_i[:], 7, None, ALU.logical_shift_right)
            dve.drain()
            nc.vector.tensor_copy(lo_b, lo_i)
            nc.vector.tensor_copy(hi_b, dst_i[:])
            dve.drain()
            dve.sem_inc(s_1h_used, 2)
            with dve.Fori(0, ET // (4 * HIST)) as i:
                for step in range(4):
                    half = step % 2
                    dve.wait_ge(s_1h_used, i * 4 + (step + 1))
                    at = bass.ds(i * 4 * HIST + step * HIST, HIST)
                    nc.vector.tensor_tensor(lo1h[:, half, :, :], iota_b[:].unsqueeze(1).to_broadcast([P, HIST, P]),
                                            lo_b[:, at].unsqueeze(2).to_broadcast([P, HIST, P]), ALU.is_equal)
                    last = nc.vector.tensor_tensor(hi1h[:, half, :, :], iota_b[:, 0:GROUPS].unsqueeze(1).to_broadcast([P, HIST, GROUPS]),
                                                   hi_b[:, at].unsqueeze(2).to_broadcast([P, HIST, GROUPS]), ALU.is_equal)
                    last.then_inc(s_1h, 1)
            dve.wait_ge(s_hist, 1)
            nc.vector.tensor_copy(hist[:, 0, :], ps_sum[0:GROUPS, 0:P])
            dve.drain()
            nc.vector.tensor_tensor_scan(hist[:, 1, :], hist[:, 0, :], zeros[0:GROUPS, :], 0.0, ALU.add, ALU.add)
            dve.drain().then_inc(s_tot, 1)
            dve.wait_ge(s_pre, 1)
            nc.vector.tensor_copy(row_pre[:], ps_sum[0:GROUPS, 256:257])
            dve.drain()
            nc.vector.scalar_tensor_tensor(hist[:, 2, :], hist[:, 1, :], row_pre[:], hist[:, 0, :], ALU.add, ALU.subtract)
            dve.drain().then_inc(s_off, 1)
            dve.wait_ge(s_offT, 1)
            nc.vector.tensor_copy(deg_n[:], ps_tr[:, 0:GROUPS])
            nc.vector.tensor_copy(off_n[:], ps_tr[:, P:P + GROUPS])
            dve.drain()
            nc.vector.tensor_scalar(bucket[:], deg_n[:], float(P - 1), None, ALU.min)
            dve.drain()
            nc.vector.tensor_tensor(bucket1h, iota_b[:].unsqueeze(1).to_broadcast([P, GROUPS, P]),
                                    bucket[:].unsqueeze(2).to_broadcast([P, GROUPS, P]), ALU.is_equal).then_inc(s_bkt, 1)
            dve.wait_ge(s_bsum, 1)
            nc.vector.tensor_copy(bkt_count[:], ps_sum[:, 0:GROUPS])
            dve.drain()
            nc.vector.tensor_tensor_scan(bkt_sum[:], bkt_count[:], zeros[:, 0:GROUPS], 0.0, ALU.add, ALU.add)
            dve.drain().then_inc(s_bscan, 1)
            dve.wait_ge(s_below, 1)
            nc.vector.tensor_tensor(bkt_first[:], ps_sum[:, 128:129], bkt_sum[:, GROUPS - 1:GROUPS], ALU.add)
            dve.drain()
            nc.vector.tensor_scalar(bkt_first[:], bkt_first[:], -1.0, float(NP), ALU.mult, ALU.add)
            dve.drain()
            nc.vector.scalar_tensor_tensor(bkt_base[:], bkt_sum[:], bkt_first[:], bkt_count[:], ALU.add, ALU.subtract)
            dve.drain().then_inc(s_base, 1)
            for g in range(0, GROUPS, BATCH):
                n = min(BATCH, GROUPS - g)
                own = (ps_gate, ps_moe)[g // BATCH % 2][:, 0:n * P].rearrange("p (a b) -> p a b", b=P)
                dve.wait_ge(s_own, g + n)
                dve.drain()
                nc.vector.tensor_tensor(sort_tmp[:, 0:n, :], own, bucket1h[:, g:g + n, :], ALU.mult).then_inc(s_rank, n)
                dve.drain()
                nc.vector.tensor_reduce(rank[:, g:g + n], sort_tmp[:, 0:n, :], AX.X, ALU.add)
            dve.drain()
            nc.vector.tensor_copy(rank_i[:, 0, :], rank[:])
            dve.drain()
            nc.vector.tensor_scalar(rank_i[:, 1, :], rank_i[:, 0, :], P - 1, None, ALU.bitwise_and)
            nc.vector.tensor_scalar(rank_i[:, 0, :], rank_i[:, 0, :], 7, None, ALU.logical_shift_right)
            dve.drain()
            nc.vector.tensor_scalar(rank_i[:, 0, :], rank_i[:, 0, :], 1.0, float(STRIDE), ALU.add, ALU.mult)
            nc.vector.tensor_scalar(rank_i[:, 1, :], rank_i[:, 1, :], float(GROUPS), None, ALU.mult)
            dve.drain()
            nc.vector.tensor_scalar(rank_i[:, 2, :], rank_i[:, 0, :], float(-(-(1 << 16) // GROUPS)), None, ALU.mult)
            dve.drain()
            nc.vector.tensor_scalar(rank_i[:, 2, :], rank_i[:, 2, :], 16, None, ALU.logical_shift_right)
            dve.drain()
            nc.vector.scalar_tensor_tensor(rank_i[:, 0, :], rank_i[:, 2, :], float(-GROUPS), rank_i[:, 0, :], ALU.mult, ALU.add)
            dve.drain()
            nc.vector.tensor_tensor(rank_i[:, 2, :], rank_i[:, 0, :], rank_i[:, 1, :], ALU.add)
            nc.vector.tensor_copy(meta[:, :, 1], off_n[:])
            nc.vector.tensor_copy(meta[:, :, 2], deg_n[:])
            dve.drain().then_inc(s_meta, 1)
            runs = run_m.rearrange("p (g k) -> p g k", k=RUN)
            places = iota[:, 0:RUN].unsqueeze(1).to_broadcast([P, GROUPS, RUN])

            def each(a):
                return a.unsqueeze(2).to_broadcast([P, GROUPS, RUN])

            dve.wait_ge(s_perm, 16)
            nc.vector.tensor_copy(deg_p[:], perm[:, :, 2])
            nc.vector.tensor_copy(node, perm[:, :, 0])
            dve.drain()
            nc.vector.tensor_scalar(rdeg[:], deg_p[:], 1.0, None, ALU.max)
            nc.vector.tensor_scalar(last_at, deg_p[:], -1.0, None, ALU.add)
            nc.vector.tensor_scalar(loop_on[:], node, float(LOOPS), None, ALU.is_lt)
            dve.drain()
            nc.vector.reciprocal(rdeg[:], rdeg[:])
            nc.vector.tensor_scalar(node, node, float(-DUMMY), None, ALU.add)
            dve.wait_ge(s_h0s, GROUPS)
            nc.vector.tensor_tensor(runs, places, each(last_at), ALU.is_equal)
            dve.wait_ge(gathered[UNITS - 1], 16 * SLOTS)
            dve.wait_ge(s_runs, 16 * (GROUPS - SLOTS))
            nc.vector.tensor_scalar(run_f, run_raw.rearrange("p g k -> p (g k)"), float(-DUMMY), None, ALU.add)
            dve.drain()
            nc.vector.tensor_tensor(run_m, run_m, run_f, ALU.mult)
            dve.drain()
            nc.vector.tensor_reduce(last_at, runs, AX.X, ALU.add)
            dve.drain()
            nc.vector.tensor_tensor(self_on[:], last_at, node, ALU.is_equal)
            dve.drain()
            nc.vector.tensor_tensor(deg_p[:], deg_p[:], self_on[:], ALU.subtract)
            nc.vector.tensor_tensor(loop_on[:], loop_on[:], self_on[:], ALU.add)
            dve.drain().then_inc(s_degp, 1)
            nc.vector.tensor_tensor(runs, places, each(deg_p[:]), ALU.is_lt)
            nc.vector.tensor_copy(perm[:, :, 2], deg_p[:])
            nc.vector.tensor_scalar(loop_cap[:], loop_on[:], 0.0, None, ALU.is_gt)
            dve.drain()
            nc.vector.tensor_scalar(loop_cap[:], loop_cap[:], -0.5, -2.0 * LOWEST, ALU.add, ALU.mult)
            dve.wait_ge(s_degT, 1)
            nc.vector.tensor_reduce(kmax[:], ps_tr[0:GROUPS, 256:384], AX.X, ALU.max)
            dve.drain()
            nc.vector.tensor_scalar(kmax_i[:], kmax[:], float(SLOTS + 1), float(SLOTS - 1), ALU.max, ALU.add)
            dve.drain()
            nc.vector.tensor_scalar(kmax_i[:], kmax_i[:], SLOTS.bit_length() - 1, None, ALU.logical_shift_right)
            dve.drain()
            nc.vector.tensor_copy(kmax[:], kmax_i[:])
            dve.drain().then_inc(s_kmax, 1)
            dve.wait_ge(s_cumP, 1)
            nc.vector.tensor_copy(cum_f[:, 0:GROUPS + 1], ps_sum[0:1, 128:128 + GROUPS + 1])
            nc.vector.tensor_reduce(cum_f[:, GROUPS + 1:GROUPS + 2], ps_sum[0:1, 256:256 + GROUPS], AX.X, ALU.max)
            dve.drain()
            nc.vector.tensor_copy(cum[:], cum_f[:])
            nc.vector.tensor_scalar(cum_at[:], cum_f[:], float(SLOTS), float(COLS - RUN), ALU.mult, ALU.min)
            dve.drain()
            nc.vector.tensor_copy(cum_full[:, 0:GROUPS], cum[:, 0:GROUPS])
            nc.vector.tensor_scalar(cum_full[:, GROUPS:GROUPS + 1], cum_f[:, GROUPS:GROUPS + 1], float(UNITS), None, ALU.add)
            dve.drain()
            nc.vector.tensor_scalar(cum_full[:, GROUPS:GROUPS + 1], cum_full[:, GROUPS:GROUPS + 1], UNITS.bit_length() - 1,
                                    UNITS.bit_length() - 1, ALU.logical_shift_right, ALU.logical_shift_left)
            dve.drain().then_inc(s_cum, 1)
            nc.vector.tensor_tensor(run_f, run_f, run_m, ALU.mult)
            dve.drain()
            nc.vector.tensor_scalar(run_raw.rearrange("p g k -> p (g k)"), run_f, float(DUMMY), None, ALU.add)
            dve.drain().then_inc(s_compact, 1)

            def compact(g):
                at = dve.value_load(cum_at[0:1, bass.ds(g, 1)], min_val=0, max_val=COLS - RUN)
                dve.wait_ge(s_compact, g + 1)
                nc.vector.tensor_scalar(slots_sb[:, bass.ds(at, RUN)], run_raw[:, bass.ds(g, 1), :].rearrange("p a k -> p (a k)"),
                                        0.0, None, ALU.add).then_inc(s_compact, 1)

            with dve.Fori(0, GROUPS // 2) as i:
                compact(i * 2)
            compact(GROUPS - 1)
            dve.drain().then_inc(s_slots, 1)

            total = all_units(dve)

            real = dve.value_load(cum[0:1, GROUPS:GROUPS + 1], min_val=2, max_val=UMAX)

            def fill_up(r, *counts):
                with dve.Fori(total * r + real, total * (r + 1)) as q:
                    dve.wait_ge(arrived, q + (r + 2))
                    dve.sem_inc(ring_free, 1)
                    for c in counts:
                        dve.sem_inc(c, 1)

            def aggregate(r, g):
                n = g + r * GROUPS
                c0, c1 = units_of(dve, g)
                dve.drain()
                nc.vector.tensor_scalar(acc, h_res[:, bass.ds(g, 1), :].rearrange("p a n -> p (a n)"), self_on[:, bass.ds(g, 1)], None, ALU.mult)
                with dve.Fori(total * r + c0, total * r + c1) as q:
                    dve.drain()
                    dve.wait_ge(arrived, q + (r + 2))
                    nc.vector.tensor_reduce(part[:], ring[:, bass.ds((q % UNITS) * SLOTS, SLOTS), :].rearrange("p s n -> p n s"),
                                            AX.X, ALU.add).then_inc(ring_free, 1)
                    dve.drain()
                    nc.vector.tensor_tensor(acc, acc, part[:], ALU.add)
                dve.drain()
                w(dve, opT_ready, n)
                nc.vector.tensor_scalar(agg[:], acc, rdeg[:, bass.ds(g, 1)], None, ALU.mult).then_inc(agg_ready, 1)

            def gate_experts(r, g, odd):
                n = g + r * GROUPS
                dve.wait_ge(bcast_ready, n + 1)
                for s in range(NS):
                    dve.wait_ge(relu_ready, n * NS + (s + 1))
                    nc.vector.tensor_tensor(strong[odd][:, s, :, :], strong[odd][:, s, :, :],
                                            ps_gate[:, s * P:(s + 1) * P].unsqueeze(1).to_broadcast([P, 4, P]), ALU.mult).then_inc(gated, 1)
                dve.wait_ge(weak_copied, n + 1)
                nc.vector.tensor_reduce(part[:], weak[:].rearrange("p e n -> p n e"), AX.X, ALU.add).then_inc(weak_added, 1)
                dve.drain()
                hg = h_res[:, bass.ds(g, 1), :].rearrange("p a n -> p (a n)")
                nc.vector.tensor_tensor(hg, hg, part[:], ALU.add)

            def add_strong(r, g):
                dve.drain()
                dve.wait_ge(w2_ready, g + (r * GROUPS + 1))
                hg = h_res[:, bass.ds(g, 1), :].rearrange("p a n -> p (a n)")
                nc.vector.tensor_tensor(hg, hg, ps_moe[:, 0:H], ALU.add).then_inc(h_done, 1)

            def choose(r, g):
                n = g + r * GROUPS
                dve.wait_ge(logits_copied, n + 1)
                nc.vector.tensor_scalar(ex_in[:, 1:2], logit[:, NE:NE + 1], -1.0, None, ALU.mult)
                nc.vector.max(top[:], logit[:, 0:NE])
                dve.drain()
                nc.vector.max_index(top_at[:], top[:], logit[:, 0:NE])
                nc.vector.tensor_tensor(ex_in[:, 0:1], top[:, 1:2], top[:, 0:1], ALU.subtract)
                dve.drain().then_inc(top_ready, 1)
                nc.vector.tensor_copy(top_f[:], top_at[:, 0:2])
                dve.drain()
                dve.wait_ge(exp_ready, n + 1)
                nc.vector.tensor_scalar(gate_n[:, 0:2], ex[:], 1.0, None, ALU.add)
                dve.drain()
                nc.vector.reciprocal(gate_n[:, 0:2], gate_n[:, 0:2])
                dve.drain()
                nc.vector.tensor_tensor(gate_n[:, 2:3], gate_n[:, 0:1], gate_n[:, 1:2], ALU.mult)
                dve.drain()
                nc.vector.tensor_tensor(gate_n[:, 3:4], gate_n[:, 2:3], ex[:, 0:1], ALU.mult)
                dve.drain()
                for k in range(2):
                    nc.vector.tensor_scalar(gate_ab[:, k, :], iota[:, 0:NE], top_f[:, k:k + 1], gate_n[:, 2 + k:3 + k], ALU.is_equal, ALU.mult)
                dve.drain()
                nc.vector.tensor_tensor(gates[:], gate_ab[:, 0, :], gate_ab[:, 1, :], ALU.add).then_inc(gates_ready, 1)

            dve.wait_ge(s_hperm, 16 * GROUPS)
            for r in range(LAYERS):
                def step(g, odd):
                    aggregate(r, g)
                    gate_experts(r, g - 2, odd)
                    choose(r, g - 1)
                    add_strong(r, g - 3)

                aggregate(r, 0)
                aggregate(r, 1)
                choose(r, 0)
                aggregate(r, 2)
                gate_experts(r, 0, 0)
                choose(r, 1)
                with dve.Fori(0, (GROUPS - 3) // 2) as i:
                    step(i * 2 + 3, 1)
                    step(i * 2 + 4, 0)
                gate_experts(r, GROUPS - 2, 1)
                choose(r, GROUPS - 1)
                add_strong(r, GROUPS - 3)
                gate_experts(r, GROUPS - 1, 0)
                add_strong(r, GROUPS - 2)
                add_strong(r, GROUPS - 1)
                fill_up(r)

            def moments(g):
                dve.drain()
                nc.vector.bn_stats(ln_st[:, 0, :], x_res[:, bass.ds(g, 1), :].rearrange("p a n -> p (a n)"))
                dve.drain()
                nc.vector.bn_aggr(ln_of[:, 0, :], ln_st[:, 0, :])
                dve.drain()
                nc.vector.tensor_copy(ln_mv[:, bass.ds(g, 1), :].rearrange("p a n -> p (a n)"), ln_of[:, 0, :])

            def all_rstd(count):
                dve.drain()
                nc.vector.tensor_scalar(ln_r[:, 0, :], ln_mv[:, :, 1], EPS_LN, None, ALU.add).then_inc(var_ready, 1)
                dve.wait_ge(rstd_ready, count)

            nc.vector.memset(gat_rows, 1.0).then_inc(ones_set, 1)
            dve.wait_ge(s_xperm, 16 * GROUPS)

            def residual(g, count):
                for k in range(count):
                    dve.wait_ge(b_out_ready, g + (k + 1))
                    xg = x_res[:, bass.ds(g + k, 1), :].rearrange("p a n -> p (a n)")
                    nc.vector.tensor_tensor(xg, ps_weak[k][:, 0:IN], xg, ALU.add).then_inc(z_ready, 1)
                dve.drain()
                for k in range(count):
                    nc.vector.bn_stats(ln_st[:, k, :], x_res[:, bass.ds(g + k, 1), :].rearrange("p a n -> p (a n)"))
                dve.drain()
                for k in range(count):
                    nc.vector.bn_aggr(ln_of[:, k, :], ln_st[:, k, :])
                dve.drain()
                nc.vector.tensor_copy(ln_mv[:, bass.ds(g, count), :], ln_of[:, 0:count, :])

            with dve.Fori(0, GROUPS // 2) as i:
                residual(i * 2, 2)
            residual(GROUPS - 1, 1)
            all_rstd(1)

            def normalize(g, odd):
                xg = x_res[:, bass.ds(g, 1), :].rearrange("p a n -> p (a n)")
                return nc.vector.tensor_scalar(xg, xg, ln_mv[:, bass.ds(g, 1), 0:1].rearrange("p a n -> p (a n)"),
                                               ln_r[:, 2, bass.ds(g, 1)], ALU.subtract, ALU.mult)

            def x1_row(g, odd, before):
                if before:
                    dve.wait_ge(x1T_ready, g - 1)
                normalize(g, odd)
                dve.drain()
                nc.vector.tensor_copy(x1[odd][:], x_res[:, bass.ds(g, 1), :].rearrange("p a n -> p (a n)")).then_inc(x1_ready, 1)

            x1_row(0, 0, False)
            x1_row(1, 1, False)
            with dve.Fori(1, GROUPS // 2) as i:
                x1_row(i * 2, 0, True)
                x1_row(i * 2 + 1, 1, True)
            x1_row(GROUPS - 1, 0, True)

            for k in range(2):
                r = LAYERS + k

                def rows_of(unit):
                    return ring[:, bass.ds(unit % UNITS * SLOTS, SLOTS), 0:GW]

                def score_unit(q):
                    dve.wait_ge(arrived, total * LAYERS + q + (r + 2))
                    nc.vector.tensor_tensor(score[:, 0:SLOTS, :], rows_of(q)[:, :, GW - HEADS:GW],
                                            ad_cur[:].unsqueeze(1).to_broadcast([P, SLOTS, HEADS]), ALU.add)

                def leaky():
                    nc.vector.scalar_tensor_tensor(score[:, 0:SLOTS, :], score[:, 0:SLOTS, :], 0.2, score[:, 0:SLOTS, :], ALU.mult, ALU.max)

                def highest():
                    nc.vector.tensor_reduce(m_new[:], score[:].rearrange("p s h -> p h s"), AX.X, ALU.max)

                def shift():
                    nc.vector.tensor_tensor(shifted[:], score[:], m_new[:].unsqueeze(1).to_broadcast([P, SLOTS + 1, HEADS]), ALU.subtract)
                    dve.drain().then_inc(shift_ready, 1)
                    nc.vector.tensor_copy(score[:, SLOTS, :], m_new[:])

                def weigh(count, unit):
                    p = ps_gate[:, 0:(SLOTS + 1) * HEADS].rearrange("p (s h) -> p s h", h=HEADS)
                    dve.wait_ge(p_ready, count)
                    nc.vector.tensor_tensor(terms[:, SLOTS, :, :], gacc[:], p[:, SLOTS, :].unsqueeze(2).to_broadcast([P, HEADS, HC]), ALU.mult)
                    nc.vector.tensor_tensor(terms[:, 0:SLOTS, :, :], rows_of(unit)[:, :, 0:HEADS * HC].rearrange("p s (h c) -> p s h c", c=HC),
                                            p[:, 0:SLOTS, :].unsqueeze(3).to_broadcast([P, SLOTS, HEADS, HC]), ALU.mult).then_inc(ring_free, 1)

                def add_up():
                    nc.vector.tensor_reduce(gacc[:].rearrange("p h c -> p (h c)"), terms[:].rearrange("p s h c -> p (h c) s"), AX.X, ALU.add)

                def turn(done, g):
                    ends, begins = done is not None, g is not None
                    if begins:
                        c0, c1 = units_of(dve, g)
                        own = gat_rows[:, bass.ds(g, 1), :].rearrange("p a n -> p (a n)")
                        target = ad[k][:, bass.ds(g, 1), :].rearrange("p a n -> p (a n)")
                        dve.wait_ge(row_done, g + (k * GROUPS + 1))
                        nc.vector.tensor_tensor(m_new[:], own[:, GW - HEADS:GW], target, ALU.add)
                        nc.vector.tensor_copy(ad_cur[:], target)
                    dve.drain()
                    if ends:
                        nc.vector.tensor_scalar(rden[:], gacc[:, :, HID], EPS_GAT, None, ALU.add)
                    if begins:
                        nc.vector.scalar_tensor_tensor(m_new[:], m_new[:], 0.2, m_new[:], ALU.mult, ALU.max)
                    dve.drain()
                    if ends:
                        nc.vector.reciprocal(rden[:], rden[:])
                    if begins:
                        nc.vector.tensor_scalar(score[:, SLOTS, :], m_new[:], loop_cap[:, bass.ds(g, 1)], None, ALU.min)
                        score_unit(total * k + c0)
                    dve.drain()
                    if ends:
                        nc.vector.tensor_tensor(y[:].rearrange("p (h c) -> p h c", c=HID), gacc[:, :, 0:HID],
                                                rden[:].unsqueeze(2).to_broadcast([P, HEADS, HID]), ALU.mult)
                    if begins:
                        leaky()
                    dve.drain()
                    if ends:
                        nc.vector.tensor_tensor(y[:], y[:], gat_b[k][:], ALU.add)
                    if begins:
                        highest()
                        nc.vector.tensor_scalar(gacc[:].rearrange("p h c -> p (h c)"), own[:, 0:HEADS * HC], loop_on[:, bass.ds(g, 1)], None, ALU.mult)
                    dve.drain()
                    if ends and k == 0:
                        nc.vector.tensor_scalar(y_neg[:], y[:], 0.0, None, ALU.min).then_inc(neg_ready, 1)
                        nc.vector.tensor_scalar(y[:], y[:], 0.0, -1.0, ALU.max, ALU.add)
                    elif ends:
                        xg = x_res[:, bass.ds(done, 1), :].rearrange("p a n -> p (a n)")
                        nc.vector.tensor_tensor(xg, y[:], xg, ALU.add)
                    if begins:
                        shift()
                    if ends and k == 0:
                        dve.drain()
                        dve.wait_ge(nexp_ready, done + 1)
                        dve.wait_ge(x1T_ready, done + GROUPS)
                        nc.vector.tensor_tensor(x1[0][:], y[:], y_exp[:], ALU.add).then_inc(x1_ready, 1)
                    elif ends:
                        moments(done)
                    return (c0, c1) if begins else None

                def units(c0, c1):
                    with dve.Fori(total * k + c0 + 1, total * k + c1) as q:
                        score_unit(q)
                        weigh(q, q + (UNITS - 1))
                        dve.drain()
                        leaky()
                        add_up()
                        dve.drain()
                        highest()
                        dve.drain()
                        shift()
                    weigh(total * k + c1, total * k + c1 + (UNITS - 1))
                    dve.drain()
                    add_up()

                units(*turn(None, 0))
                with dve.Fori(0, GROUPS - 1) as i:
                    units(*turn(i, i + 1))
                turn(GROUPS - 1, None)
                fill_up(r, shift_ready, p_ready)
            all_rstd(2)
            with dve.Fori(0, GROUPS) as g:
                normalize(g, 0).then_inc(z_done, 1)

        @block.scalar
        def _(act):
            act.wait_ge(s_prepP, 1)
            nc.scalar.activation(b1_t[:], ps_weak[0][:, 0:LAYERS * NS * 4], ACT.Copy)
            act.drain().then_inc(s_prepP, 1)
            for k in range(2):
                act.wait_ge(s_prepP, 3 + 4 * k)
                nc.scalar.activation(gat_wt[:], ps_weak[0][:, 128:256], ACT.Copy)
                act.drain().then_inc(s_prepP, 1)
                act.wait_ge(s_prepP, 5 + 4 * k)
                nc.scalar.activation(gat_w[k][:, P:P + 2 * HEADS], ps_weak[1][:, 0:2 * HEADS], ACT.Copy)
                act.drain().then_inc(s_prepP, 1)

            act.wait_ge(s_xin, 16)
            with act.Fori(0, GROUPS) as g:
                nc.scalar.activation(x1[0][:], x_res[:, bass.ds(g, 1), :].rearrange("p a n -> p (a n)"), ACT.Copy).then_inc(s_xc, 1)
                act.wait_ge(s_xT, g + 1)
                nc.scalar.activation(x1_t[0][:], ps_w1[0][:, 0:P], ACT.Copy).then_inc(s_xTs, 1)
                act.wait_ge(s_h0, g + 1)
                nc.scalar.activation(h_res[:, bass.ds(g, 1), :].rearrange("p a n -> p (a n)"), ps_w1[1][:, 0:H], ACT.Copy).then_inc(s_h0s, 1)

            act.wait_ge(s_cum, 1)
            with act.Fori(0, GROUPS // 2) as i:
                at = act.value_load(cum_at[0:1, bass.ds(i * 2 + 1, 1)], min_val=0, max_val=COLS - RUN)
                act.wait_ge(s_compact, i * 2 + 2)
                nc.scalar.activation(slots_sb[:, bass.ds(at, RUN)], run_raw[:, bass.ds(i * 2 + 1, 1), :].rearrange("p a k -> p (a k)"),
                                     ACT.Copy).then_inc(s_compact, 1)

            def operands(r, g, odd):
                n = g + r * GROUPS
                if r == 0:
                    act.wait_ge(s_hperm, 16 * GROUPS)
                else:
                    act.wait_ge(h_done, g + ((r - 1) * GROUPS + 1))
                w(act, opT_ready, n)
                nc.scalar.activation(h_cur[0][:], h_res[:, bass.ds(g, 1), :].rearrange("p a n -> p (a n)"), ACT.Copy).then_inc(hcur_ready, 1)
                act.wait_ge(opT_ready, n + 1)
                w(act, logits_ready, n)
                nc.scalar.activation(h_t[0][:], ps_tr[:, 0:H], ACT.Copy)
                w(act, weak_ready, n - 1)
                nc.scalar.activation(agg_t[odd][:], ps_tr[:, H:2 * H], ACT.Copy).then_inc(opT_copied, 1)

            def logits(r, g):
                act.wait_ge(logits_ready, g + (r * GROUPS + 1))
                nc.scalar.activation(logit[:], ps_moe[:, H:H + NE + 1], ACT.Copy).then_inc(logits_copied, 1)

            def gate_exp(r, g):
                act.wait_ge(top_ready, g + (r * GROUPS + 1))
                nc.scalar.activation(ex[:], ex_in[:], ACT.Exp).then_inc(exp_ready, 1)

            def relu(r, g, odd, experts):
                n = g + r * GROUPS
                w(act, w2_ready, n - 1)
                for s in experts:
                    act.wait_ge(w1_ready, n * NS + (s + 1))
                    for c in range(4):
                        j = (r * NS + s) * 4 + c
                        last = nc.scalar.activation(strong[odd][:, s, c, :], ps_w1[s % 2][:, c * P:(c + 1) * P], ACT.Relu, bias=b1_t[:, j:j + 1])
                    last.then_inc(relu_ready, 1)

            def weak_relu(r, g, odd):
                n = g + r * GROUPS
                act.wait_ge(gatesT_ready, n + 1)
                w(act, w2_ready, n - 1)
                nc.scalar.activation(gates_t[odd][:], ps_moe[0:NE, 384:512], ACT.Copy).then_inc(gatesT_copied, 1)
                act.wait_ge(weak_ready, n + 1)
                act.wait_ge(gates_ready, n + 1)
                w(act, weak_added, n)
                for e in range(NW):
                    last = nc.scalar.activation(weak[:, e, :], ps_weak[e // 2][:, (e % 2) * H:(e % 2 + 1) * H], ACT.Relu, scale=gates[:, e:e + 1])
                last.then_inc(weak_copied, 1)

            for r in range(LAYERS):
                def step(g, odd):
                    operands(r, g, odd)
                    relu(r, g - 1, 1 - odd, (0, 1))
                    gate_exp(r, g - 1)
                    relu(r, g - 1, 1 - odd, (2, 3))
                    logits(r, g)
                    weak_relu(r, g - 1, 1 - odd)

                operands(r, 0, 0)
                logits(r, 0)
                relu(r, 0, 0, range(NS))
                operands(r, 1, 1)
                gate_exp(r, 0)
                logits(r, 1)
                weak_relu(r, 0, 0)
                relu(r, 1, 1, range(NS))
                operands(r, 2, 0)
                gate_exp(r, 1)
                logits(r, 2)
                weak_relu(r, 1, 1)
                with act.Fori(0, (GROUPS - 3) // 2) as i:
                    step(i * 2 + 3, 1)
                    step(i * 2 + 4, 0)
                gate_exp(r, GROUPS - 1)
                relu(r, GROUPS - 1, 0, range(NS))
                weak_relu(r, GROUPS - 1, 0)

            def state(g, odd, before):
                act.wait_ge(h_done, g + (LAYERS - 1) * GROUPS + 1)
                if before:
                    act.wait_ge(houtT_ready, g - 1)
                nc.scalar.activation(h_cur[odd][:], h_res[:, bass.ds(g, 1), :].rearrange("p a n -> p (a n)"), ACT.Copy).then_inc(hout_ready, 1)

            def state_t(g, odd):
                act.wait_ge(houtT_ready, g + 1)
                nc.scalar.activation(h_t[odd][:], ps_w1[odd][:, 0:H], ACT.Copy).then_inc(houtT_copied, 1)

            state(0, 0, False)
            state(1, 1, False)
            state_t(0, 0)
            with act.Fori(1, GROUPS // 2) as i:
                state(i * 2, 0, True)
                state_t(i * 2 - 1, 1)
                state(i * 2 + 1, 1, True)
                state_t(i * 2, 0)
            state(GROUPS - 1, 0, True)
            state_t(GROUPS - 2, 1)
            state_t(GROUPS - 1, 0)

            def all_rstd(count):
                act.wait_ge(var_ready, count)
                nc.scalar.activation(ln_r[:, 1, :], ln_r[:, 0, :], ACT.Ln)
                act.drain()
                nc.scalar.activation(ln_r[:, 2, :], ln_r[:, 1, :], ACT.Exp, scale=-0.5).then_inc(rstd_ready, 1)

            all_rstd(1)

            def table_operand(k, g, odd):
                act.wait_ge(x1T_ready, g + (k * GROUPS + 1))
                nc.scalar.activation(x1_t[odd][:], ps_w1[odd][:, 0:P], ACT.Copy).then_inc(x1T_copied, 1)

            def table_row(k, g, odd):
                act.wait_ge(row_ready, g + (k * GROUPS + 1))
                row = gat_rows[:, bass.ds(g, 1), :].rearrange("p a n -> p (a n)")
                nc.scalar.activation(row[:, 0:HEADS * HC].rearrange("p (h c) -> p h c", c=HC)[:, :, 0:HID],
                                     ps_weak[odd][:, 0:P].rearrange("p (h c) -> p h c", c=HID), ACT.Copy)
                nc.scalar.activation(row[:, GW - HEADS:GW], ps_weak[odd][:, P:P + HEADS], ACT.Copy)
                nc.scalar.activation(ad[k][:, bass.ds(g, 1), :].rearrange("p a n -> p (a n)"), ps_weak[odd][:, P + HEADS:P + 2 * HEADS], ACT.Copy)
                act.drain().then_inc(row_done, 1)

            act.wait_ge(ones_set, 1)
            table_operand(0, 0, 0)
            with act.Fori(0, GROUPS // 2) as i:
                table_operand(0, i * 2 + 1, 1)
                table_row(0, i * 2, 0)
                table_operand(0, i * 2 + 2, 0)
                table_row(0, i * 2 + 1, 1)
            table_row(0, GROUPS - 1, 0)

            total = all_units(act)

            def weights(k, g):
                c0, c1 = units_of(act, g)
                with act.Fori(total * k + c0, total * k + c1) as q:
                    act.wait_ge(shift_ready, q + 1)
                    nc.scalar.activation(ps_gate[:, 0:(SLOTS + 1) * HEADS], shifted[:].rearrange("p s h -> p (s h)"), ACT.Exp).then_inc(p_ready, 1)

            def elu_exp(g):
                act.wait_ge(neg_ready, g + 1)
                nc.scalar.activation(y_exp[:], y_neg[:], ACT.Exp).then_inc(nexp_ready, 1)

            weights(0, 0)
            elu_exp(0)
            weights(0, 1)
            table_operand(1, 0, 0)
            act.wait_ge(table_done, 16 * GROUPS * LAYERS)
            with act.Fori(2, GROUPS) as g:
                elu_exp(g - 1)
                weights(0, g)
                table_row(1, g - 2, 0)
                table_operand(1, g - 1, 0)
            elu_exp(GROUPS - 1)
            table_row(1, GROUPS - 2, 0)
            table_operand(1, GROUPS - 1, 0)
            table_row(1, GROUPS - 1, 0)
            with act.Fori(0, GROUPS) as g:
                weights(1, g)
            all_rstd(2)

        @block.tensor
        def _(pe):
            mm = nc.tensor.matmul
            pe.wait_ge(s_const, 1)
            pe.wait_ge(s_par, 16 * PAR_DMAS)
            nc.tensor.transpose(ps_weak[0][:, 0:LAYERS * NS * 4], b1_rows[:], ident[0:LAYERS * NS * 4, 0:LAYERS * NS * 4]).then_inc(s_prepP, 1)
            for k in range(2):
                pe.wait_ge(s_prepP, 2 + 4 * k)
                nc.tensor.transpose(ps_weak[0][:, 128:256], gat_w[k][:, 0:P], ident[:]).then_inc(s_prepP, 1)
                pe.wait_ge(s_prepP, 4 + 4 * k)
                mm(ps_weak[1][:, 0:2 * HEADS], gat_wt[:], gat_a[k][:], start=True, stop=True).then_inc(s_prepP, 1)
            pe.wait_ge(s_prepP, 10)
            def count(i, step):
                pe.wait_ge(s_1h, i * 4 + (step + 1))
                for t in range(HIST):
                    last = mm(ps_sum[0:GROUPS, 0:P], hi1h[:, step % 2, t, :], lo1h[:, step % 2, t, :], start=False, stop=False)
                last.then_inc(s_1h_used, 1)

            def first_state(g, i, step):
                pe.wait_ge(s_xc, g + 1)
                nc.tensor.transpose(ps_w1[0][:, 0:P], x1[0][:], ident[:]).then_inc(s_xT, 1)
                count(i, step)
                pe.wait_ge(s_xTs, g + 1)
                mm(ps_w1[1][:, 0:H], ones_row[:], b_in_r[:], start=True, stop=False)
                mm(ps_w1[1][:, 0:H], x1_t[0][:], w_in[:], start=False, stop=True).then_inc(s_h0, 1)
                count(i, step + 1)
                pe.wait_ge(s_h0s, g + 1)

            mm(ps_sum[0:GROUPS, 0:P], zero_b[:, 0:GROUPS], zero_b[:], start=True, stop=False)
            with pe.Fori(0, GROUPS // 2) as i:
                first_state(i * 2, i, 0)
                first_state(i * 2 + 1, i, 2)
            first_state(GROUPS - 1, GROUPS // 2, 0)
            for step in range(2, 4 * (ET // (4 * HIST) - GROUPS // 2)):
                count(GROUPS // 2 + step // 4, step % 4)
            mm(ps_sum[0:GROUPS, 0:P], zero_b[:, 0:GROUPS], zero_b[:], start=False, stop=True).then_inc(s_hist, 1)
            pe.wait_ge(s_tot, 1)
            mm(ps_sum[0:GROUPS, 256:257], tri[0:GROUPS, 0:GROUPS], hist[:, 1, P - 1:P], start=True, stop=True).then_inc(s_pre, 1)
            pe.wait_ge(s_off, 1)
            nc.tensor.transpose(ps_tr[:, 0:GROUPS], hist[:, 0, :], ident[0:GROUPS, 0:GROUPS])
            nc.tensor.transpose(ps_tr[:, P:P + GROUPS], hist[:, 2, :], ident[0:GROUPS, 0:GROUPS]).then_inc(s_offT, 1)
            pe.wait_ge(s_bkt, 1)
            for g in range(GROUPS):
                last = mm(ps_sum[:, g:g + 1], bucket1h[:, g, :], ones_b[:, 0:1], start=True, stop=True)
            last.then_inc(s_bsum, 1)
            pe.wait_ge(s_bscan, 1)
            mm(ps_sum[:, 128:129], tri[:], bkt_sum[:, GROUPS - 1:GROUPS], start=True, stop=True).then_inc(s_below, 1)
            pe.wait_ge(s_base, 1)
            for g in range(GROUPS):
                own = (ps_gate, ps_moe)[g // BATCH % 2][:, g % BATCH * P:(g % BATCH + 1) * P]
                w(pe, s_rank, (g // BATCH - 1) * BATCH)
                mm(own, bkt_base[:, g:g + 1].to_broadcast([P, P]), ident[:], start=True, stop=False)
                mm(own, tri_b[:], bucket1h[:, g, :], start=False, stop=True).then_inc(s_own, 1)

            pe.wait_ge(s_degp, 1)
            nc.tensor.transpose(ps_tr[0:GROUPS, 256:384], deg_p[:], ident[:]).then_inc(s_degT, 1)
            pe.wait_ge(s_kmax, 1)
            mm(ps_sum[0:1, 128:128 + GROUPS + 1], kmax[:], tri[0:GROUPS, 0:GROUPS + 1], start=True, stop=True)
            nc.tensor.transpose(ps_sum[0:1, 256:256 + GROUPS], kmax[:], ident[0:GROUPS, 0:GROUPS]).then_inc(s_cumP, 1)

            def operands(r, g):
                n = g + r * GROUPS
                pe.wait_ge(hcur_ready, n + 1)
                w(pe, opT_copied, n)
                nc.tensor.transpose(ps_tr[:, 0:P], h_cur[0][:, 0:P], ident[:])
                nc.tensor.transpose(ps_tr[:, P:H], h_cur[0][:, P:H], ident[:])
                pe.wait_ge(agg_ready, n + 1)
                nc.tensor.transpose(ps_tr[:, H:H + P], agg[:, 0:P], ident[:])
                nc.tensor.transpose(ps_tr[:, H + P:2 * H], agg[:, P:H], ident[:]).then_inc(opT_ready, 1)

            def router(r, g, odd):
                n = g + r * GROUPS
                w(pe, h_done, n - 2)
                w(pe, gatesT_copied, n - 1)
                pe.wait_ge(opT_copied, n + 1)
                lg = ps_moe[:, H:H + NE + 1]
                mm(lg, ones_row[:], rt_b[:, r, :], start=True, stop=False)
                for k in range(2):
                    mm(lg, h_t[0][:, k * P:(k + 1) * P], rt_w[:, r, k, :], start=False, stop=False)
                for k in range(2):
                    last = mm(lg, agg_t[odd][:, k * P:(k + 1) * P], rt_w[:, r, 2 + k, :], start=False, stop=k == 1)
                last.then_inc(logits_ready, 1)

            def strong_first(r, g, odd, experts):
                n = g + r * GROUPS
                for s in experts:
                    w(pe, relu_ready, n * NS + (s - 1))
                    for c in range(4):
                        for k in range(2):
                            last = mm(ps_w1[s % 2][:, c * P:(c + 1) * P], w1_w[:, k, s, c * P:(c + 1) * P],
                                      agg_t[odd][:, k * P:(k + 1) * P], start=k == 0, stop=k == 1)
                    last.then_inc(w1_ready, 1)

            def gates_transposed(r, g, more):
                n = g + r * GROUPS
                if more:
                    pe.wait_ge(logits_copied, n + 2)
                else:
                    pe.wait_ge(h_done, n - 1)
                nc.tensor.transpose(ps_moe[0:NE, 384:512], gates[:], ident[:]).then_inc(gatesT_ready, 1)

            def weak_experts(r, g, odd):
                n = g + r * GROUPS
                w(pe, weak_copied, n)
                for j in range(2):
                    mm(ps_weak[j][:], ones_b[:], wk_parts[:, r, j * 512:(j + 1) * 512], start=True, stop=False)
                    for k in range(2):
                        last = mm(ps_weak[j][:], agg_t[odd][:, k * P:(k + 1) * P], wk_w[:, k, j * 512:(j + 1) * 512], start=False, stop=k == 1)
                last.then_inc(weak_ready, 1)

            def broadcast(r, g):
                n = g + r * GROUPS
                pe.wait_ge(gates_ready, n + 1)
                w(pe, gated, n * NS)
                for s in range(NS):
                    last = mm(ps_gate[:, s * P:(s + 1) * P], gates[:, NW + s:NW + s + 1].to_broadcast([P, P]), ident[:], start=True, stop=True)
                last.then_inc(bcast_ready, 1)

            def second(r, g, odd, more):
                n = g + r * GROUPS
                pe.wait_ge(gatesT_copied, n + (2 if more else 1))
                w(pe, h_done, n)
                mm(ps_moe[:, 0:H], gates_t[odd][:], b2_w[:], start=True, stop=False)
                for s in range(NS):
                    pe.wait_ge(gated, n * NS + (s + 1))
                    for c in range(4):
                        last = mm(ps_moe[:, 0:H], strong[odd][:, s, c, :], w2_w[:, c, s, :], start=False, stop=s == NS - 1 and c == 3)
                last.then_inc(w2_ready, 1)

            for r in range(LAYERS):
                def step(g, odd):
                    operands(r, g)
                    strong_first(r, g - 1, 1 - odd, range(NS))
                    router(r, g, odd)
                    broadcast(r, g - 1)
                    gates_transposed(r, g - 1, True)
                    weak_experts(r, g - 1, 1 - odd)
                    second(r, g - 2, odd, True)

                pe.wait_ge(s_wts, 16 * WT_DMAS * (r + 1))
                operands(r, 0)
                router(r, 0, 0)
                strong_first(r, 0, 0, range(NS))
                weak_experts(r, 0, 0)
                operands(r, 1)
                router(r, 1, 1)
                broadcast(r, 0)
                gates_transposed(r, 0, True)
                strong_first(r, 1, 1, range(NS))
                operands(r, 2)
                router(r, 2, 0)
                broadcast(r, 1)
                gates_transposed(r, 1, True)
                weak_experts(r, 1, 1)
                second(r, 0, 0, True)
                with pe.Fori(0, (GROUPS - 3) // 2) as i:
                    step(i * 2 + 3, 1)
                    step(i * 2 + 4, 0)
                strong_first(r, GROUPS - 1, 0, range(NS))
                broadcast(r, GROUPS - 1)
                gates_transposed(r, GROUPS - 1, False)
                weak_experts(r, GROUPS - 1, 0)
                second(r, GROUPS - 2, 1, True)
                second(r, GROUPS - 1, 0, False)

            def state_t(g, odd, before):
                pe.wait_ge(hout_ready, g + 1)
                if before:
                    pe.wait_ge(houtT_copied, g - 1)
                nc.tensor.transpose(ps_w1[odd][:, 0:P], h_cur[odd][:, 0:P], ident[:])
                nc.tensor.transpose(ps_w1[odd][:, P:H], h_cur[odd][:, P:H], ident[:]).then_inc(houtT_ready, 1)

            def project(g, odd, before):
                if before:
                    pe.wait_ge(z_ready, g - 1)
                mm(ps_weak[odd][:, 0:IN], ones_row[:], b_out_r[:], start=True, stop=False)
                pe.wait_ge(houtT_copied, g + 1)
                for k in range(2):
                    last = mm(ps_weak[odd][:, 0:IN], h_t[odd][:, k * P:(k + 1) * P], w_out[:, k, :], start=False, stop=k == 1)
                last.then_inc(b_out_ready, 1)

            state_t(0, 0, False)
            state_t(1, 1, False)
            project(0, 0, False)
            state_t(2, 0, True)
            project(1, 1, False)
            with pe.Fori(1, GROUPS // 2) as i:
                state_t(i * 2 + 1, 1, True)
                project(i * 2, 0, True)
                state_t(i * 2 + 2, 0, True)
                project(i * 2 + 1, 1, True)
            project(GROUPS - 1, 0, True)

            def table_operand(k, g, odd, before):
                n = g + k * GROUPS
                pe.wait_ge(x1_ready, n + 1)
                if before:
                    pe.wait_ge(x1T_copied, n + 1 - before)
                nc.tensor.transpose(ps_w1[odd][:, 0:P], x1[odd][:], ident[:]).then_inc(x1T_ready, 1)

            def table_row(k, g, odd, before):
                n = g + k * GROUPS
                pe.wait_ge(x1T_copied, n + 1)
                if before:
                    pe.wait_ge(row_done, n + 1 - before)
                mm(ps_weak[odd][:, 0:P + 2 * HEADS], x1_t[odd][:], gat_w[k][:], start=True, stop=True).then_inc(row_ready, 1)

            pe.wait_ge(z_ready, GROUPS)
            table_operand(0, 0, 0, 0)
            table_operand(0, 1, 1, 0)
            table_row(0, 0, 0, 0)
            table_operand(0, 2, 0, 2)
            table_row(0, 1, 1, 0)
            with pe.Fori(1, GROUPS // 2) as i:
                table_operand(0, i * 2 + 1, 1, 2)
                table_row(0, i * 2, 0, 2)
                table_operand(0, i * 2 + 2, 0, 2)
                table_row(0, i * 2 + 1, 1, 2)
            table_row(0, GROUPS - 1, 0, 2)
            with pe.Fori(0, GROUPS) as g:
                table_operand(1, g, 0, 1)
                table_row(1, g, 0, 1)


_INS = ['x', 'src', 'dst', 'L0_gnn_W_in', 'L0_gnn_b_in', 'L0_gnn_router_W', 'L0_gnn_router_b', 'L0_gnn_weak_W', 'L0_gnn_weak_b',
        'L0_gnn_strong_W1', 'L0_gnn_strong_b1', 'L0_gnn_strong_W2', 'L0_gnn_strong_b2', 'L0_gnn_conf_W', 'L0_gnn_conf_b',
        'L0_gnn_W_out', 'L0_gnn_b_out', 'L1_gnn_W1', 'L1_gnn_a_src1', 'L1_gnn_a_dst1', 'L1_gnn_b1', 'L1_gnn_W2',
        'L1_gnn_a_src2', 'L1_gnn_a_dst2', 'L1_gnn_b2']


def kernel(**inputs):
    import numpy as np
    import concourse.bacc as bacc
    from concourse.bass_utils import run_bass_kernel_spmd

    nc = bacc.Bacc("TRN2", target_bir_lowering=False, num_devices=1)
    arrays, args = {}, []
    for name in _INS:
        a = np.ascontiguousarray(inputs[name])
        if name == "x":
            a = np.concatenate([a, np.zeros((NP - N, IN), a.dtype)])
        elif name == "src":
            a = np.concatenate([a, np.zeros(EP - E, a.dtype)])
        elif name == "dst":
            a = np.concatenate([a, np.full(EP - E, NP, a.dtype)])
        arrays[f"in_{name}"] = a
        args.append(nc.dram_tensor(f"in_{name}", a.shape, mybir.dt.from_np(a.dtype), kind="ExternalInput").ap())
    args.append(nc.dram_tensor("out", (NP, IN), F32, kind="ExternalOutput").ap())
    gnn_kernel(nc, *args)
    r = run_bass_kernel_spmd(nc, [arrays], core_ids=[0])
    return r.results[0]["out"][:N]
```
